# Optimizing a Trainium2 kernel written in Bass

```python
import numpy as np
import jax
import jax.numpy as jnp

def _softmax(x, axis=-1):
    return jax.nn.softmax(x, axis=axis)

def _gelu(x):
    return jax.nn.gelu(x, approximate=True)

def _silu(x):
    return jax.nn.silu(x)

def _sigmoid(x):
    return jax.nn.sigmoid(x)

def _layernorm(x, axis=-1, eps=1e-05):
    m = jnp.mean(x, axis=axis, keepdims=True)
    v = jnp.var(x, axis=axis, keepdims=True)
    return (x - m) / jnp.sqrt(v + eps)

def _scatter_add(tgt, idx, src, axis=0):
    return tgt.at[idx].add(src)

def _segment_sum(src, seg, n):
    return jax.ops.segment_sum(src, seg, n)
kernel_name = 'mk_hybrid_d1_jaxref_r8_841fab'

def setup_inputs(seed: int=0):
    np.random.seed(seed)
    _w = jnp.asarray

    def _L0_attn_a_setup():
        import jax, jax.numpy as jnp
        import numpy as np
        import math
        DIM = 128
        NUM_HEADS = 8
        HEAD_DIM = DIM // NUM_HEADS // 2
        DEPTH = 6
        LAMBDA_INIT = 0.8 - 0.6 * math.exp(-0.3 * DEPTH)
        EPS = 1e-05
        key = jax.random.key(seed)
        ks = jax.random.split(key, 10)
        B, S = (2, 256)
        x = jax.random.normal(ks[0], (B, S, DIM), dtype=jnp.float32)
        sc = DIM ** (-0.5)
        Wq = jax.random.normal(ks[1], (DIM, DIM), dtype=jnp.float32) * sc
        Wk = jax.random.normal(ks[2], (DIM, DIM), dtype=jnp.float32) * sc
        Wv = jax.random.normal(ks[3], (DIM, DIM), dtype=jnp.float32) * sc
        Wo = jax.random.normal(ks[4], (DIM, DIM), dtype=jnp.float32) * sc
        lq1 = jax.random.normal(ks[5], (HEAD_DIM,), dtype=jnp.float32) * 0.1
        lk1 = jax.random.normal(ks[6], (HEAD_DIM,), dtype=jnp.float32) * 0.1
        lq2 = jax.random.normal(ks[7], (HEAD_DIM,), dtype=jnp.float32) * 0.1
        lk2 = jax.random.normal(ks[8], (HEAD_DIM,), dtype=jnp.float32) * 0.1
        return {'x': x, 'Wq': Wq, 'Wk': Wk, 'Wv': Wv, 'Wo': Wo, 'lq1': lq1, 'lk1': lk1, 'lq2': lq2, 'lk2': lk2}
    _L0_attn_a_in = _L0_attn_a_setup()

    def _L0_attn_b_setup():
        import jax, jax.numpy as jnp
        import numpy as np
        from functools import partial
        LN_EPS = 1000000.0
        FEAT_EPS = 1e-06

        def _layernorm(x, gamma, beta):
            mu = jnp.mean(x, axis=-1, keepdims=True)
            var = jnp.var(x, axis=-1, keepdims=True)
            return gamma * (x - mu) / jnp.sqrt(var + LN_EPS) + beta

        def _phi(x, omega):
            m = omega.shape[0]
            proj = jnp.einsum('bhsd,md->bhsm', x, omega)
            z = proj - 0.5 * jnp.sum(x * x, axis=-1, keepdims=True)
            z = z - jnp.max(z, axis=-1, keepdims=True)
            return jnp.exp(z) / jnp.sqrt(jnp.asarray(m, x.dtype)) + FEAT_EPS

        def _forward(batch, Wq, Wk, Wv, Wo, omega, W1, b1, W2, b2, gamma, beta):
            B, S, D = batch.shape
            M, dh = omega.shape
            H = D // dh
            scale = dh ** (-0.25)

            def heads(W):
                return (batch @ W).reshape(B, S, H, dh).transpose(0, 2, 1, 3)
            q = heads(Wq) * scale
            k = heads(Wk) * scale
            v = heads(Wv)
            qp = _phi(q, omega)
            kp = _phi(k, omega)
            qs = qp.transpose(2, 0, 1, 3)
            ks = kp.transpose(2, 0, 1, 3)
            vs = v.transpose(2, 0, 1, 3)

            def step(carry, qkv):
                S_kv, s_k = carry
                qt, kt, vt = qkv
                S_kv = S_kv + kt[..., :, None] * vt[..., None, :]
                s_k = s_k + kt
                num = jnp.einsum('bhm,bhmd->bhd', qt, S_kv)
                den = jnp.einsum('bhm,bhm->bh', qt, s_k)
                return ((S_kv, s_k), num / (den[..., None] + FEAT_EPS))
            carry0 = (jnp.zeros((B, H, M, dh), batch.dtype), jnp.zeros((B, H, M), batch.dtype))
            _, outs = jax.lax.scan(step, carry0, (qs, ks, vs))
            attn = outs.transpose(1, 0, 2, 3).reshape(B, S, D) @ Wo
            h = _layernorm(batch + attn, gamma, beta)
            out = jnp.maximum(h @ W1 + b1, 0.0) @ W2 + b2
            return out
        key = jax.random.key(seed)
        ks = jax.random.split(key, 8)
        B, S, D, H, dh, M, DFF = (4, 128, 128, 16, 64, 128, 512)
        w = 0.02
        return {'batch': jax.random.normal(ks[0], (B, S, D), jnp.float32), 'Wq': jax.random.normal(ks[1], (D, D), jnp.float32) * w, 'Wk': jax.random.normal(ks[2], (D, D), jnp.float32) * w, 'Wv': jax.random.normal(ks[3], (D, D), jnp.float32) * w, 'Wo': jax.random.normal(ks[4], (D, D), jnp.float32) * w, 'omega': jax.random.normal(ks[5], (M, dh), jnp.float32), 'W1': jax.random.normal(ks[6], (D, DFF), jnp.float32) * w, 'b1': jnp.zeros((DFF,), jnp.float32), 'W2': jax.random.normal(ks[7], (DFF, D), jnp.float32) * w, 'b2': jnp.zeros((D,), jnp.float32), 'gamma': jnp.ones((D,), jnp.float32), 'beta': jnp.zeros((D,), jnp.float32)}
    _L0_attn_b_in = _L0_attn_b_setup()

    def _L0_ffn_setup():
        import jax, jax.numpy as jnp
        import numpy as np
        B, S, H, E = (4, 256, 128, 8)
        key = jax.random.key(seed)
        k1, k2, k3 = jax.random.split(key, 3)
        scale_w = 1.0 / np.sqrt(H)
        return {'x': jax.random.normal(k1, (B, S, H), dtype=jnp.float32), 'router_w': jax.random.normal(k2, (H, E), dtype=jnp.float32) * scale_w, 'router_b': jnp.zeros((E,), dtype=jnp.float32), 'expert_w': jax.random.normal(k3, (E, H, H), dtype=jnp.float32) * scale_w, 'expert_b': jnp.zeros((E, H), dtype=jnp.float32)}
    _L0_ffn_in = _L0_ffn_setup()
    _d = {'L0_attn_a_x': _L0_attn_a_in['x'], 'L0_attn_a_Wq': _L0_attn_a_in['Wq'], 'L0_attn_a_Wk': _L0_attn_a_in['Wk'], 'L0_attn_a_Wv': _L0_attn_a_in['Wv'], 'L0_attn_a_Wo': _L0_attn_a_in['Wo'], 'L0_attn_a_lq1': _L0_attn_a_in['lq1'], 'L0_attn_a_lk1': _L0_attn_a_in['lk1'], 'L0_attn_a_lq2': _L0_attn_a_in['lq2'], 'L0_attn_a_lk2': _L0_attn_a_in['lk2'], 'L0_attn_b_Wq': _L0_attn_b_in['Wq'], 'L0_attn_b_Wk': _L0_attn_b_in['Wk'], 'L0_attn_b_Wv': _L0_attn_b_in['Wv'], 'L0_attn_b_Wo': _L0_attn_b_in['Wo'], 'L0_attn_b_omega': _L0_attn_b_in['omega'], 'L0_attn_b_W1': _L0_attn_b_in['W1'], 'L0_attn_b_b1': _L0_attn_b_in['b1'], 'L0_attn_b_W2': _L0_attn_b_in['W2'], 'L0_attn_b_b2': _L0_attn_b_in['b2'], 'L0_attn_b_gamma': _L0_attn_b_in['gamma'], 'L0_attn_b_beta': _L0_attn_b_in['beta'], 'L0_ffn_router_w': _L0_ffn_in['router_w'], 'L0_ffn_router_b': _L0_ffn_in['router_b'], 'L0_ffn_expert_w': _L0_ffn_in['expert_w'], 'L0_ffn_expert_b': _L0_ffn_in['expert_b']}
    _x0 = _d['L0_attn_a_x']
    _d['L0_attn_a_x'] = jax.random.normal(jax.random.fold_in(jax.random.key(seed), 1), (2, 1024, 128), dtype=_x0.dtype)
    del _x0
    return _d

def reference(L0_attn_a_x, L0_attn_a_Wq, L0_attn_a_Wk, L0_attn_a_Wv, L0_attn_a_Wo, L0_attn_a_lq1, L0_attn_a_lk1, L0_attn_a_lq2, L0_attn_a_lk2, L0_attn_b_Wq, L0_attn_b_Wk, L0_attn_b_Wv, L0_attn_b_Wo, L0_attn_b_omega, L0_attn_b_W1, L0_attn_b_b1, L0_attn_b_W2, L0_attn_b_b2, L0_attn_b_gamma, L0_attn_b_beta, L0_ffn_router_w, L0_ffn_router_b, L0_ffn_expert_w, L0_ffn_expert_b):

    def _L0_attn_a_ref(x, Wq, Wk, Wv, Wo, lq1, lk1, lq2, lk2):
        import jax, jax.numpy as jnp
        import numpy as np
        import math
        DIM = 128
        NUM_HEADS = 8
        HEAD_DIM = DIM // NUM_HEADS // 2
        DEPTH = 6
        LAMBDA_INIT = 0.8 - 0.6 * math.exp(-0.3 * DEPTH)
        EPS = 1e-05
        B, S, D = x.shape
        H, hd = (NUM_HEADS, HEAD_DIM)
        scaling = hd ** (-0.5)
        q = (x @ Wq.T).reshape(B, S, 2 * H, hd).transpose(0, 2, 1, 3) * scaling
        k = (x @ Wk.T).reshape(B, S, 2 * H, hd).transpose(0, 2, 1, 3)
        v = (x @ Wv.T).reshape(B, S, H, 2 * hd).transpose(0, 2, 1, 3)
        scores = jnp.einsum('bhqd,bhkd->bhqk', q, k)
        scores = jnp.nan_to_num(scores)
        causal = jnp.triu(jnp.full((S, S), -jnp.inf, dtype=scores.dtype), 1)
        attn = jax.nn.softmax(scores + causal, axis=-1)
        lam1 = jnp.exp(jnp.sum(lq1 * lk1))
        lam2 = jnp.exp(jnp.sum(lq2 * lk2))
        lam = lam1 - lam2 + LAMBDA_INIT
        attn = attn.reshape(B, H, 2, S, S)
        w = attn[:, :, 0] - lam * attn[:, :, 1]
        o = jnp.einsum('bhqk,bhkd->bhqd', w, v)
        o = o * jax.lax.rsqrt(jnp.mean(o * o, axis=-1, keepdims=True) + EPS)
        o = o * (1.0 - LAMBDA_INIT)
        o = o.transpose(0, 2, 1, 3).reshape(B, S, H * 2 * hd)
        return o @ Wo.T

    def _L0_attn_b_ref(batch, Wq, Wk, Wv, Wo, omega, W1, b1, W2, b2, gamma, beta):
        import jax, jax.numpy as jnp
        import numpy as np
        from functools import partial
        LN_EPS = 1000000.0
        FEAT_EPS = 1e-06

        def _layernorm(x, gamma, beta):
            mu = jnp.mean(x, axis=-1, keepdims=True)
            var = jnp.var(x, axis=-1, keepdims=True)
            return gamma * (x - mu) / jnp.sqrt(var + LN_EPS) + beta

        def _phi(x, omega):
            m = omega.shape[0]
            proj = jnp.einsum('bhsd,md->bhsm', x, omega)
            z = proj - 0.5 * jnp.sum(x * x, axis=-1, keepdims=True)
            z = z - jnp.max(z, axis=-1, keepdims=True)
            return jnp.exp(z) / jnp.sqrt(jnp.asarray(m, x.dtype)) + FEAT_EPS

        def _forward(batch, Wq, Wk, Wv, Wo, omega, W1, b1, W2, b2, gamma, beta):
            B, S, D = batch.shape
            M, dh = omega.shape
            H = D // dh
            scale = dh ** (-0.25)

            def heads(W):
                return (batch @ W).reshape(B, S, H, dh).transpose(0, 2, 1, 3)
            q = heads(Wq) * scale
            k = heads(Wk) * scale
            v = heads(Wv)
            qp = _phi(q, omega)
            kp = _phi(k, omega)
            qs = qp.transpose(2, 0, 1, 3)
            ks = kp.transpose(2, 0, 1, 3)
            vs = v.transpose(2, 0, 1, 3)

            def step(carry, qkv):
                S_kv, s_k = carry
                qt, kt, vt = qkv
                S_kv = S_kv + kt[..., :, None] * vt[..., None, :]
                s_k = s_k + kt
                num = jnp.einsum('bhm,bhmd->bhd', qt, S_kv)
                den = jnp.einsum('bhm,bhm->bh', qt, s_k)
                return ((S_kv, s_k), num / (den[..., None] + FEAT_EPS))
            carry0 = (jnp.zeros((B, H, M, dh), batch.dtype), jnp.zeros((B, H, M), batch.dtype))
            _, outs = jax.lax.scan(step, carry0, (qs, ks, vs))
            attn = outs.transpose(1, 0, 2, 3).reshape(B, S, D) @ Wo
            h = _layernorm(batch + attn, gamma, beta)
            out = jnp.maximum(h @ W1 + b1, 0.0) @ W2 + b2
            return out
        return _forward(batch, Wq, Wk, Wv, Wo, omega, W1, b1, W2, b2, gamma, beta)

    def _L0_ffn_ref(x, router_w, router_b, expert_w, expert_b):
        import jax, jax.numpy as jnp
        import numpy as np
        B, S, H, E = (4, 256, 128, 8)
        b, s, h = x.shape
        xt = x.reshape(b * s, h)
        logits = xt @ router_w + router_b
        probs = jax.nn.softmax(logits, axis=-1)
        gate = jnp.max(probs, axis=-1)
        idx = jnp.argmax(probs, axis=-1)
        out_all = jnp.einsum('th,ehd->ted', xt, expert_w) + expert_b[None, :, :]
        e_out = jnp.take_along_axis(out_all, idx[:, None, None], axis=1)[:, 0, :]
        y = gate[:, None] * e_out
        return y.reshape(b, s, h)
    x = L0_attn_a_x
    x = x + _L0_attn_a_ref(_layernorm(x, axis=-1), L0_attn_a_Wq, L0_attn_a_Wk, L0_attn_a_Wv, L0_attn_a_Wo, L0_attn_a_lq1, L0_attn_a_lk1, L0_attn_a_lq2, L0_attn_a_lk2)
    x = x + _L0_ffn_ref(_layernorm(x, axis=-1), L0_ffn_router_w, L0_ffn_router_b, L0_ffn_expert_w, L0_ffn_expert_b)
    x = x + _L0_attn_b_ref(_layernorm(x, axis=-1), L0_attn_b_Wq, L0_attn_b_Wk, L0_attn_b_Wv, L0_attn_b_Wo, L0_attn_b_omega, L0_attn_b_W1, L0_attn_b_b1, L0_attn_b_W2, L0_attn_b_b2, L0_attn_b_gamma, L0_attn_b_beta)
    x = x + _L0_ffn_ref(_layernorm(x, axis=-1), L0_ffn_router_w, L0_ffn_router_b, L0_ffn_expert_w, L0_ffn_expert_b)
    return x

_drawn_inputs = setup_inputs


def setup_inputs(seed=0):
    import zlib

    import numpy as np

    out = dict(_drawn_inputs(seed))
    spreads = {'L0_attn_b_b1': (0.0, 0.1),
     'L0_attn_b_b2': (0.0, 0.1),
     'L0_attn_b_gamma': (1.0, 0.6),
     'L0_attn_b_beta': (0.0, 0.284),
     'L0_ffn_router_b': (0.0, 0.1),
     'L0_ffn_expert_b': (0.0, 0.1)}
    factors = {'L0_attn_a_lq1': 2.927,
     'L0_attn_b_Wq': 64.0,
     'L0_attn_b_Wk': 64.0,
     'L0_attn_b_Wv': 64.0,
     'L0_attn_b_Wo': 64.0,
     'L0_attn_b_omega': 64.0}
    for name, (base, spread) in spreads.items():
        noise = np.random.default_rng([zlib.crc32(name.encode()), seed]).standard_normal(out[name].shape)
        drawn = base * np.exp(spread * noise) if base else spread * noise
        out[name] = jnp.asarray(drawn.astype(out[name].dtype))
    for name, factor in factors.items():
        out[name] = (out[name] * factor).astype(out[name].dtype)
    return out
```

```python
import math
from contextlib import ExitStack

import concourse.bass as bass
from concourse import mybir

CLEARED = 5

P = 128
B, S, D = 2, 1024, 128
TOK = B * S
NT = TOK // P
TB = S // P
GT = 4
NG = NT // GT
W5 = GT * P
HEADS = 8
HD = D // HEADS // 2
VD = 2 * HD
NU = B * HEADS
SLOTS = 3
TERMS = 6
KROWS = TERMS * HD
ZROWS = 96
MROW = 96
PARTS = 3
LAMBDA_INIT = 0.8 - 0.6 * math.exp(-0.3 * 6)
ATT_EPS = 1e-5
LN_EPS = 1e-5
SCORE_SCALE = HD ** -0.5
OPERAND_BOUND = 4.0e18
MASKED = -3.0e38
AG = 12
BC = 20
NE = 8
COPIES = 12
OHR = COPIES * NE
LH, LD, LM = 2, 64, 128
LU = B * LH
FEAT_EPS = 1e-6
LN2_EPS = 1e6
VW = 96
FF = 512
FC = FF // P

fp32 = mybir.dt.float32
bf16 = mybir.dt.bfloat16
ALU = mybir.AluOpType
ACT = mybir.ActivationFunctionType
AX = mybir.AxisListType

A_GROUPS = [(i, (h,)) for i in (7, 6, 5, 4) for h in (0, 1)] + [(i, (0, 1)) for i in (3, 2, 1, 0)]
B_CHUNKS = []
for half in (0, 1):
    for kt in range(8 if half == 0 else 4):
        width = min(512, 128 * ((8 if half == 0 else 4) - kt))
        for heads in (((0,), (1,)) if width > 256 else ((0, 1),)):
            B_CHUNKS.append((half, kt, heads, width))
assert len(A_GROUPS) == AG and len(B_CHUNKS) == BC
MASKS = [(half, kt) for half in (0, 1) for kt in ((4, 5, 6, 7) if half == 0 else (0, 1, 2, 3))]


def last_chunk(half, kt):
    return max(c for c, (hf, k, _, _) in enumerate(B_CHUNKS) if (hf, k) == (half, kt))


def hybrid_kernel(nc, x_d, wqT_d, wkT_d, wvT_d, woT_d, lam_d, bwq_d, bwk_d, bwv_d, bwo_d, omT_d,
                  w1_d, b1_d, w2_d, b2_d, gam_d, bet_d, rw_d, rb_d, ew_d, eb_d, out_d):
    ctx = ExitStack()
    with ctx:
        def sb(name, shape, dt=fp32):
            return ctx.enter_context(nc.sbuf_tensor(name, shape, dt))

        def sem(name):
            return ctx.enter_context(nc.semaphore(name))

        X = sb("X", [P, NT, D])
        arena = sb("arena", [P, NU * 2 * W5])
        E = sb("E", [P, 12, 2, W5])
        Qop = sb("Qop", [P, SLOTS, 2, S], bf16)
        Kop = sb("Kop", [P, SLOTS, 2, S], bf16)
        Vu = sb("Vu", [P, NU, TB, 32])
        Vs = sb("Vs", [P, SLOTS, TB, 32])
        NM = sb("NM", [P, SLOTS, 2, 2, 4])
        MR = sb("MR", [P, SLOTS, 2, 2, 4])
        M3 = sb("M3", [P, SLOTS, 2, 2, PARTS, 4], bf16)
        MT = sb("MT", [24, SLOTS, 2, P], bf16)
        ident = sb("ident", [P, P])
        identb = sb("identb", [P, P], bf16)
        maskA = sb("maskA", [P, P], bf16)
        maskT = sb("maskT", [P, P])
        half_c = sb("half_c", [P, NT])
        wT = sb("wT", [P, 4, D])
        lamv = sb("lamv", [P, 4, HD])
        lamw = sb("lamw", [P, 2, HD])
        lams = sb("lams", [P, 4])
        warm = sb("warm", [P, 1])
        st = sb("st", [P, NT, 6])
        mv = sb("mv", [P, NT, 2])
        rstd = sb("rstd", [P, NT])
        ve = sb("ve", [P, NT])
        rw = sb("rw", [P, OHR])
        rb = sb("rb", [P, NE])
        ew = sb("ew", [P, NE, D])
        ebf = sb("ebf", [NE, D])
        ebr = sb("ebr", [NE, D])
        ebp = sb("ebp", [NE, PARTS, D], bf16)
        eb = sb("eb", [OHR, D], bf16)
        sel = sb("sel", [OHR, NE, P], bf16)
        rev = sb("rev", [P, NE])
        bw = sb("bw", [P, 4, D])
        om = sb("om", [P, LH, LM])
        w1 = sb("w1", [P, FF])
        b1 = sb("b1", [P, FC])
        w2 = sb("w2", [P, FC, D])
        b2 = sb("b2", [P, 1])
        gam = sb("gam", [P, D])
        bet = sb("bet", [P, D])
        ps = ctx.enter_context(nc.psum_tensor("ps", [P, 8, W5], fp32))

        def view(big, at, shape):
            n = 1
            for k in shape:
                n *= k
            flat = big[:, at:at + n]
            if len(shape) == 1:
                return flat
            names = "abcd"[:len(shape)]
            return flat.rearrange("p (" + " ".join(names) + ") -> p " + " ".join(names),
                                  **{c: k for c, k in zip(names[1:], shape[1:])})

        Ef = E[:, :, :, :].rearrange("p a b c -> p (a b c)")
        XN = view(arena, 0, [NT, D])
        XT = view(arena, 2048, [TOK])
        QS = view(arena, 4096, [2, S])
        QR = view(arena, 6144, [2, S])
        QP = view(arena, 8192, [3072]).bitcast(bf16).rearrange("p (q t s) -> p q t s", q=2, t=3)
        QP2 = view(arena, 11264, [3072]).bitcast(bf16).rearrange("p (q t s) -> p q t s", q=2, t=3)
        QPb = [QP, QP2]
        OT = arena
        OA = view(Ef, 0, [B, TB * HEADS * 2, 17])
        RL = view(Ef, 4352, [B, TB * HEADS * 2])
        TT = view(Ef, 4608, [B, TB * HEADS * 2, VD])
        DD = view(Ef, 8704, [B, TB * HEADS, VD])
        SQ = view(Ef, 10752, [TB * HEADS, VD])
        MS = sb("MS", [P, B, TB * HEADS])
        OTT = view(arena, 0, [TOK])
        FXN = view(arena, 2048, [NT, D])
        FXT = view(arena, 4096, [TOK])
        XM = view(arena, 6144, [4, W5])
        YT = view(arena, 8192, [2, W5])
        LG = sb("LG", [P, NG, GT, NE])
        LE = sb("LE", [P, NG, GT, NE])
        MX = sb("MX", [P, 5, NG, GT])
        OH = sb("OH", [P, 2, GT, COPIES, NE], bf16)
        OHT = sb("OHT", [OHR, 2, W5], bf16)
        BX = view(arena, 0, [NT, D])
        BXT = view(arena, 2048, [TOK])
        QKT = view(arena, 4096, [2, TOK])
        EQK = view(arena, 8192, [2, NT, LH, LM])
        KP = view(Ef, 0, [NT, LH, LM])
        QKPT = view(Ef, 4096, [2, NT, LH, P])
        VA = sb("VA", [P, NT, LH, VW])
        Vuf = Vu[:, :, :, :].rearrange("p u a b -> p (u a b)")
        ST = view(Vuf, 0, [TB - 1, LU, VW])
        AM = view(Vuf, 2688, [2, LU, P])
        AO = view(arena, 2048, [NT, D])
        QKSQ = view(arena, 2048, [2, W5])
        NN = sb("NN", [P, 2, NT, LH])
        RM = sb("RM", [P, 2, NT, LH])
        DN = sb("DN", [P, 2, LU])
        AOT = view(arena, 8192, [TOK])
        H2 = view(arena, 10240, [NT, D])
        HT = view(arena, 12288, [TOK])
        HID = view(arena, 4096, [FC, W5])
        UT = view(arena, 14336, [2, W5])

        def hid(g):
            return view(arena, 4096 + 2048 * (g % 2), [FC, W5])

        q_scr = nc.dram_tensor("q_scratch", [NU * 2 * KROWS, S], bf16, kind="Internal").ap()
        k_scr = nc.dram_tensor("k_scratch", [NU * 2 * KROWS, S], bf16, kind="Internal").ap()

        s_x = [sem(f"x_loaded_{b}") for b in range(B)]
        s_w = sem("attention_weights_loaded")
        s_lam = sem("lambda_vectors_loaded")
        s_w2 = sem("other_weights_loaded")
        s_om = sem("omega_loaded")
        s_rw = sem("router_loaded")
        s_ebl = sem("expert_bias_loaded")
        s_ebd = sem("expert_bias_placed")
        s_rwz = sem("router_cleared")
        s_omz = sem("omega_cleared")
        s_cst = sem("constants_ready")
        s_cz = sem("constants_cleared")
        s_oz = sem("operands_cleared")
        s_dve = sem("vector_chain")
        s_pool = sem("pool_chain")
        s_pass = sem("pool_past_a_wait")
        s_act = sem("scalar_chain")
        s_var = sem("variances_ready")
        s_rstd = sem("rstd_ready")
        s_xn = sem("normalised")
        s_xt = sem("transposed_in_psum")
        s_xte = sem("transposed_in_sbuf")
        s_qk = sem("qk_projected")
        s_qke = sem("qk_scaled")
        s_qkc = sem("qk_bounded")
        s_vp = sem("v_projected")
        s_ve = sem("v_stored")
        s_part = [sem("q_parts_ready"), sem("k_parts_ready")]
        s_scr = [sem(f"scratch_written_{b}") for b in range(B)]
        s_ld = [sem(f"operands_loaded_{s}") for s in range(SLOTS)]
        s_m = [[sem(f"maxima_placed_{s}_{h}") for h in range(2)] for s in range(SLOTS)]
        s_a = sem("score_group_ready")
        s_max = sem("maximum_taken")
        s_sstep = sem("split_step")
        s_split = sem("maxima_split")
        s_mt = sem("maxima_transposed")
        s_mte = sem("maxima_in_sbuf")
        s_b = sem("score_chunk_ready")
        s_exp = sem("chunk_exponentiated")
        s_mask = sem("diagonal_masked")
        s_pv = sem("outputs_accumulated")
        s_pve = sem("outputs_stored")
        s_vs = sem("values_staged")
        s_lamr = sem("lambda_ready")

        block = ctx.enter_context(nc.Block())


        s_oT = sem("out_transposed")
        s_oA = sem("out_collected")
        s_ms = sem("head_squares_summed")
        s_hr = sem("head_rstd_ready")
        s_hd = sem("heads_joined")
        s_hs = sem("heads_squared")
        s_hn = sem("heads_normalised")
        s_oT2 = sem("heads_transposed")
        s_oT2e = sem("heads_transposed_in_sbuf")
        s_wo = sem("attention_projected")
        s_x1 = sem("residual_updated")

        ffn = [dict((n, sem(f"ffn{k}_{n}")) for n in (
            "var", "rstd", "xn", "xt", "xte", "lg", "sub", "exp", "oh", "oht", "ohte",
            "g", "xm", "e", "y", "ye", "yt", "x")) for k in range(2)]
        la = dict((n, sem(f"la_{n}")) for n in (
            "var", "rstd", "xn", "xt", "xte", "qk", "qke", "v", "ve", "vz", "sq", "nt", "nn", "pr", "rm",
            "ex", "kp", "ft", "fte", "at", "ate", "st", "ste", "o", "oe", "ot", "ote", "wo", "res",
            "var2", "rstd2", "h1", "h", "ht", "hte", "u", "ue", "y", "ye", "yt", "x", "nsq"))
        s_out = sem("out_written")

        @block.sync
        def _(sp):
            xv = x_d.rearrange("(t p) d -> p t d", p=P)
            for b in range(B):
                sp.dma_start(X[:, b * TB:(b + 1) * TB, :], xv[:, b * TB:(b + 1) * TB, :]).then_inc(s_x[b], 16)
                if b == 0:
                    for i, w in enumerate((wqT_d, wkT_d, wvT_d, woT_d)):
                        sp.dma_start(wT[:, i, :], w).then_inc(s_w, 16)
            sp.dma_start(lamv[:, :, :], lam_d.rearrange("(o a) d -> o a d", o=1).broadcast_to([P, 4, HD])).then_inc(s_lam, 16)
            for b in range(B):
                for qk, scr in enumerate((q_scr, k_scr)):
                    rows = scr.rearrange("(b r t) s -> b r t s", b=B, t=TERMS)[b]
                    sp.wait_ge(s_part[qk], b + 1)
                    src = QPb[b][:, qk, :, :]
                    if qk == 0:
                        for t0, n in ((0, 3), (3, 2), (5, 1)):
                            sp.dma_start(rows[:, t0:t0 + n, :], src[:, 0:n, :]).then_inc(s_scr[b], 16)
                    else:
                        for t, part in enumerate((0, 0, 0, 1, 1, 2)):
                            sp.dma_start(rows[:, t, :], src[:, part, :]).then_inc(s_scr[b], 16)

            def load_operands(w, slot):
                for scr, op in ((q_scr, Qop), (k_scr, Kop)):
                    sp.dma_start(op[0:KROWS, slot, :, :],
                                 scr[bass.ds(w * (2 * KROWS), 2 * KROWS), :].rearrange("(h r) s -> r h s", h=2)
                                 ).then_inc(s_ld[slot], 16)

            def place_maxima(slot, half):
                q0 = (1 - half) * W5
                for h in range(2):
                    sp.dma_start(Qop[MROW:MROW + PARTS, slot, h, q0:q0 + W5].rearrange("r (t q) -> r t q", t=4),
                                 MT[12 * h:12 * h + 12, slot, half, :]).then_inc(s_m[slot][half], 16)

            sp.wait_ge(s_scr[0], 16 * 9)
            sp.wait_ge(s_scr[1], 16 * 9)
            sp.wait_ge(s_oz, CLEARED)
            load_operands(0, 0)
            load_operands(1, 1)
            sp.wait_ge(s_mte, 1)
            place_maxima(0, 0)

            def unit(u, s, load=True, ahead=True):
                sp.wait_ge(s_b, u * BC + 1)
                if load:
                    load_operands(u + 2, (s + 2) % SLOTS)
                sp.wait_ge(s_mte, 2 * u + 2)
                place_maxima(s, 1)
                if ahead:
                    sp.wait_ge(s_mte, 2 * u + 3)
                    place_maxima((s + 1) % SLOTS, 0)

            with sp.Fori(0, 4) as t:
                for s in range(SLOTS):
                    unit(t * SLOTS + s, s)
            for u in range(12, NU):
                unit(u, u % SLOTS, load=u + 2 < NU, ahead=u + 1 < NU)
            ov = out_d.rearrange("(t p) d -> p t d", p=P)
            for g in range(NG):
                sp.wait_ge(ffn[1]["x"], g + 1)
                sp.dma_start(ov[:, g * GT:(g + 1) * GT, :], X[:, g * GT:(g + 1) * GT, :]).then_inc(s_out, 16)
            sp.wait_ge(s_out, 16 * NG)

        @block.gpsimd
        def _(pool):
            chain = [0]

            def link(ins):
                chain[0] += 1
                ins.then_inc(s_pool, 1)
                pool.wait_ge(s_pool, chain[0])

            pool.memset(ident[:, :], 0.0).then_inc(s_cz, 1)
            pool.wait_ge(s_cz, 1)
            pool.affine_select(out=ident[:, :], in_=ident[:, :], compare_op=ALU.not_equal, fill=1.0, base=0,
                               pattern=[[-1, P]], channel_multiplier=1).then_inc(s_cst, 1)
            pool.memset(half_c[:, :], -0.5).then_inc(s_cst, 1)

            def rsqrt(out, var, tmp, eps, scale, done):
                link(pool.tensor_scalar(tmp, var, scale, eps, ALU.mult, ALU.add))
                pool.tensor_tensor(out, tmp, half_c[:, 0:1].broadcast_to(tmp.shape) if len(tmp.shape) > 1 else tmp,
                                   ALU.pow).then_inc(done, 1)

            pool.memset(Qop[:, :, :, :].bitcast(fp32), 0.0).then_inc(s_oz, 1)
            for b in range(B):
                if b == 0:
                    pool.wait_ge(s_cst, 2)
                pool.wait_ge(s_var, b + 1)
                rsqrt(rstd[:, b * TB:(b + 1) * TB], mv[:, b * TB:(b + 1) * TB, 1], ve[:, b * TB:(b + 1) * TB],
                      LN_EPS, 1.0, s_rstd)
            link(pool.memset(Kop[:, :, :, :], 1.0))
            pool.memset(Kop[0:ZROWS, :, :, :].bitcast(fp32), 0.0).then_inc(s_oz, 1)
            link(pool.memset(maskT[:, :], 1.0))
            link(pool.affine_select(out=maskT[:, :], in_=maskT[:, :], compare_op=ALU.is_ge, fill=0.0, base=0,
                                    pattern=[[1, P]], channel_multiplier=-1))
            link(pool.memset(maskA[:, :], 0.0))
            pool.affine_select(out=maskA[:, :], in_=maskA[:, :], compare_op=ALU.is_ge, fill=MASKED, base=0,
                               pattern=[[-1, P]], channel_multiplier=1).then_inc(s_oz, 1)
            pool.tensor_copy(identb[:, :], ident[:, :]).then_inc(s_oz, 1)
            pool.memset(E[:, 8 + 1, :, 0:P], 0.0).then_inc(s_pv, 3)
            pool.memset(Vu[:, :, :, VD:32], 0.0).then_inc(s_vs, 1)
            pool.wait_ge(s_vs, 1)
            pool.memset(Vu[:, :, :, VD:VD + 1], 1.0).then_inc(s_oz, 1)

            def wait(sm, value):
                pool.wait_ge(sm, value)
                pool.sem_inc(s_pass, 1)

            def split(n, slot, half):
                src = NM[:, slot, half, :, :]
                part = [M3[:, slot, half, :, k, :] for k in range(PARTS)]
                rem = MR[:, slot, half, :, :]
                pool.tensor_copy(part[0], src).then_inc(s_sstep, 1)
                wait(s_sstep, n * 3 + 1)
                pool.tensor_tensor(rem, src, part[0], ALU.subtract).then_inc(s_sstep, 1)
                wait(s_sstep, n * 3 + 2)
                pool.tensor_copy(part[1], rem).then_inc(s_sstep, 1)
                wait(s_sstep, n * 3 + 3)
                pool.tensor_tensor(part[2], rem, part[1], ALU.subtract).then_inc(s_split, 1)

            def stage_values(u, slot):
                pool.tensor_copy(Vs[:, slot, :, :].rearrange("p a b -> p (a b)"),
                                 Vu[:, :, :, :].rearrange("p u a b -> p (u a b)")[:, bass.ds(u * (TB * 32), TB * 32)]
                                 ).then_inc(s_vs, 1)

            def mask(u, j):
                half, kt = MASKS[j]
                q0 = P * (kt % 4)
                wait(s_exp, u * BC + (2 + last_chunk(half, kt) + 1))
                diag = E[:, half * 8 + kt, :, q0:q0 + P]
                pool.affine_select(out=diag, in_=diag, compare_op=ALU.is_ge, fill=0.0, base=0,
                                   pattern=[[0, 2], [1, P]], channel_multiplier=-1).then_inc(s_mask, 1)

            pool.wait_ge(s_ve, NG)
            pool.wait_ge(s_oz, CLEARED)
            stage_values(0, 0)
            wait(s_max, 8)
            split(0, 0, 0)
            wait(s_max, AG)
            split(1, 0, 1)

            def unit(u, s, ahead=True):
                if ahead:
                    wait(s_pv, 2 * u + 1)
                    stage_values(u + 1, (s + 1) % SLOTS)
                mask(u, 0)
                mask(u, 1)
                if ahead:
                    wait(s_max, u * AG + AG + 8)
                    split(2 * u + 2, (s + 1) % SLOTS, 0)
                for j in range(2, 8):
                    mask(u, j)
                if ahead:
                    wait(s_max, u * AG + 2 * AG)
                    split(2 * u + 3, (s + 1) % SLOTS, 1)

            with pool.Fori(0, 5) as t:
                for s in range(SLOTS):
                    unit(t * SLOTS + s, s)
            unit(NU - 1, (NU - 1) % SLOTS, ahead=False)

            for k, w in enumerate((bwq_d, bwk_d, bwv_d, bwo_d)):
                pool.dma_start(bw[:, k, :], w).then_inc(s_w2, 16)
            pool.dma_start(w1[:, :], w1_d).then_inc(s_w2, 16)
            pool.dma_start(w2[:, :, :], w2_d.rearrange("(c p) d -> p c d", p=P)).then_inc(s_w2, 16)
            pool.dma_start(b1[:, :], b1_d).then_inc(s_w2, 16)
            pool.dma_start(b2[:, :], b2_d).then_inc(s_w2, 16)
            pool.dma_start(gam[:, :], gam_d.broadcast_to([P, D])).then_inc(s_w2, 16)
            pool.dma_start(bet[:, :], bet_d.broadcast_to([P, D])).then_inc(s_w2, 16)
            pool.dma_start(rb[:, :], rb_d.broadcast_to([P, NE])).then_inc(s_w2, 16)
            pool.dma_start(ew[:, :, :], ew_d).then_inc(s_w2, 16)
            pool.dma_start(ebf[:, :], eb_d).then_inc(s_ebl, 16)
            pool.memset(rw[:, :], 0.0).then_inc(s_rwz, 1)
            pool.wait_ge(s_rwz, 1)
            pool.dma_start(rw[:, 0:NE], rw_d).then_inc(s_rw, 16)
            pool.memset(om[:, :, :], 0.0).then_inc(s_omz, 1)
            pool.wait_ge(s_omz, 1)
            for h in range(LH):
                pool.dma_start(om[h * LD:(h + 1) * LD, h, :], omT_d).then_inc(s_om, 16)
            link(pool.memset(eb[:, :], 0.0))
            pool.wait_ge(s_ebl, 16)
            link(pool.tensor_copy(ebp[:, 0, :], ebf[:, :]))
            link(pool.tensor_tensor(ebr[:, :], ebf[:, :], ebp[:, 0, :], ALU.subtract))
            link(pool.tensor_copy(ebp[:, 1, :], ebr[:, :]))
            link(pool.tensor_tensor(ebp[:, 2, :], ebr[:, :], ebp[:, 1, :], ALU.subtract))
            for k in range(PARTS):
                pool.dma_start(eb[k * NE:(k + 1) * NE, :], ebp[:, k, :]).then_inc(s_ebd, 16)
            link(pool.memset(sel[:, :, :], 0.0))
            link(pool.affine_select(out=sel[:, :, :], in_=sel[:, :, :], compare_op=ALU.not_equal, fill=1.0, base=0,
                                    pattern=[[-1, NE], [0, P]], channel_multiplier=1))
            for e in range(NE):
                last = pool.memset(rev[:, e:e + 1], float(NE - e))
            last.then_inc(s_cst, 1)
            for b in range(B):
                pool.wait_ge(s_ms, b + 1)
                rsqrt(MS[:, b, :], MS[:, b, :], MS[:, b, :], ATT_EPS, 1.0 / VD, s_hr)

            def ffn_rstd(f, g):
                r = slice(g * GT, (g + 1) * GT)
                pool.wait_ge(f["var"], g + 1)
                rsqrt(rstd[:, r], mv[:, r, 1], ve[:, r], LN_EPS, 1.0, f["rstd"])

            for g in range(NG):
                ffn_rstd(ffn[0], g)
            link(pool.memset(VA[:, :, :, LD:VW], 0.0))
            pool.memset(VA[:, :, :, LD:LD + 1], 1.0).then_inc(la["vz"], 1)
            for g in range(NG):
                r = slice(g * GT, (g + 1) * GT)
                pool.wait_ge(la["var"], g + 1)
                rsqrt(rstd[:, r], mv[:, r, 1], ve[:, r], LN_EPS, 1.0, la["rstd"])
            c = 1.0 / math.sqrt(LM)
            for t in range(NT):
                pool.wait_ge(la["ex"], 4 * (t + 1))
                pool.tensor_scalar(KP[:, t, :, :].rearrange("p a b -> p (a b)"),
                                   EQK[:, 1, t, :, :].rearrange("p a b -> p (a b)"), c, FEAT_EPS,
                                   ALU.mult, ALU.add).then_inc(la["kp"], 1)
            for g in range(NG):
                r = slice(g * GT, (g + 1) * GT)
                pool.wait_ge(la["var2"], g + 1)
                rsqrt(rstd[:, r], mv[:, r, 1], ve[:, r], LN2_EPS, 1.0, la["rstd2"])
            for g in range(NG):
                ffn_rstd(ffn[1], g)

        @block.scalar
        def _(act):
            for g in range(NG):
                act.wait_ge(s_xt, g + 1)
                act.copy(XT[:, g * W5:(g + 1) * W5], ps[:, g % 2, :]).then_inc(s_xte, 1)
                if g % 2 == 0:
                    continue
                b = g // 2
                for qk in range(2):
                    if b:
                        act.wait_ge(s_part[qk], 1)
                    for n in range(2):
                        act.wait_ge(s_qk, 4 * b + 2 * qk + n + 1)
                        act.activation(QS[:, qk, n * W5:(n + 1) * W5], ps[:, 2 + 2 * qk + n, :], ACT.Copy,
                                       scale=(SCORE_SCALE, 1.0)[qk]).then_inc(s_qke, 1)
                for g2 in (2 * b, 2 * b + 1):
                    act.wait_ge(s_vp, g2 + 1)
                    if g2 == 0:
                        act.wait_ge(s_oz, CLEARED)
                    src = ps[:, 6 + g2 % 2, :].rearrange("p (t h d) -> p h t d", t=GT, h=HEADS)
                    dst = Vu[:, b * HEADS:(b + 1) * HEADS, (g2 % 2) * GT:(g2 % 2 + 1) * GT, 0:VD]
                    for h in range(HEADS):
                        last = act.copy(dst[:, h, :, :], src[:, h, :, :])
                    last.then_inc(s_ve, 1)
            act.wait_ge(s_dve, lam_sums)
            act.activation(lams[:, 2:4], lams[:, 0:2], ACT.Exp).then_inc(s_act, 1)

            def exp_chunk(u, c):
                half, kt, heads, width = B_CHUNKS[c]
                act.wait_ge(s_b, u * BC + (1 + c + 1))
                if c in (0, 14):
                    act.wait_ge(s_pv, 2 * u + (half + 2))
                bank = 4 + c % 2
                dst = E[:, half * 8 + kt, heads[0]:heads[-1] + 1, W5 - width:W5]
                src = ps[:, bank, 0:len(heads) * width].rearrange("p (h q) -> p h q", h=len(heads))
                act.activation(dst, src, ACT.Exp).then_inc(s_exp, 1)

            def store_outputs(u, half):
                act.wait_ge(s_pv, 2 * u + (half + 4))
                act.copy(OT[:, bass.ds(u * (2 * W5) + half * W5, W5)], ps[:, 6, :]).then_inc(s_pve, 1)

            act.wait_ge(s_oz, CLEARED)
            act.activation(warm[:, 0:1], half_c[:, 0:1], ACT.Exp).then_inc(s_exp, 2)

            def unit(u):
                for c in range(BC):
                    exp_chunk(u, c)
                    if c == 18:
                        store_outputs(u, 0)
                store_outputs(u, 1)

            act.sem_inc(s_pve, 1)
            with act.Fori(0, 5) as t:
                for s in range(SLOTS):
                    unit(t * SLOTS + s)
            unit(NU - 1)

            for b in range(B):
                act.wait_ge(s_hd, b + 1)
                if b:
                    act.wait_ge(s_ms, b)
                act.activation(SQ[:, :, :], DD[:, b, :, :], ACT.Square).then_inc(s_hs, 1)
            for g in range(NG):
                act.wait_ge(s_oT2, g + 1)
                act.copy(OTT[:, g * W5:(g + 1) * W5], ps[:, g % 2, :]).then_inc(s_oT2e, 1)

            def ffn_act(f):
                def head(g):
                    act.wait_ge(f["xt"], g + 1)
                    act.copy(FXT[:, g * W5:(g + 1) * W5], ps[:, 0, :]).then_inc(f["xte"], 1)
                    act.wait_ge(f["sub"], g + 1)
                    act.activation(LE[:, g, :, :], LG[:, g, :, :], ACT.Exp).then_inc(f["exp"], 1)
                    act.wait_ge(f["oht"], g + 1)
                    if g >= 2:
                        act.wait_ge(f["y"], g - 1)
                    act.copy(OHT[:, g % 2, :], ps[0:OHR, 1, 0:W5 // 2].bitcast(bf16)).then_inc(f["ohte"], 1)

                head(0)
                for g in range(NG):
                    if g + 1 < NG:
                        head(g + 1)
                    act.wait_ge(f["y"], g + 1)
                    if g >= 2:
                        act.wait_ge(f["yt"], g - 1)
                    act.copy(YT[:, g % 2, :], ps[:, 5 + g % 2, :]).then_inc(f["ye"], 1)

            ffn_act(ffn[0])
            for g in range(NG):
                act.wait_ge(la["xt"], g + 1)
                act.copy(BXT[:, g * W5:(g + 1) * W5], ps[:, g % 2, :]).then_inc(la["xte"], 1)
                for qk in range(2):
                    act.wait_ge(la["qk"], 2 * g + qk + 1)
                    act.activation(QKT[:, qk, g * W5:(g + 1) * W5], ps[:, 2 + qk, :], ACT.Copy,
                                   scale=LD ** -0.25).then_inc(la["qke"], 1)
                act.wait_ge(la["v"], g + 1)
                if g == 0:
                    act.wait_ge(la["vz"], 1)
                act.copy(VA[:, g * GT:(g + 1) * GT, :, 0:LD],
                         ps[:, 4, :].rearrange("p (t h d) -> p t h d", t=GT, h=LH)).then_inc(la["ve"], 1)
            for g in range(NG):
                for qk in range(2):
                    n = 2 * g + qk
                    act.wait_ge(la["nt"], n + 1)
                    if n >= 2:
                        act.wait_ge(la["nn"], n - 1)
                    act.activation(QKSQ[:, n % 2, :], ps[:, 6 + n % 2, :], ACT.Square).then_inc(la["sq"], 1)
            def store_features(t):
                act.wait_ge(la["ft"], t + 1)
                act.activation(QKPT[:, :, t, :, :], ps[:, 6 + t % 2, :].rearrange("p (q h s) -> p q h s", q=2, h=LH),
                               ACT.Copy, scale=c_feat, bias=FEAT_EPS).then_inc(la["fte"], 1)

            for t in range(NT):
                for qk in range(2):
                    n = 2 * t + qk
                    act.wait_ge(la["rm"], n + 1)
                    for h in range(LH):
                        act.activation(EQK[:, qk, t, h, :], ps[:, n % 6, h * LM:(h + 1) * LM], ACT.Exp,
                                       bias=RM[:, qk, t, h:h + 1]).then_inc(la["ex"], 1)
                if t >= 3:
                    store_features(t - 3)
            for t in range(NT - 3, NT):
                store_features(t)
            for g in range(NG):
                act.wait_ge(la["ot"], g + 1)
                act.copy(AOT[:, g * W5:(g + 1) * W5], ps[:, g % 2, :]).then_inc(la["ote"], 1)
            for g in range(NG):
                act.wait_ge(la["ht"], g + 1)
                act.copy(HT[:, g * W5:(g + 1) * W5], ps[:, g % 2, :]).then_inc(la["hte"], 1)
                for f in range(FC):
                    n = g * FC + f
                    act.wait_ge(la["u"], n + 1)
                    if f == 0 and g >= 2:
                        act.wait_ge(la["y"], g - 1)
                    act.activation(hid(g)[:, f, :], ps[:, 2 + n % 2, :], ACT.Relu,
                                   bias=b1[:, f:f + 1]).then_inc(la["ue"], 1)
                act.wait_ge(la["y"], g + 1)
                if g >= 2:
                    act.wait_ge(la["yt"], g - 1)
                act.activation(UT[:, g % 2, :], ps[:, 4 + g % 2, :], ACT.Identity,
                               bias=b2[:, 0:1]).then_inc(la["ye"], 1)
            ffn_act(ffn[1])

        @block.tensor
        def _(pe):
            def transposes(bank, srcs, idn, done):
                for k, src in enumerate(srcs):
                    last = pe.transpose(ps[:, bank, k * P:(k + 1) * P], src, idn)
                last.then_inc(done, 1)

            def feature_transposes(t):
                pe.wait_ge(la["ex"], 4 * (t + 1))
                if t >= 2:
                    pe.wait_ge(la["fte"], t - 1)
                if t < 2:
                    pe.wait_ge(la["sq"], 2 * NG)
                for k in range(4):
                    last = pe.transpose(ps[:, 6 + t % 2, k * P:(k + 1) * P], EQK[:, k // 2, t, k % 2, :], ident[:, :])
                last.then_inc(la["ft"], 1)

            pe.wait_ge(s_cst, 1)
            for g in range(NG):
                pe.wait_ge(s_xn, g + 1)
                if g >= 2:
                    pe.wait_ge(s_xte, g - 1)
                transposes(g % 2, [XN[:, g * GT + k, :] for k in range(GT)], ident[:, :], s_xt)
                if g % 2 == 0:
                    continue
                b = g // 2
                if b == 0:
                    pe.wait_ge(s_w, 64)
                pe.wait_ge(s_xte, g + 1)
                for qk in range(2):
                    for n in range(2):
                        if b:
                            pe.wait_ge(s_qke, 2 * qk + n + 1)
                        pe.matmul(ps[:, 2 + 2 * qk + n, :], wT[:, qk, :], XT[:, b * S + n * W5:b * S + (n + 1) * W5],
                                  start=True, stop=True).then_inc(s_qk, 1)
                for g2 in (2 * b, 2 * b + 1):
                    if b:
                        pe.wait_ge(s_ve, g2 - 1)
                    for k in range(GT):
                        t = g2 * GT + k
                        last = pe.matmul(ps[:, 6 + g2 % 2, k * P:(k + 1) * P], XT[:, t * P:(t + 1) * P], wT[:, 2, :],
                                         start=True, stop=True)
                    last.then_inc(s_vp, 1)

            def score_group(w, n, slot):
                i, heads = A_GROUPS[n]
                kk = P * (i + 1)
                first = 2 * (n % 2)
                for j, h in enumerate(heads):
                    if len(heads) == 1:
                        pieces = [(first, 0, 0, min(kk, W5))] + ([(first + 1, 0, W5, kk)] if kk > W5 else [])
                    elif kk > 256:
                        pieces = [(first + j, 0, 0, kk)]
                    else:
                        pieces = [(first, j * kk, 0, kk)]
                    for bank, at, k0, k1 in pieces:
                        diag = k1 == kk
                        pe.matmul(ps[:, bank, at:at + k1 - k0], Qop[0:ZROWS, slot, h, i * P:(i + 1) * P],
                                  Kop[0:ZROWS, slot, h, k0:k1], start=True, stop=not diag)
                        if diag:
                            last = pe.matmul(ps[:, bank, at + k1 - k0 - P:at + k1 - k0], identb[:, :], maskA[:, :],
                                             start=False, stop=True)
                last.then_inc(s_a, 1)

            def score_chunk(u, c, slot):
                half, kt, heads, width = B_CHUNKS[c]
                q1 = S if half == 0 else W5
                pe.wait_ge(s_exp, u * BC + (c + 1))
                for j, h in enumerate(heads):
                    last = pe.matmul(ps[:, 4 + c % 2, j * width:(j + 1) * width],
                                     Kop[0:MROW + PARTS, slot, h, kt * P:(kt + 1) * P],
                                     Qop[0:MROW + PARTS, slot, h, q1 - width:q1], start=True, stop=True)
                last.then_inc(s_b, 1)

            def outputs(u, half, kt0, slot):
                last_kt = 7 if half == 0 else 3
                pe.wait_ge(s_exp, u * BC + (2 + last_chunk(half, kt0 + 1) + 1))
                masked = [j for j, (hf, kt) in enumerate(MASKS) if hf == half and kt <= kt0 + 1]
                if masked:
                    pe.wait_ge(s_mask, u * 8 + (max(masked) + 1))
                if kt0 == 0:
                    pe.wait_ge(s_pve, 2 * u + (half + 1))
                    if half == 0:
                        pe.wait_ge(s_vs, u + 2)
                for kt in (kt0, kt0 + 1):
                    q0 = 0 if (half == 0 and kt < 4) or (half == 1 and kt == 1) else P * (kt % 4)
                    for h in (0, 1):
                        col = 32 * (2 * h + kt % 2)
                        last = pe.matmul(ps[col:col + 32, 6, q0:W5], Vs[:, slot, kt, :],
                                         E[:, half * 8 + kt, h, q0:W5], start=kt < 2, stop=kt >= last_kt - 1)
                if kt0 + 1 == last_kt:
                    last.then_inc(s_pv, 1)

            def transpose_maxima(n, slot, half):
                pe.wait_ge(s_split, n + 1)
                pe.wait_ge(s_mte, n)
                pe.transpose(ps[0:24, 7, 0:P // 2].bitcast(bf16),
                             M3[:, slot, half, :, :, :].rearrange("p a b c -> p (a b c)"),
                             identb[:, :]).then_inc(s_mt, 1)

            pe.wait_ge(s_ld[0], 32)
            pe.wait_ge(s_oz, CLEARED)
            pe.wait_ge(s_ve, NG)
            for n in range(AG):
                if n >= 2:
                    pe.wait_ge(s_max, n - 1)
                score_group(0, n, 0)
            transpose_maxima(0, 0, 0)

            def unit(u, t, s, ahead=True):
                nxt = (s + 1) % SLOTS
                loads = t + 1 if s < 2 else t + 2
                given = 0
                pe.wait_ge(s_m[s][0], 32 * (t + 1))
                for c in range(BC):
                    if c == 14:
                        pe.wait_ge(s_m[s][1], 32 * (t + 1))
                    score_chunk(u, c, s)
                    if ahead and given < AG and c * AG >= given * (BC - 1):
                        if given == 0:
                            pe.wait_ge(s_ld[nxt], 32 * loads)
                        pe.wait_ge(s_max, u * AG + (AG + given - 1))
                        score_group(u, given, nxt)
                        given += 1
                    if c == 3:
                        transpose_maxima(2 * u + 1, s, 1)
                    if c == 15 and ahead:
                        transpose_maxima(2 * u + 2, nxt, 0)
                    for at, half, kt0 in ((5, 0, 0), (9, 0, 2), (14, 0, 4), (16, 0, 6), (19, 1, 0)):
                        if c == at:
                            outputs(u, half, kt0, s)
                if ahead:
                    while given < AG:
                        pe.wait_ge(s_max, u * AG + (AG + given - 1))
                        score_group(u, given, nxt)
                        given += 1
                outputs(u, 1, 2, s)

            pe.sem_inc(s_b, 1)
            with pe.Fori(0, 5) as t:
                for s in range(SLOTS):
                    unit(t * SLOTS + s, t, s)
            unit(NU - 1, 5, 0, ahead=False)

            for n in range(2 * NU):
                if n == 0:
                    pe.wait_ge(s_pve, 2 * NU + 1)
                if n >= 8:
                    pe.wait_ge(s_oA, n - 7)
                transposes(n % 8, [OT[:, n * W5 + k * P:n * W5 + (k + 1) * P] for k in range(4)], ident[:, :], s_oT)
            for g in range(NG):
                if g == 0:
                    pe.wait_ge(s_oA, 2 * NU)
                pe.wait_ge(s_hn, g // 2 + 1)
                if g >= 2:
                    pe.wait_ge(s_oT2e, g - 1)
                b = g // 2
                dd = DD[:, b, :, :].rearrange("p (t h) d -> p t (h d)", t=TB)
                transposes(g % 2, [dd[:, (g % 2) * GT + k, :] for k in range(GT)], ident[:, :], s_oT2)
                pe.wait_ge(s_oT2e, g + 1)
                for k in range(GT):
                    t = g * GT + k
                    last = pe.matmul(ps[:, 2 + g, k * P:(k + 1) * P], OTT[:, t * P:(t + 1) * P], wT[:, 3, :],
                                     start=True, stop=True)
                last.then_inc(s_wo, 1)

            def ffn_pe(f):
                def head_x(g):
                    pe.wait_ge(f["xn"], g + 1)
                    if g:
                        pe.wait_ge(f["xte"], g)
                    transposes(0, [FXN[:, g * GT + k, :] for k in range(GT)], ident[:, :], f["xt"])

                def head_router(g):
                    pe.wait_ge(f["xte"], g + 1)
                    if g:
                        pe.wait_ge(f["sub"], g)
                    for k in range(GT):
                        t = g * GT + k
                        last = pe.matmul(ps[:, 2, k * OHR:(k + 1) * OHR], FXT[:, t * P:(t + 1) * P], rw[:, :],
                                         start=True, stop=True)
                    last.then_inc(f["lg"], 1)

                def head_onehot(g):
                    pe.wait_ge(f["oh"], g + 1)
                    if g:
                        pe.wait_ge(f["ohte"], g)
                    bank = ps[0:OHR, 1, 0:W5 // 2].bitcast(bf16)
                    for k in range(GT):
                        last = pe.transpose(bank[:, k * P:(k + 1) * P],
                                            OH[:, g % 2, k, :, :].rearrange("p a b -> p (a b)"), identb[:, :])
                    last.then_inc(f["oht"], 1)

                def spread(g, e):
                    n = g * NE + e
                    if n >= 2:
                        pe.wait_ge(f["xm"], n - 1)
                    pe.matmul(ps[:, 3 + n % 2, :], sel[:, e, :], OHT[:, g % 2, :], start=True, stop=True
                              ).then_inc(f["g"], 1)

                def expert(g, e):
                    pe.wait_ge(f["xm"], g * NE + e + 1)
                    mm = pe.matmul(ps[:, 5 + g % 2, :], ew[:, e, :], XM[:, e % 4, :], start=False, stop=e == NE - 1)
                    mm.then_inc(f["y"] if e == NE - 1 else f["e"], 1)

                head_x(0)
                head_router(0)
                head_onehot(0)
                for g in range(NG):
                    pe.wait_ge(f["ohte"], g + 1)
                    if g >= 2:
                        pe.wait_ge(f["ye"], g - 1)
                    pe.matmul(ps[:, 5 + g % 2, :], eb[:, :], OHT[:, g % 2, :], start=True, stop=False)
                    spread(g, 0)
                    spread(g, 1)
                    for e in range(NE):
                        if e == 1 and g + 1 < NG:
                            head_x(g + 1)
                        if e == 3 and g + 1 < NG:
                            head_router(g + 1)
                        expert(g, e)
                        if e + 2 < NE:
                            spread(g, e + 2)
                    if g + 1 < NG:
                        head_onehot(g + 1)
                    pe.wait_ge(f["ye"], g + 1)
                    if g:
                        pe.wait_ge(f["x"], g)
                    transposes(7, [YT[:, g % 2, k * P:(k + 1) * P] for k in range(GT)], ident[:, :], f["yt"])

            pe.wait_ge(s_x1, NG)
            pe.wait_ge(s_w2, 16 * 12)
            pe.wait_ge(s_rw, 16)
            pe.wait_ge(s_ebd, 48)
            pe.wait_ge(s_cst, 3)
            ffn_pe(ffn[0])

            pe.wait_ge(ffn[0]["x"], NG)
            for g in range(NG):
                pe.wait_ge(la["xn"], g + 1)
                if g >= 2:
                    pe.wait_ge(la["xte"], g - 1)
                transposes(g % 2, [BX[:, g * GT + k, :] for k in range(GT)], ident[:, :], la["xt"])
                pe.wait_ge(la["xte"], g + 1)
                for qk in range(2):
                    if g:
                        pe.wait_ge(la["qke"], 2 * (g - 1) + qk + 1)
                    pe.matmul(ps[:, 2 + qk, :], bw[:, qk, :], BXT[:, g * W5:(g + 1) * W5], start=True, stop=True
                              ).then_inc(la["qk"], 1)
                if g:
                    pe.wait_ge(la["ve"], g)
                for k in range(GT):
                    t = g * GT + k
                    last = pe.matmul(ps[:, 4, k * P:(k + 1) * P], BXT[:, t * P:(t + 1) * P], bw[:, 2, :],
                                     start=True, stop=True)
                last.then_inc(la["v"], 1)
            pe.wait_ge(la["qke"], 2 * NG)
            pe.wait_ge(la["ve"], NG)
            for g in range(NG):
                for qk in range(2):
                    n = 2 * g + qk
                    if n >= 2:
                        pe.wait_ge(la["sq"], n - 1)
                    transposes(6 + n % 2, [QKT[:, qk, (g * GT + k) * P:(g * GT + k + 1) * P] for k in range(GT)],
                               ident[:, :], la["nt"])
            pe.wait_ge(s_om, 32)
            for t in range(NT):
                for qk in range(2):
                    n = 2 * t + qk
                    if n >= 6:
                        pe.wait_ge(la["ex"], 2 * (n - 5))
                    pe.matmul(ps[:, n % 6, 0:LH * LM], QKT[:, qk, t * P:(t + 1) * P],
                              om[:, :, :].rearrange("p a b -> p (a b)"), start=True, stop=True).then_inc(la["pr"], 1)
                if t >= 2:
                    feature_transposes(t - 2)
            for t in (NT - 2, NT - 1):
                feature_transposes(t)
            pe.wait_ge(la["ex"], 4 * NT)
            pe.wait_ge(la["fte"], NT)
            pe.wait_ge(la["kp"], NT)

            def at_products(c):
                if c >= 2:
                    pe.wait_ge(la["ate"], c - 1)
                for j in range(LU):
                    t, h = (j // LH) * TB + c, j % LH
                    last = pe.matmul(ps[:, c % 2, j * P:(j + 1) * P], QKPT[:, 1, t, h, :], QKPT[:, 0, t, h, :],
                                     start=True, stop=True)
                last.then_inc(la["at"], 1)

            at_products(0)
            for c in range(TB):
                if c + 1 < TB:
                    at_products(c + 1)
                if c < TB - 1:
                    if c >= 2:
                        pe.wait_ge(la["ste"], c - 1)
                    for j in range(LU):
                        t, h = (j // LH) * TB + c, j % LH
                        last = pe.matmul(ps[:, 2 + c % 2, j * VW:(j + 1) * VW], KP[:, t, h, :], VA[:, t, h, :],
                                         start=True, stop=True)
                    last.then_inc(la["st"], 1)
                pe.wait_ge(la["ate"], c + 1)
                if c:
                    pe.wait_ge(la["ste"], c)
                if c >= 2:
                    pe.wait_ge(la["oe"], c - 1)
                for j in range(LU):
                    t, h = (j // LH) * TB + c, j % LH
                    dst = ps[:, 4 + c % 2, j * VW:(j + 1) * VW]
                    last = pe.matmul(dst, AM[:, c % 2, j, :], VA[:, t, h, :], start=True, stop=c == 0)
                    if c:
                        last = pe.matmul(dst, QKPT[:, 0, t, h, :], ST[:, c - 1, j, :], start=False, stop=True)
                last.then_inc(la["o"], 1)
            pe.wait_ge(la["oe"], TB)
            for g in range(NG):
                if g >= 2:
                    pe.wait_ge(la["ote"], g - 1)
                transposes(g % 2, [AO[:, g * GT + k, :] for k in range(GT)], ident[:, :], la["ot"])
                pe.wait_ge(la["ote"], g + 1)
                for k in range(GT):
                    t = g * GT + k
                    last = pe.matmul(ps[:, 2 + g, k * P:(k + 1) * P], AOT[:, t * P:(t + 1) * P], bw[:, 3, :],
                                     start=True, stop=True)
                last.then_inc(la["wo"], 1)
            pe.wait_ge(la["res"], NG)
            for g in range(NG):
                pe.wait_ge(la["h"], g + 1)
                if g >= 2:
                    pe.wait_ge(la["hte"], g - 1)
                transposes(g % 2, [H2[:, g * GT + k, :] for k in range(GT)], ident[:, :], la["ht"])
                pe.wait_ge(la["hte"], g + 1)
                for f in range(FC):
                    n = g * FC + f
                    if n >= 2:
                        pe.wait_ge(la["ue"], n - 1)
                    pe.matmul(ps[:, 2 + n % 2, :], w1[:, f * P:(f + 1) * P], HT[:, g * W5:(g + 1) * W5],
                              start=True, stop=True).then_inc(la["u"], 1)
                if g >= 2:
                    pe.wait_ge(la["ye"], g - 1)
                for f in range(FC):
                    pe.wait_ge(la["ue"], g * FC + f + 1)
                    last = pe.matmul(ps[:, 4 + g % 2, :], w2[:, f, :], hid(g)[:, f, :], start=f == 0, stop=f == FC - 1)
                last.then_inc(la["y"], 1)
                pe.wait_ge(la["ye"], g + 1)
                if g:
                    pe.wait_ge(la["x"], g)
                transposes(7, [UT[:, g % 2, k * P:(k + 1) * P] for k in range(GT)], ident[:, :], la["yt"])
            pe.wait_ge(la["x"], NG)
            ffn_pe(ffn[1])

        @block.vector
        def _(dve):
            chain = [0]

            def fence(ins):
                chain[0] += 1
                ins.then_inc(s_dve, 1)
                dve.wait_ge(s_dve, chain[0])

            def stats(tiles, src, done):
                for t in tiles:
                    last = dve.bn_stats(st[:, t, :], src(t))
                fence(last)
                for t in tiles:
                    last = dve.bn_aggr(mv[:, t, :], st[:, t, :])
                last.then_inc(done, 1)

            def normalise(tiles, dst, src, done):
                for t in tiles:
                    last = dve.tensor_scalar(dst(t), src(t), mv[:, t, 0:1], rstd[:, t:t + 1], ALU.subtract, ALU.mult)
                last.then_inc(done, 1)

            for b in range(B):
                dve.wait_ge(s_x[b], 16)
                stats(range(b * TB, (b + 1) * TB), lambda t: X[:, t, :], s_var)
            for g in range(NG):
                dve.wait_ge(s_var, g // 2 + 1)
                dve.wait_ge(s_rstd, g // 2 + 1)
                normalise(range(g * GT, (g + 1) * GT), lambda t: XN[:, t, :], lambda t: X[:, t, :], s_xn)
            dve.wait_ge(s_lam, 16)
            for k in range(2):
                last = dve.tensor_tensor(lamw[:, k, :], lamv[:, 2 * k, :], lamv[:, 2 * k + 1, :], ALU.mult)
            fence(last)
            fence(dve.tensor_reduce(lams[:, 0:2], lamw[:, :, :], AX.X, ALU.add))
            assert chain[0] == lam_sums
            for b in range(B):
                for qk in range(2):
                    part = QPb[b]
                    dve.wait_ge(s_qke, 4 * b + 2 * qk + 2)
                    fence(dve.tensor_scalar(QS[:, qk, :], QS[:, qk, :], OPERAND_BOUND, -OPERAND_BOUND, ALU.min, ALU.max))
                    fence(dve.tensor_copy(part[:, qk, 0, :], QS[:, qk, :]))
                    fence(dve.tensor_tensor(QR[:, qk, :], QS[:, qk, :], part[:, qk, 0, :], ALU.subtract))
                    fence(dve.tensor_copy(part[:, qk, 1, :], QR[:, qk, :]))
                    dve.tensor_tensor(part[:, qk, 2, :], QR[:, qk, :], part[:, qk, 1, :], ALU.subtract
                                      ).then_inc(s_part[qk], 1)
            dve.wait_ge(s_act, 1)
            fence(dve.tensor_tensor(lams[:, 0:1], lams[:, 3:4], lams[:, 2:3], ALU.subtract))
            fence(dve.tensor_scalar(lams[:, 1:2], lams[:, 0:1], 1.0, -LAMBDA_INIT, ALU.mult, ALU.add))

            def maximum(w, n, slot):
                i, heads = A_GROUPS[n]
                kk = P * (i + 1)
                first = 2 * (n % 2)
                dve.wait_ge(s_a, w * AG + (n + 1))
                out = NM[:, slot, 0 if i >= 4 else 1, heads[0]:heads[-1] + 1, i % 4]
                if len(heads) == 1:
                    src = ps[:, first:first + 2, :].rearrange("p b c -> p (b c)")[:, 0:kk]
                elif kk > 256:
                    src = ps[:, first:first + 2, 0:kk]
                else:
                    src = ps[:, first, 0:2 * kk].rearrange("p (h k) -> p h k", h=2)
                dve.tensor_reduce(out, src, AX.X, ALU.max, negate=True).then_inc(s_max, 1)

            def store_maxima(n, slot, half):
                dve.wait_ge(s_mt, n + 1)
                dve.tensor_copy(MT[:, slot, half, :], ps[0:24, 7, 0:P // 2].bitcast(bf16)).then_inc(s_mte, 1)

            for n in range(AG):
                maximum(0, n, 0)
            store_maxima(0, 0, 0)

            def unit(u, s, ahead=True):
                nxt = (s + 1) % SLOTS
                for n in range(AG):
                    if ahead:
                        maximum(u + 1, n, nxt)
                    if n == 2:
                        store_maxima(2 * u + 1, s, 1)
                    if n == 9 and ahead:
                        store_maxima(2 * u + 2, nxt, 0)

            with dve.Fori(0, 5) as t:
                for s in range(SLOTS):
                    unit(t * SLOTS + s, s)
            unit(NU - 1, (NU - 1) % SLOTS, ahead=False)

            oa = OA[:, :, :, :].rearrange("p b (t u h) e -> p b t u h e", t=TB, u=HEADS)
            for n in range(2 * NU):
                u, half = n // 2, n % 2
                dve.wait_ge(s_oT, n + 1)
                t0 = 4 if half == 0 else 0
                src = ps[:, n % 8, :].rearrange("p (c h k e) -> p c h e k", c=4, h=2, k=2)[:, :, :, 0:17, :]
                dve.tensor_reduce(oa[:, u // HEADS, t0:t0 + 4, u % HEADS, :, :], src, AX.X, ALU.add
                                  ).then_inc(s_oA, 1)
            dve.wait_ge(s_oA, 2 * NU)
            for b in range(B):
                fence(dve.reciprocal(RL[:, b, :], OA[:, b, :, 16]))
                odd = RL[:, b, :].rearrange("p (n h) -> p n h", h=2)[:, :, 1]
                fence(dve.tensor_scalar(odd, odd, lams[:, 1:2], None, ALU.mult))
                fence(dve.tensor_tensor(TT[:, b, :, :], OA[:, b, :, 0:VD],
                                        RL[:, b, :].rearrange("p (n o) -> p n o", o=1).broadcast_to([P, TB * HEADS * 2, VD]),
                                        ALU.mult))
                tt = TT[:, b, :, :].rearrange("p (n h) d -> p n h d", h=2)
                dve.tensor_tensor(DD[:, b, :, :], tt[:, :, 0, :], tt[:, :, 1, :], ALU.add).then_inc(s_hd, 1)
            for b in range(B):
                dve.wait_ge(s_hs, b + 1)
                dve.tensor_reduce(MS[:, b, :], SQ[:, :, :], AX.X, ALU.add).then_inc(s_ms, 1)
            for b in range(B):
                dve.wait_ge(s_hd, b + 1)
                dve.wait_ge(s_hr, b + 1)
                fence(dve.tensor_scalar(RL[:, b, 0:TB * HEADS], MS[:, b, :], 1.0 - LAMBDA_INIT, None, ALU.mult))
                dve.tensor_tensor(DD[:, b, :, :], DD[:, b, :, :],
                                  RL[:, b, 0:TB * HEADS].rearrange("p (n o) -> p n o", o=1).broadcast_to([P, TB * HEADS, VD]),
                                  ALU.mult).then_inc(s_hn, 1)
            for g in range(NG):
                dve.wait_ge(s_wo, g + 1)
                xg = X[:, g * GT:(g + 1) * GT, :].rearrange("p a b -> p (a b)")
                dve.tensor_tensor(xg, ps[:, 2 + g, :], xg, ALU.add).then_inc(s_x1, 1)

            def ffn_dve(f, before):
                def head_steps(g):
                    tiles = range(g * GT, (g + 1) * GT)

                    def ln():
                        stats(tiles, lambda t: X[:, t, :], f["var"])

                    def norm():
                        dve.wait_ge(f["var"], g + 1)
                        dve.wait_ge(f["rstd"], g + 1)
                        normalise(tiles, lambda t: FXN[:, t, :], lambda t: X[:, t, :], f["xn"])

                    def b4(a):
                        return a.rearrange("p (t o) -> p t o", o=1).broadcast_to([P, GT, NE])

                    def logits():
                        dve.wait_ge(f["lg"], g + 1)
                        src = ps[:, 2, 0:GT * OHR].rearrange("p (t e) -> p t e", t=GT)[:, :, 0:NE]
                        fence(dve.tensor_tensor(LG[:, g, :, :], src,
                                                rb[:, :].rearrange("p (o e) -> p o e", o=1).broadcast_to([P, GT, NE]),
                                                ALU.add))
                        fence(dve.tensor_reduce(MX[:, 0, g, :], LG[:, g, :, :], AX.X, ALU.max))
                        dve.tensor_tensor(LG[:, g, :, :], LG[:, g, :, :], b4(MX[:, 0, g, :]), ALU.subtract
                                          ).then_inc(f["sub"], 1)

                    def choose():
                        dve.wait_ge(f["exp"], g + 1)
                        dve.tensor_reduce(MX[:, 1, g, :], LE[:, g, :, :], AX.X, ALU.add)
                        fence(dve.tensor_reduce(MX[:, 2, g, :], LE[:, g, :, :], AX.X, ALU.max))
                        dve.reciprocal(MX[:, 3, g, :], MX[:, 1, g, :])
                        fence(dve.tensor_tensor(LG[:, g, :, :], LE[:, g, :, :], b4(MX[:, 2, g, :]), ALU.is_ge))
                        dve.tensor_tensor(MX[:, 3, g, :], MX[:, 3, g, :], MX[:, 2, g, :], ALU.mult)
                        fence(dve.tensor_tensor(LG[:, g, :, :], LG[:, g, :, :],
                                                rev[:, :].rearrange("p (o e) -> p o e", o=1).broadcast_to([P, GT, NE]),
                                                ALU.mult))
                        fence(dve.tensor_reduce(MX[:, 4, g, :], LG[:, g, :, :], AX.X, ALU.max))
                        if g >= 2:
                            dve.wait_ge(f["oht"], g - 1)
                        for k in range(GT):
                            last = dve.tensor_tensor(
                                OH[:, g % 2, k, :, :],
                                LG[:, g, k, :].rearrange("p (o e) -> p o e", o=1).broadcast_to([P, COPIES, NE]),
                                MX[:, 4, g, k:k + 1].rearrange("p (o e) -> p o e", o=1).broadcast_to([P, COPIES, NE]),
                                ALU.is_equal)
                        last.then_inc(f["oh"], 1)

                    return {0: ln, 1: norm, 4: logits, 5: choose}

                dve.wait_ge(*before)
                for step in head_steps(0).values():
                    step()
                for g in range(NG):
                    steps = head_steps(g + 1) if g + 1 < NG else {}
                    for e in range(NE):
                        n = g * NE + e
                        dve.wait_ge(f["g"], n + 1)
                        if n >= 4:
                            back = n - 4
                            if back % NE == NE - 1:
                                dve.wait_ge(f["y"], back // NE + 1)
                            else:
                                dve.wait_ge(f["e"], back - back // NE + 1)
                        dve.tensor_tensor(XM[:, e % 4, :], ps[:, 3 + n % 2, :], FXT[:, g * W5:(g + 1) * W5], ALU.mult
                                          ).then_inc(f["xm"], 1)
                        if e in steps:
                            steps[e]()
                    dve.wait_ge(f["yt"], g + 1)
                    for k in range(GT):
                        t = g * GT + k
                        last = dve.scalar_tensor_tensor(out=X[:, t, :], in0=ps[:, 7, k * P:(k + 1) * P],
                                                        scalar=MX[:, 3, g, k:k + 1], in1=X[:, t, :],
                                                        op0=ALU.mult, op1=ALU.add)
                    last.then_inc(f["x"], 1)

            dve.wait_ge(s_w2, 16 * 12)
            dve.wait_ge(s_cst, 3)
            ffn_dve(ffn[0], (s_x1, NG))

            dve.wait_ge(ffn[0]["x"], NG)
            for g in range(NG):
                stats(range(g * GT, (g + 1) * GT), lambda t: X[:, t, :], la["var"])
            for g in range(NG):
                dve.wait_ge(la["var"], g + 1)
                dve.wait_ge(la["rstd"], g + 1)
                normalise(range(g * GT, (g + 1) * GT), lambda t: BX[:, t, :], lambda t: X[:, t, :], la["xn"])
            for g in range(NG):
                for qk in range(2):
                    n = 2 * g + qk
                    dve.wait_ge(la["sq"], n + 1)
                    fence(dve.tensor_reduce(NN[:, qk, g * GT:(g + 1) * GT, :],
                                            QKSQ[:, n % 2, :].rearrange("p (t h d) -> p t h d", t=GT, h=LH),
                                            AX.X, ALU.add))
                    nn = NN[:, qk, g * GT:(g + 1) * GT, :].rearrange("p a b -> p (a b)")
                    dve.tensor_scalar(nn, nn, 0.5, None, ALU.mult).then_inc(la["nn"], 1)
            dve.wait_ge(la["nn"], 2 * NG)
            for t in range(NT):
                for qk in range(2):
                    n = 2 * t + qk
                    dve.wait_ge(la["pr"], n + 1)
                    fence(dve.tensor_reduce(RM[:, qk, t, :], ps[:, n % 6, 0:LH * LM].rearrange("p (h m) -> p h m", h=LH),
                                            AX.X, ALU.max))
                    fence(dve.tensor_tensor(RM[:, qk, t, :], RM[:, qk, t, :], NN[:, qk, t, :], ALU.subtract))
                    dve.scalar_tensor_tensor(out=RM[:, qk, t, :], in0=RM[:, qk, t, :], scalar=-1.0,
                                             in1=NN[:, qk, t, :], op0=ALU.mult, op1=ALU.subtract).then_inc(la["rm"], 1)
            mt4 = maskT[:, :].rearrange("p (o q) -> p o q", o=1).broadcast_to([P, LU, P])
            ao = AO[:, :, :].rearrange("p (b t) (h d) -> p b h t d", b=B, h=LH)

            def causal(c):
                dve.wait_ge(la["at"], c + 1)
                if c >= 2:
                    dve.wait_ge(la["o"], c - 1)
                dve.tensor_tensor(AM[:, c % 2, :, :], ps[:, c % 2, :].rearrange("p (j q) -> p j q", j=LU), mt4,
                                  ALU.mult).then_inc(la["ate"], 1)

            causal(0)
            for c in range(TB):
                if c < TB - 1:
                    dve.wait_ge(la["st"], c + 1)
                    src = ps[:, 2 + c % 2, 0:LU * VW].rearrange("p (j v) -> p j v", j=LU)
                    if c == 0:
                        dve.tensor_copy(ST[:, 0, :, :], src).then_inc(la["ste"], 1)
                    else:
                        dve.wait_ge(la["ste"], c)
                        dve.tensor_tensor(ST[:, c, :, :], src, ST[:, c - 1, :, :], ALU.add).then_inc(la["ste"], 1)
                if c + 1 < TB:
                    causal(c + 1)
                dve.wait_ge(la["o"], c + 1)
                res = ps[:, 4 + c % 2, 0:LU * VW].rearrange("p (j v) -> p j v", j=LU)
                fence(dve.tensor_scalar(DN[:, c % 2, :], res[:, :, LD], FEAT_EPS, None, ALU.add))
                fence(dve.reciprocal(DN[:, c % 2, :], DN[:, c % 2, :]))
                for b in range(B):
                    last = dve.tensor_tensor(
                        ao[:, b, :, c, :], res[:, b * LH:(b + 1) * LH, 0:LD],
                        DN[:, c % 2, b * LH:(b + 1) * LH].rearrange("p (j o) -> p j o", o=1).broadcast_to([P, LH, LD]),
                        ALU.mult)
                last.then_inc(la["oe"], 1)
            for g in range(NG):
                dve.wait_ge(la["wo"], g + 1)
                bg = BX[:, g * GT:(g + 1) * GT, :].rearrange("p a b -> p (a b)")
                dve.tensor_tensor(bg, ps[:, 2 + g, :], bg, ALU.add).then_inc(la["res"], 1)
                dve.wait_ge(la["res"], g + 1)
                stats(range(g * GT, (g + 1) * GT), lambda t: BX[:, t, :], la["var2"])
            g4 = gam[:, :].rearrange("p (o d) -> p o d", o=1).broadcast_to([P, GT, D])
            b4 = bet[:, :].rearrange("p (o d) -> p o d", o=1).broadcast_to([P, GT, D])
            for g in range(NG):
                dve.wait_ge(la["var2"], g + 1)
                dve.wait_ge(la["rstd2"], g + 1)
                normalise(range(g * GT, (g + 1) * GT), lambda t: H2[:, t, :], lambda t: BX[:, t, :], la["h1"])
                dve.wait_ge(la["h1"], g + 1)
                hg = H2[:, g * GT:(g + 1) * GT, :]
                fence(dve.tensor_tensor(hg, hg, g4, ALU.mult))
                dve.tensor_tensor(hg, hg, b4, ALU.add).then_inc(la["h"], 1)
            for g in range(NG):
                dve.wait_ge(la["yt"], g + 1)
                xg = X[:, g * GT:(g + 1) * GT, :].rearrange("p a b -> p (a b)")
                dve.tensor_tensor(xg, ps[:, 7, :], xg, ALU.add).then_inc(la["x"], 1)
            ffn_dve(ffn[1], (la["x"], NG))


lam_sums = 4
c_feat = 1.0 / math.sqrt(LM)


def kernel(**inputs):
    import numpy as _np
    import concourse.bacc as _bacc
    from concourse import mybir as _mybir
    from concourse.bass_utils import run_bass_kernel_spmd as _run

    a, b, f = "L0_attn_a_", "L0_attn_b_", "L0_ffn_"
    g = {k: _np.asarray(v) for k, v in inputs.items()}
    arrays = [
        ("x", g[a + "x"].reshape(TOK, D)),
        ("a_wqT", g[a + "Wq"].T), ("a_wkT", g[a + "Wk"].T), ("a_wvT", g[a + "Wv"].T), ("a_woT", g[a + "Wo"].T),
        ("a_lam", _np.stack([g[a + "lq1"], g[a + "lk1"], g[a + "lq2"], g[a + "lk2"]])),
        ("b_wq", g[b + "Wq"]), ("b_wk", g[b + "Wk"]), ("b_wv", g[b + "Wv"]), ("b_wo", g[b + "Wo"]),
        ("b_omegaT", g[b + "omega"].T),
        ("b_w1", g[b + "W1"]), ("b_b1", g[b + "b1"].reshape(FC, P).T), ("b_w2", g[b + "W2"]),
        ("b_b2", g[b + "b2"].reshape(D, 1)), ("b_gamma", g[b + "gamma"].reshape(1, D)),
        ("b_beta", g[b + "beta"].reshape(1, D)),
        ("f_rw", g[f + "router_w"]), ("f_rb", g[f + "router_b"].reshape(1, NE)),
        ("f_ew", g[f + "expert_w"].transpose(1, 0, 2)), ("f_eb", g[f + "expert_b"]),
    ]
    nc = _bacc.Bacc("TRN2", target_bir_lowering=False, num_devices=1)
    feed, args = {}, []
    for name, arr in arrays:
        arr = _np.ascontiguousarray(arr)
        feed[name] = arr
        args.append(nc.dram_tensor(name, arr.shape, _mybir.dt.from_np(arr.dtype), kind="ExternalInput").ap())
    args.append(nc.dram_tensor("out", (TOK, D), _mybir.dt.float32, kind="ExternalOutput").ap())
    hybrid_kernel(nc, *args)
    r = _run(nc, [feed], core_ids=[0])
    return r.results[0]["out"].reshape(B, S, D)
```

```python
import math
from contextlib import ExitStack

import concourse.bass as bass
from concourse import mybir

PACE = 17
MT_AT = 15
MT1_AT = 6
ST1_AT = 4
STO_AT = 17
O1_AT = 19
LEFT = 1
ONEHOT_E = 6
LOGITS_E = 3
CHOOSE_E = 4
COMBINE_E = 1
ST_AT = 9
EARLY = 0
CLEARED = 6

P = 128
B, S, D = 2, 1024, 128
TOK = B * S
NT = TOK // P
TB = S // P
GT = 4
NG = NT // GT
W5 = GT * P
HEADS = 8
HD = D // HEADS // 2
VD = 2 * HD
NU = B * HEADS
SLOTS = 3
TERMS = 6
KROWS = TERMS * HD
ZROWS = 96
MROW = 96
PARTS = 3
LAMBDA_INIT = 0.8 - 0.6 * math.exp(-0.3 * 6)
ATT_EPS = 1e-5
HEAD_GAIN = 1.0 - LAMBDA_INIT
HEADS_AT = 64
HEADS_C = 1
INVERT_AT = 0
LN_EPS = 1e-5
SCORE_SCALE = HD ** -0.5
OPERAND_BOUND = 4.0e18
MASKED = -3.0e38
AG = 12
BC = 20
NE = 8
COPIES = 12
OHR = COPIES * NE
LH, LD, LM = 2, 64, 128
LU = B * LH
FEAT_EPS = 1e-6
LN2_EPS = 1e6
VW = 96
FF = 512
FC = FF // P

fp32 = mybir.dt.float32
bf16 = mybir.dt.bfloat16
ALU = mybir.AluOpType
ACT = mybir.ActivationFunctionType
AX = mybir.AxisListType

A_GROUPS = [(i, (h,)) for i in (7, 6, 5, 4) for h in (0, 1)] + [(i, (0, 1)) for i in (3, 2, 1, 0)]
B_CHUNKS = []
for half in (0, 1):
    for kt in range(8 if half == 0 else 4):
        width = min(512, 128 * ((8 if half == 0 else 4) - kt))
        for heads in (((0,), (1,)) if width > 256 else ((0, 1),)):
            B_CHUNKS.append((half, kt, heads, width))
assert len(A_GROUPS) == AG and len(B_CHUNKS) == BC
MASKS = [(half, kt) for half in (0, 1) for kt in ((4, 5, 6, 7) if half == 0 else (0, 1, 2, 3))]


def last_chunk(half, kt):
    return max(c for c, (hf, k, _, _) in enumerate(B_CHUNKS) if (hf, k) == (half, kt))


def hybrid_kernel(nc, x_d, wqT_d, wkT_d, wvT_d, woT_d, lam_d, bwq_d, bwk_d, bwv_d, bwo_d, omT_d,
                  w1_d, b1_d, w2_d, b2_d, gam_d, bet_d, rw_d, rb_d, ew_d, eb_d, out_d):
    ctx = ExitStack()
    with ctx:
        def sb(name, shape, dt=fp32):
            return ctx.enter_context(nc.sbuf_tensor(name, shape, dt))

        def sem(name):
            return ctx.enter_context(nc.semaphore(name))

        X = sb("X", [P, NT, D])
        arena = sb("arena", [P, NU * 2 * W5])
        E = sb("E", [P, 12, 2, W5])
        Qop = sb("Qop", [P, SLOTS, 2, S], bf16)
        Kop = sb("Kop", [P, SLOTS, 2, S], bf16)
        Vu = sb("Vu", [P, NU, TB, 32])
        Vs = sb("Vs", [P, SLOTS, TB, 32])
        NM = sb("NM", [P, SLOTS, 2, 2, 4])
        MR = sb("MR", [P, SLOTS, 2, 2, 4])
        M3 = sb("M3", [P, SLOTS, 2, 2, PARTS, 4], bf16)
        MT = sb("MT", [24, SLOTS, 2, P], bf16)
        ident = sb("ident", [P, P])
        identb = sb("identb", [P, P], bf16)
        maskA = sb("maskA", [P, P], bf16)
        maskT = sb("maskT", [P, P])
        half_c = sb("half_c", [P, NT])
        wT = sb("wT", [P, 4, D])
        lamv = sb("lamv", [P, 4, HD])
        lamw = sb("lamw", [P, 2, HD])
        lams = sb("lams", [P, 4])
        warm = sb("warm", [P, 1])
        st = sb("st", [P, NT, 6])
        mv = sb("mv", [P, NT, 2])
        rstd = sb("rstd", [P, NT])
        ve = sb("ve", [P, NT])
        rw = sb("rw", [P, OHR])
        rb = sb("rb", [P, NE])
        ew = sb("ew", [P, NE, D])
        ebf = sb("ebf", [NE, D])
        ebr = sb("ebr", [NE, D])
        ebp = sb("ebp", [NE, PARTS, D], bf16)
        eb = sb("eb", [OHR, D], bf16)
        sel = sb("sel", [OHR, NE, P], bf16)
        rev = sb("rev", [P, NE])
        bw = sb("bw", [P, 4, D])
        om = sb("om", [P, LH, LM])
        w1 = sb("w1", [P, FF])
        b1 = sb("b1", [P, FC])
        w2 = sb("w2", [P, FC, D])
        b2 = sb("b2", [P, 1])
        pick = sb("pick", [P, 2 * (VD + 1)])
        gam = sb("gam", [P, D])
        bet = sb("bet", [P, D])
        ps = ctx.enter_context(nc.psum_tensor("ps", [P, 8, W5], fp32))

        def view(big, at, shape):
            n = 1
            for k in shape:
                n *= k
            flat = big[:, at:at + n]
            if len(shape) == 1:
                return flat
            names = "abcd"[:len(shape)]
            return flat.rearrange("p (" + " ".join(names) + ") -> p " + " ".join(names),
                                  **{c: k for c, k in zip(names[1:], shape[1:])})

        Ef = E[:, :, :, :].rearrange("p a b c -> p (a b c)")
        XN = view(arena, 0, [NT, D])
        XT = view(arena, 2048, [TOK])
        QSb = [view(arena, 4096, [2, S]), view(arena, 14336, [2, S])]
        QR = view(arena, 6144, [2, S])
        QP = view(arena, 8192, [3072]).bitcast(bf16).rearrange("p (q t s) -> p q t s", q=2, t=3)
        QP2 = view(arena, 11264, [3072]).bitcast(bf16).rearrange("p (q t s) -> p q t s", q=2, t=3)
        QPb = [QP, QP2]
        OT = view(arena, 2048, [2, W5])
        TT = view(arena, 3072, [TB, 2, VD])
        OD = view(arena, 3328, [TB, VD])
        SQ = view(arena, 3456, [TB, VD])
        RL = view(arena, 3584, [TB, 2])
        MS = view(arena, 3600, [2, TB])
        MV = view(arena, 3616, [TB])
        DD = view(arena, 0, [TB, NU * VD])
        OTT = view(arena, 14336, [TOK])
        FXN = view(arena, 2048, [NT, D])
        FXT = view(arena, 4096, [TOK])
        XM = view(arena, 6144, [4, W5])
        YT = view(arena, 8192, [2, W5])
        LG = sb("LG", [P, NG, GT, NE])
        LE = sb("LE", [P, NG, GT, NE])
        MX = sb("MX", [P, 5, NG, GT])
        OH = sb("OH", [P, 2, GT, COPIES, NE], bf16)
        OHT = sb("OHT", [OHR, 2, W5], bf16)
        BX = view(arena, 0, [NT, D])
        BXT = view(arena, 2048, [TOK])
        QKT = view(arena, 4096, [2, TOK])
        EQK = view(arena, 8192, [2, NT, LH, LM])
        KP = view(Ef, 0, [NT, LH, LM])
        QKPT = view(Ef, 4096, [2, NT, LH, P])
        VA = sb("VA", [P, NT, LH, VW])
        Vuf = Vu[:, :, :, :].rearrange("p u a b -> p (u a b)")
        ST = view(Vuf, 0, [TB - 1, LU, VW])
        AM = view(Vuf, 2688, [2, LU, P])
        AO = view(arena, 2048, [NT, D])
        QKSQ = view(arena, 2048, [2, W5])
        NN = sb("NN", [P, 2, NT, LH])
        RM = sb("RM", [P, 2, NT, LH])
        DN = sb("DN", [P, 2, LU])
        AOT = view(arena, 8192, [TOK])
        H2 = view(arena, 10240, [NT, D])
        HT = view(arena, 12288, [TOK])
        HID = view(arena, 4096, [FC, W5])
        UT = view(arena, 14336, [2, W5])

        def hid(g):
            return view(arena, 4096 + 2048 * (g % 2), [FC, W5])

        q_scr = nc.dram_tensor("q_scratch", [NU * 2 * KROWS, S], bf16, kind="Internal").ap()
        k_scr = nc.dram_tensor("k_scratch", [NU * 2 * KROWS, S], bf16, kind="Internal").ap()

        s_x = [sem(f"x_loaded_{g}") for g in range(NG)]
        s_w = sem("attention_weights_loaded")
        s_lam = sem("lambda_vectors_loaded")
        s_w2 = sem("other_weights_loaded")
        s_om = sem("omega_loaded")
        s_rw = sem("router_loaded")
        s_ebl = sem("expert_bias_loaded")
        s_ebd = sem("expert_bias_placed")
        s_rwz = sem("router_cleared")
        s_omz = sem("omega_cleared")
        s_cst = sem("constants_ready")
        s_cz = sem("constants_cleared")
        s_oz = sem("operands_cleared")
        s_dve = sem("vector_chain")
        s_pool = sem("pool_chain")
        s_pass = sem("pool_past_a_wait")
        s_act = sem("lambda_exponentials_ready")
        s_lsum = sem("lambda_sums_ready")
        s_var = sem("variances_ready")
        s_rstd = sem("rstd_ready")
        s_xn = sem("normalised")
        s_xt = sem("transposed_in_psum")
        s_xte = sem("transposed_in_sbuf")
        s_qk = sem("qk_projected")
        s_qke = sem("qk_scaled")
        s_qkc = sem("qk_bounded")
        s_vp = sem("v_projected")
        s_ve = sem("v_stored")
        s_cut = sem("steps_of_cutting_k_and_q")
        s_scr = [sem(f"scratch_written_{b}") for b in range(B)]
        s_ld = [sem(f"operands_loaded_{s}") for s in range(SLOTS)]
        s_m = [[sem(f"maxima_placed_{s}_{h}") for h in range(2)] for s in range(SLOTS)]
        s_a = sem("score_group_ready")
        s_max = sem("maximum_taken")
        s_sstep = sem("split_step")
        s_split = sem("maxima_split")
        s_mt = sem("maxima_transposed")
        s_mte = sem("maxima_in_sbuf")
        s_b = sem("score_chunk_ready")
        s_exp = sem("chunk_exponentiated")
        s_mask = sem("diagonal_masked")
        s_pv = sem("outputs_accumulated")
        s_pve = sem("outputs_stored")
        s_vs = sem("values_staged")
        s_lamr = sem("lambda_ready")

        block = ctx.enter_context(nc.Block())


        s_hp = sem("heads_as_tokens")
        s_hq = sem("head_sums_inverted")
        s_ht = sem("heads_divided")
        s_hs = sem("head_squares_summed")
        s_hstep = sem("head_step")
        s_hn = sem("heads_normalised")
        s_oT2 = sem("heads_transposed")
        s_oT2e = sem("heads_transposed_in_sbuf")
        s_wo = sem("attention_projected")
        s_x1 = sem("residual_updated")

        ffn = [dict((n, sem(f"ffn{k}_{n}")) for n in (
            "var", "rstd", "xn", "xt", "xte", "lg", "sub", "exp", "oh", "oht", "ohte",
            "g", "xm", "e", "y", "ye", "yt", "x")) for k in range(2)]
        la = dict((n, sem(f"la_{n}")) for n in (
            "var", "rstd", "xn", "xt", "xte", "qk", "qke", "v", "ve", "vz", "sq", "nt", "nn", "pr", "rm",
            "ex", "kp", "ft", "fte", "at", "ate", "st", "ste", "o", "oe", "ot", "ote", "wo", "res",
            "var2", "rstd2", "h1", "h", "ht", "hte", "u", "ue", "y", "ye", "yt", "x", "nsq"))
        s_out = sem("out_written")

        @block.sync
        def _(sp):
            xv = x_d.rearrange("(t p) d -> p t d", p=P)
            for g in range(NG):
                sp.dma_start(X[:, g * GT:(g + 1) * GT, :], xv[:, g * GT:(g + 1) * GT, :]).then_inc(s_x[g], 16)
                if g == 1:
                    for i, w in enumerate((wqT_d, wkT_d, wvT_d, woT_d)):
                        sp.dma_start(wT[:, i, :], w).then_inc(s_w, 16)
            sp.dma_start(lamv[:, :, :], lam_d.rearrange("(o a) d -> o a d", o=1).broadcast_to([P, 4, HD])).then_inc(s_lam, 16)
            for k, w in enumerate((bwq_d, bwk_d, bwv_d, bwo_d)):
                sp.dma_start(bw[:, k, :], w).then_inc(s_w2, 16)
            sp.dma_start(w1[:, :], w1_d).then_inc(s_w2, 16)
            sp.dma_start(w2[:, :, :], w2_d.rearrange("(c p) d -> p c d", p=P)).then_inc(s_w2, 16)
            sp.dma_start(b1[:, :], b1_d).then_inc(s_w2, 16)
            sp.dma_start(b2[:, :], b2_d).then_inc(s_w2, 16)
            sp.dma_start(gam[:, :], gam_d.broadcast_to([P, D])).then_inc(s_w2, 16)
            sp.dma_start(bet[:, :], bet_d.broadcast_to([P, D])).then_inc(s_w2, 16)
            sp.dma_start(rb[:, :], rb_d.broadcast_to([P, NE])).then_inc(s_w2, 16)
            sp.dma_start(ew[:, :, :], ew_d).then_inc(s_w2, 16)
            sp.dma_start(ebf[:, :], eb_d).then_inc(s_ebl, 16)

            def write_operands(b):
                rows = [scr.rearrange("(b r t) s -> b r t s", b=B, t=TERMS)[b] for scr in (q_scr, k_scr)]
                for part, terms in enumerate(((0, 1, 2), (3, 4), (5,))):
                    sp.wait_ge(s_cut, 10 * b + (2, 4, 5)[part])
                    for t in terms:
                        sp.dma_start(rows[1][:, t, :], QPb[b][:, 1, part, :]).then_inc(s_scr[b], 16)
                sp.wait_ge(s_cut, 10 * b + 10)
                for t0, n in ((0, 3), (3, 2), (5, 1)):
                    sp.dma_start(rows[0][:, t0:t0 + n, :], QPb[b][:, 0, 0:n, :]).then_inc(s_scr[b], 16)

            def load_operands(w, slot):
                for scr, op in ((q_scr, Qop), (k_scr, Kop)):
                    sp.dma_start(op[0:KROWS, slot, :, :],
                                 scr[bass.ds(w * (2 * KROWS), 2 * KROWS), :].rearrange("(h r) s -> r h s", h=2)
                                 ).then_inc(s_ld[slot], 16)

            def place_maxima(slot, half):
                q0 = (1 - half) * W5
                for h in range(2):
                    sp.dma_start(Qop[MROW:MROW + PARTS, slot, h, q0:q0 + W5].rearrange("r (t q) -> r t q", t=4),
                                 MT[12 * h:12 * h + 12, slot, half, :]).then_inc(s_m[slot][half], 16)

            write_operands(0)
            sp.wait_ge(s_scr[0], 16 * 9)
            sp.wait_ge(s_oz, CLEARED)
            load_operands(0, 0)
            load_operands(1, 1)
            sp.wait_ge(s_mte, 1)
            place_maxima(0, 0)

            def unit(u, s, load=True, ahead=True):
                sp.wait_ge(s_b, u * BC + 1)
                if load:
                    load_operands(u + 2, (s + 2) % SLOTS)
                sp.wait_ge(s_mte, 2 * u + 2)
                place_maxima(s, 1)
                if ahead:
                    sp.wait_ge(s_mte, 2 * u + 3)
                    place_maxima((s + 1) % SLOTS, 0)

            for u in range(SLOTS):
                unit(u, u)
            write_operands(1)
            sp.wait_ge(s_scr[1], 16 * 9)
            with sp.Fori(1, 4) as t:
                for s in range(SLOTS):
                    unit(t * SLOTS + s, s)
            for u in range(12, NU):
                unit(u, u % SLOTS, load=u + 2 < NU, ahead=u + 1 < NU)
            ov = out_d.rearrange("(t p) d -> p t d", p=P)
            for g in range(NG):
                sp.wait_ge(ffn[1]["x"], g + 1)
                sp.dma_start(ov[:, g * GT:(g + 1) * GT, :], X[:, g * GT:(g + 1) * GT, :]).then_inc(s_out, 16)
            sp.wait_ge(s_out, 16 * NG)

        @block.gpsimd
        def _(pool):
            chain = [0]

            def link(ins):
                chain[0] += 1
                ins.then_inc(s_pool, 1)
                pool.wait_ge(s_pool, chain[0])

            pool.memset(ident[:, :], 0.0).then_inc(s_cz, 1)
            pool.wait_ge(s_cz, 1)
            pool.affine_select(out=ident[:, :], in_=ident[:, :], compare_op=ALU.not_equal, fill=1.0, base=0,
                               pattern=[[-1, P]], channel_multiplier=1).then_inc(s_cst, 1)
            pool.memset(half_c[:, :], -0.5).then_inc(s_cst, 1)

            def rsqrt(out, var, tmp, eps, scale, done):
                link(pool.tensor_scalar(tmp, var, scale, eps, ALU.mult, ALU.add))
                pool.tensor_tensor(out, tmp, half_c[:, 0:1].broadcast_to(tmp.shape) if len(tmp.shape) > 1 else tmp,
                                   ALU.pow).then_inc(done, 1)

            pool.wait_ge(s_cst, 2)
            for g in range(NG):
                pool.wait_ge(s_var, g + 1)
                rsqrt(rstd[:, g * GT:(g + 1) * GT], mv[:, g * GT:(g + 1) * GT, 1], ve[:, g * GT:(g + 1) * GT],
                      LN_EPS, 1.0, s_rstd)
                if g == 1:
                    pool.memset(Qop[:, :, :, :].bitcast(fp32), 0.0).then_inc(s_oz, 1)
            link(pool.memset(Kop[:, :, :, :], 1.0))
            pool.memset(Kop[0:ZROWS, :, :, :].bitcast(fp32), 0.0).then_inc(s_oz, 1)
            link(pool.memset(maskT[:, :], 1.0))
            link(pool.affine_select(out=maskT[:, :], in_=maskT[:, :], compare_op=ALU.is_ge, fill=0.0, base=0,
                                    pattern=[[1, P]], channel_multiplier=-1))
            link(pool.memset(maskA[:, :], 0.0))
            pool.affine_select(out=maskA[:, :], in_=maskA[:, :], compare_op=ALU.is_ge, fill=MASKED, base=0,
                               pattern=[[-1, P]], channel_multiplier=1).then_inc(s_oz, 1)
            pool.tensor_copy(identb[:, :], ident[:, :]).then_inc(s_oz, 1)
            pool.memset(E[:, 8 + 1, :, 0:P], 0.0).then_inc(s_pv, 3)
            pool.memset(Vu[:, :, :, VD:32], 0.0).then_inc(s_vs, 1)
            pool.wait_ge(s_vs, 1)
            pool.memset(Vu[:, :, :, VD:VD + 1], 1.0).then_inc(s_oz, 1)
            link(pool.memset(pick[:, :], 0.0))
            for n in range(4):
                cols = pick[:, (n // 2) * (VD + 1):(n // 2 + 1) * (VD + 1)]
                last = pool.affine_select(out=cols, in_=cols, compare_op=ALU.not_equal, fill=1.0, base=-32 * n,
                                          pattern=[[-1, VD + 1]], channel_multiplier=1)
                last.then_inc(s_oz, 1) if n == 3 else link(last)

            def wait(sm, value):
                pool.wait_ge(sm, value)
                pool.sem_inc(s_pass, 1)

            def split(n, slot, half):
                src = NM[:, slot, half, :, :]
                part = [M3[:, slot, half, :, k, :] for k in range(PARTS)]
                rem = MR[:, slot, half, :, :]
                pool.tensor_copy(part[0], src).then_inc(s_sstep, 1)
                wait(s_sstep, n * 3 + 1)
                pool.tensor_tensor(rem, src, part[0], ALU.subtract).then_inc(s_sstep, 1)
                wait(s_sstep, n * 3 + 2)
                pool.tensor_copy(part[1], rem).then_inc(s_sstep, 1)
                wait(s_sstep, n * 3 + 3)
                pool.tensor_tensor(part[2], rem, part[1], ALU.subtract).then_inc(s_split, 1)

            def stage_values(u, slot):
                pool.tensor_copy(Vs[:, slot, :, :].rearrange("p a b -> p (a b)"),
                                 Vu[:, :, :, :].rearrange("p u a b -> p (u a b)")[:, bass.ds(u * (TB * 32), TB * 32)]
                                 ).then_inc(s_vs, 1)

            def mask(u, j):
                half, kt = MASKS[j]
                q0 = P * (kt % 4)
                wait(s_exp, u * BC + (2 + last_chunk(half, kt) + 1))
                diag = E[:, half * 8 + kt, :, q0:q0 + P]
                pool.affine_select(out=diag, in_=diag, compare_op=ALU.is_ge, fill=0.0, base=0,
                                   pattern=[[0, 2], [1, P]], channel_multiplier=-1).then_inc(s_mask, 1)

            pool.memset(rw[:, :], 0.0).then_inc(s_rwz, 1)
            pool.wait_ge(s_rwz, 1)
            pool.dma_start(rw[:, 0:NE], rw_d).then_inc(s_rw, 16)
            pool.memset(om[:, :, :], 0.0).then_inc(s_omz, 1)
            pool.wait_ge(s_omz, 1)
            for h in range(LH):
                pool.dma_start(om[h * LD:(h + 1) * LD, h, :], omT_d).then_inc(s_om, 16)
            link(pool.memset(eb[:, :], 0.0))
            pool.wait_ge(s_ebl, 16)
            link(pool.tensor_copy(ebp[:, 0, :], ebf[:, :]))
            link(pool.tensor_tensor(ebr[:, :], ebf[:, :], ebp[:, 0, :], ALU.subtract))
            link(pool.tensor_copy(ebp[:, 1, :], ebr[:, :]))
            link(pool.tensor_tensor(ebp[:, 2, :], ebr[:, :], ebp[:, 1, :], ALU.subtract))
            for k in range(PARTS):
                pool.dma_start(eb[k * NE:(k + 1) * NE, :], ebp[:, k, :]).then_inc(s_ebd, 16)
            link(pool.memset(sel[:, :, :], 0.0))
            link(pool.affine_select(out=sel[:, :, :], in_=sel[:, :, :], compare_op=ALU.not_equal, fill=1.0, base=0,
                                    pattern=[[-1, NE], [0, P]], channel_multiplier=1))
            for e in range(NE):
                last = pool.memset(rev[:, e:e + 1], float(NE - e))
            last.then_inc(s_cst, 1)
            pool.wait_ge(s_ve, NG)
            pool.wait_ge(s_oz, CLEARED)
            stage_values(0, 0)
            wait(s_max, 8)
            split(0, 0, 0)
            wait(s_max, AG)
            split(1, 0, 1)

            def heads(w):
                wait(s_ht, w + 1)
                pool.tensor_tensor(OD, TT[:, :, 0, :], TT[:, :, 1, :], ALU.add).then_inc(s_hstep, 1)
                wait(s_hstep, 4 * w + 1)
                pool.tensor_tensor(SQ, OD, OD, ALU.mult).then_inc(s_hstep, 1)
                wait(s_hs, w + 1)
                pool.tensor_scalar(MV, MS[:, 0, :], HEAD_GAIN ** -2 / VD, HEAD_GAIN ** -2 * ATT_EPS, ALU.mult, ALU.add
                                   ).then_inc(s_hstep, 1)
                wait(s_hstep, 4 * w + 3)
                pool.tensor_tensor(MS[:, 1, :], MV, half_c[:, 0:TB], ALU.pow).then_inc(s_hstep, 1)
                wait(s_hstep, 4 * w + 4)
                dst = DD[:, :, bass.ds(w * VD, VD)]
                pool.tensor_tensor(dst, OD, MS[:, 1, :].rearrange("p (t o) -> p t o", o=1).broadcast_to([P, TB, VD]),
                                   ALU.mult).then_inc(s_hn, 1)

            def unit(u, s, ahead=True, first=False):
                if ahead:
                    wait(s_pv, 2 * u + 1)
                    stage_values(u + 1, (s + 1) % SLOTS)
                if not first:
                    heads(u - 1)
                mask(u, 0)
                mask(u, 1)
                if ahead:
                    wait(s_max, u * AG + AG + 8)
                    split(2 * u + 2, (s + 1) % SLOTS, 0)
                for j in range(2, 8):
                    mask(u, j)
                if ahead:
                    wait(s_max, u * AG + 2 * AG)
                    split(2 * u + 3, (s + 1) % SLOTS, 1)

            for s in range(SLOTS):
                unit(s, s, first=s == 0)
            with pool.Fori(1, 5) as t:
                for s in range(SLOTS):
                    unit(t * SLOTS + s, s)
            unit(NU - 1, (NU - 1) % SLOTS, ahead=False)
            heads(NU - 1)

            def layer_norm(names, g, dst, src, eps):
                r = slice(g * GT, (g + 1) * GT)
                pool.wait_ge(names["var"], g + 1)
                rsqrt(rstd[:, r], mv[:, r, 1], ve[:, r], eps, 1.0, names["rstd"])
                pool.wait_ge(names["rstd"], g + 1)
                for t in range(g * GT, (g + 1) * GT):
                    last = pool.tensor_scalar(dst[:, t, :], src[:, t, :], mv[:, t, 0:1], rstd[:, t:t + 1],
                                              ALU.subtract, ALU.mult)
                last.then_inc(names["xn"], 1)

            for g in range(NG):
                layer_norm(ffn[0], g, FXN, X, LN_EPS)
            link(pool.memset(VA[:, :, :, LD:VW], 0.0))
            pool.memset(VA[:, :, :, LD:LD + 1], 1.0).then_inc(la["vz"], 1)
            for g in range(NG):
                layer_norm(la, g, BX, X, LN_EPS)
            c = 1.0 / math.sqrt(LM)
            for t in range(NT):
                pool.wait_ge(la["ex"], 4 * (t + 1))
                pool.tensor_scalar(KP[:, t, :, :].rearrange("p a b -> p (a b)"),
                                   EQK[:, 1, t, :, :].rearrange("p a b -> p (a b)"), c, FEAT_EPS,
                                   ALU.mult, ALU.add).then_inc(la["kp"], 1)
            for g in range(NG):
                r = slice(g * GT, (g + 1) * GT)
                pool.wait_ge(la["var2"], g + 1)
                rsqrt(rstd[:, r], mv[:, r, 1], ve[:, r], LN2_EPS, 1.0, la["rstd2"])
            for g in range(NG):
                layer_norm(ffn[1], g, FXN, X, LN_EPS)

        @block.scalar
        def _(act):
            for g in range(NG):
                act.wait_ge(s_xt, g + 1)
                act.copy(XT[:, g * W5:(g + 1) * W5], ps[:, g % 2, :]).then_inc(s_xte, 1)
                if g % 2 == 0:
                    continue
                b = g // 2
                for qk in range(2):
                    for n in range(2):
                        act.wait_ge(s_qk, 4 * b + 2 * qk + n + 1)
                        act.activation(QSb[b][:, qk, n * W5:(n + 1) * W5], ps[:, 2 + 2 * qk + n, :], ACT.Copy,
                                       scale=(SCORE_SCALE, 1.0)[qk]).then_inc(s_qke, 1)
                for g2 in (2 * b, 2 * b + 1):
                    act.wait_ge(s_vp, g2 + 1)
                    if g2 == 0:
                        act.wait_ge(s_oz, CLEARED)
                    src = ps[:, 6 + g2 % 2, :].rearrange("p (t h d) -> p h t d", t=GT, h=HEADS)
                    dst = Vu[:, b * HEADS:(b + 1) * HEADS, (g2 % 2) * GT:(g2 % 2 + 1) * GT, 0:VD]
                    for h in range(HEADS):
                        last = act.copy(dst[:, h, :, :], src[:, h, :, :])
                    last.then_inc(s_ve, 1)
            act.wait_ge(s_lsum, 1)
            act.activation(lams[:, 2:4], lams[:, 0:2], ACT.Exp).then_inc(s_act, 1)

            def exp_chunk(u, c):
                half, kt, heads, width = B_CHUNKS[c]
                act.wait_ge(s_b, u * BC + (1 + c + 1))
                if c in (0, 14):
                    act.wait_ge(s_pv, 2 * u + (half + 2))
                bank = 4 + c % 2
                dst = E[:, half * 8 + kt, heads[0]:heads[-1] + 1, W5 - width:W5]
                src = ps[:, bank, 0:len(heads) * width].rearrange("p (h q) -> p h q", h=len(heads))
                act.activation(dst, src, ACT.Exp).then_inc(s_exp, 1)

            def store_outputs(u, half, first):
                act.wait_ge(s_pv, 2 * u + (half + 4))
                if not first:
                    act.wait_ge(s_hp, u)
                act.copy(OT[:, half, :], ps[:, 6, :]).then_inc(s_pve, 1)

            act.wait_ge(s_oz, CLEARED)
            act.activation(warm[:, 0:1], half_c[:, 0:1], ACT.Exp).then_inc(s_exp, 2)

            def unit(u, first=False):
                for c in range(BC):
                    exp_chunk(u, c)
                    if c == STO_AT:
                        store_outputs(u, 0, first)
                store_outputs(u, 1, first)

            act.sem_inc(s_pve, 1)
            for s in range(SLOTS):
                unit(s, first=s == 0)
            with act.Fori(1, 5) as t:
                for s in range(SLOTS):
                    unit(t * SLOTS + s)
            unit(NU - 1)

            for g in range(NG):
                act.wait_ge(s_oT2, g + 1)
                act.copy(OTT[:, g * W5:(g + 1) * W5], ps[:, g % 2, :]).then_inc(s_oT2e, 1)

            def ffn_act(f):
                def copy_x(g):
                    act.wait_ge(f["xt"], g + 1)
                    act.copy(FXT[:, g * W5:(g + 1) * W5], ps[:, 0, :]).then_inc(f["xte"], 1)

                def choose(g):
                    act.wait_ge(f["sub"], g + 1)
                    act.activation(LE[:, g, :, :], LG[:, g, :, :], ACT.Exp).then_inc(f["exp"], 1)
                    act.wait_ge(f["oht"], g + 1)
                    if g >= 2:
                        act.wait_ge(f["y"], g - 1)
                    act.copy(OHT[:, g % 2, :], ps[0:OHR, 1, 0:W5 // 2].bitcast(bf16)).then_inc(f["ohte"], 1)

                def copy_y(g):
                    act.wait_ge(f["y"], g + 1)
                    if g >= 2:
                        act.wait_ge(f["yt"], g - 1)
                    act.copy(YT[:, g % 2, :], ps[:, 5 + g % 2, :]).then_inc(f["ye"], 1)

                copy_x(0)
                choose(0)
                for g in range(NG):
                    if g + 1 < NG:
                        copy_x(g + 1)
                    if g:
                        copy_y(g - 1)
                    if g + 1 < NG:
                        choose(g + 1)
                copy_y(NG - 1)

            ffn_act(ffn[0])
            for g in range(NG):
                act.wait_ge(la["xt"], g + 1)
                act.copy(BXT[:, g * W5:(g + 1) * W5], ps[:, g % 2, :]).then_inc(la["xte"], 1)
                for qk in range(2):
                    act.wait_ge(la["qk"], 2 * g + qk + 1)
                    act.activation(QKT[:, qk, g * W5:(g + 1) * W5], ps[:, 2 + qk, :], ACT.Copy,
                                   scale=LD ** -0.25).then_inc(la["qke"], 1)
                act.wait_ge(la["v"], g + 1)
                if g == 0:
                    act.wait_ge(la["vz"], 1)
                act.copy(VA[:, g * GT:(g + 1) * GT, :, 0:LD],
                         ps[:, 4, :].rearrange("p (t h d) -> p t h d", t=GT, h=LH)).then_inc(la["ve"], 1)
            for g in range(NG):
                for qk in range(2):
                    n = 2 * g + qk
                    act.wait_ge(la["nt"], n + 1)
                    if n >= 2:
                        act.wait_ge(la["nn"], n - 1)
                    act.activation(QKSQ[:, n % 2, :], ps[:, 6 + n % 2, :], ACT.Square).then_inc(la["sq"], 1)
            def store_features(t):
                act.wait_ge(la["ft"], t + 1)
                act.activation(QKPT[:, :, t, :, :], ps[:, 6 + t % 2, :].rearrange("p (q h s) -> p q h s", q=2, h=LH),
                               ACT.Copy, scale=c_feat, bias=FEAT_EPS).then_inc(la["fte"], 1)

            for t in range(NT):
                for qk in range(2):
                    n = 2 * t + qk
                    act.wait_ge(la["rm"], n + 1)
                    for h in range(LH):
                        act.activation(EQK[:, qk, t, h, :], ps[:, n % 6, h * LM:(h + 1) * LM], ACT.Exp,
                                       bias=RM[:, qk, t, h:h + 1]).then_inc(la["ex"], 1)
                if t >= 3:
                    store_features(t - 3)
            for t in range(NT - 3, NT):
                store_features(t)
            for g in range(NG):
                act.wait_ge(la["ot"], g + 1)
                act.copy(AOT[:, g * W5:(g + 1) * W5], ps[:, g % 2, :]).then_inc(la["ote"], 1)
            for g in range(NG):
                act.wait_ge(la["ht"], g + 1)
                act.copy(HT[:, g * W5:(g + 1) * W5], ps[:, g % 2, :]).then_inc(la["hte"], 1)
                for f in range(FC):
                    n = g * FC + f
                    act.wait_ge(la["u"], n + 1)
                    if f == 0 and g >= 2:
                        act.wait_ge(la["y"], g - 1)
                    act.activation(hid(g)[:, f, :], ps[:, 2 + n % 2, :], ACT.Relu,
                                   bias=b1[:, f:f + 1]).then_inc(la["ue"], 1)
                act.wait_ge(la["y"], g + 1)
                if g >= 2:
                    act.wait_ge(la["yt"], g - 1)
                act.activation(UT[:, g % 2, :], ps[:, 4 + g % 2, :], ACT.Identity,
                               bias=b2[:, 0:1]).then_inc(la["ye"], 1)
            ffn_act(ffn[1])

        @block.tensor
        def _(pe):
            def transposes(bank, srcs, idn, done):
                for k, src in enumerate(srcs):
                    last = pe.transpose(ps[:, bank, k * P:(k + 1) * P], src, idn)
                last.then_inc(done, 1)

            def feature_transposes(t):
                pe.wait_ge(la["ex"], 4 * (t + 1))
                if t >= 2:
                    pe.wait_ge(la["fte"], t - 1)
                if t < 2:
                    pe.wait_ge(la["sq"], 2 * NG)
                for k in range(4):
                    last = pe.transpose(ps[:, 6 + t % 2, k * P:(k + 1) * P], EQK[:, k // 2, t, k % 2, :], ident[:, :])
                last.then_inc(la["ft"], 1)

            pe.wait_ge(s_cst, 1)
            for g in range(NG):
                pe.wait_ge(s_xn, g + 1)
                if g >= 2:
                    pe.wait_ge(s_xte, g - 1)
                transposes(g % 2, [XN[:, g * GT + k, :] for k in range(GT)], ident[:, :], s_xt)
                if g % 2 == 0:
                    continue
                b = g // 2
                if b == 0:
                    pe.wait_ge(s_w, 64)
                pe.wait_ge(s_xte, g + 1)
                for qk in range(2):
                    for n in range(2):
                        if b:
                            pe.wait_ge(s_qke, 2 * qk + n + 1)
                        pe.matmul(ps[:, 2 + 2 * qk + n, :], wT[:, qk, :], XT[:, b * S + n * W5:b * S + (n + 1) * W5],
                                  start=True, stop=True).then_inc(s_qk, 1)
                for g2 in (2 * b, 2 * b + 1):
                    if b:
                        pe.wait_ge(s_ve, g2 - 1)
                    for k in range(GT):
                        t = g2 * GT + k
                        last = pe.matmul(ps[:, 6 + g2 % 2, k * P:(k + 1) * P], XT[:, t * P:(t + 1) * P], wT[:, 2, :],
                                         start=True, stop=True)
                    last.then_inc(s_vp, 1)

            def score_group(w, n, slot):
                i, heads = A_GROUPS[n]
                kk = P * (i + 1)
                first = 2 * (n % 2)
                for j, h in enumerate(heads):
                    if len(heads) == 1:
                        pieces = [(first, 0, 0, min(kk, W5))] + ([(first + 1, 0, W5, kk)] if kk > W5 else [])
                    elif kk > 256:
                        pieces = [(first + j, 0, 0, kk)]
                    else:
                        pieces = [(first, j * kk, 0, kk)]
                    for bank, at, k0, k1 in pieces:
                        diag = k1 == kk
                        pe.matmul(ps[:, bank, at:at + k1 - k0], Qop[0:ZROWS, slot, h, i * P:(i + 1) * P],
                                  Kop[0:ZROWS, slot, h, k0:k1], start=True, stop=not diag)
                        if diag:
                            last = pe.matmul(ps[:, bank, at + k1 - k0 - P:at + k1 - k0], identb[:, :], maskA[:, :],
                                             start=False, stop=True)
                last.then_inc(s_a, 1)

            def score_chunk(u, c, slot):
                half, kt, heads, width = B_CHUNKS[c]
                q1 = S if half == 0 else W5
                pe.wait_ge(s_exp, u * BC + (c + 1))
                for j, h in enumerate(heads):
                    last = pe.matmul(ps[:, 4 + c % 2, j * width:(j + 1) * width],
                                     Kop[0:MROW + PARTS, slot, h, kt * P:(kt + 1) * P],
                                     Qop[0:MROW + PARTS, slot, h, q1 - width:q1], start=True, stop=True)
                last.then_inc(s_b, 1)

            def outputs(u, half, kt0, slot):
                last_kt = 7 if half == 0 else 3
                pe.wait_ge(s_exp, u * BC + (2 + last_chunk(half, kt0 + 1) + 1))
                masked = [j for j, (hf, kt) in enumerate(MASKS) if hf == half and kt <= kt0 + 1]
                if masked:
                    pe.wait_ge(s_mask, u * 8 + (max(masked) + 1))
                if kt0 == 0:
                    pe.wait_ge(s_pve, 2 * u + (half + 1))
                    if half == 0:
                        pe.wait_ge(s_vs, u + 2)
                for kt in (kt0, kt0 + 1):
                    q0 = 0 if (half == 0 and kt < 4) or (half == 1 and kt == 1) else P * (kt % 4)
                    for h in (0, 1):
                        col = 32 * (2 * h + kt % 2)
                        last = pe.matmul(ps[col:col + 32, 6, q0:W5], Vs[:, slot, kt, :],
                                         E[:, half * 8 + kt, h, q0:W5], start=kt < 2, stop=kt >= last_kt - 1)
                if kt0 + 1 == last_kt:
                    last.then_inc(s_pv, 1)

            def transpose_maxima(n, slot, half):
                pe.wait_ge(s_split, n + 1)
                pe.wait_ge(s_mte, n)
                pe.transpose(ps[0:24, 7, 0:P // 2].bitcast(bf16),
                             M3[:, slot, half, :, :, :].rearrange("p a b c -> p (a b c)"),
                             identb[:, :]).then_inc(s_mt, 1)

            pe.wait_ge(s_ld[0], 32)
            pe.wait_ge(s_oz, CLEARED)
            pe.wait_ge(s_qke, 4 * B)
            for n in range(AG):
                if n >= 2:
                    pe.wait_ge(s_max, n - 1)
                score_group(0, n, 0)
            transpose_maxima(0, 0, 0)

            def head_products(w):
                pe.wait_ge(s_pve, 2 * w + 3)
                pe.wait_ge(s_mte, min(2 * w + 3, 2 * NU) if isinstance(w, int) else 2 * w + 3)
                for t in range(TB):
                    half, q = (1, t) if t < 4 else (0, t - 4)
                    last = pe.matmul(ps[:, 7, HEADS_AT + t * 2 * (VD + 1):HEADS_AT + (t + 1) * 2 * (VD + 1)],
                                     OT[:, half, q * P:(q + 1) * P], pick[:, :], start=True, stop=True)
                last.then_inc(s_hp, 1)

            pe.sem_inc(s_b, 1)

            def unit(u, t, s, ahead=True, first=False):
                nxt = (s + 1) % SLOTS
                loads = t + 1 if s < 2 else t + 2
                given = 0
                pe.wait_ge(s_m[s][0], 32 * (t + 1))
                for c in range(BC):
                    if c == 14:
                        pe.wait_ge(s_m[s][1], 32 * (t + 1))
                    score_chunk(u, c, s)
                    if c == HEADS_C and not first:
                        head_products(u - 1)
                    if ahead and given < AG and c * AG >= given * PACE:
                        if given == 0:
                            pe.wait_ge(s_ld[nxt], 32 * loads)
                        pe.wait_ge(s_max, u * AG + (AG + given - 1))
                        score_group(u, given, nxt)
                        given += 1
                    if c == MT1_AT:
                        if not first:
                            pe.wait_ge(s_ht, u)
                        transpose_maxima(2 * u + 1, s, 1)
                    if c == MT_AT and ahead:
                        transpose_maxima(2 * u + 2, nxt, 0)
                    for at, half, kt0 in ((5, 0, 0), (9, 0, 2), (14, 0, 4), (16, 0, 6), (O1_AT, 1, 0)):
                        if c == at:
                            outputs(u, half, kt0, s)
                if ahead:
                    while given < AG:
                        if given == AG - LEFT and O1_AT > 19:
                            outputs(u, 1, 0, s)
                        pe.wait_ge(s_max, u * AG + (AG + given - 1))
                        score_group(u, given, nxt)
                        given += 1
                elif O1_AT > 19:
                    outputs(u, 1, 0, s)
                outputs(u, 1, 2, s)

            pe.wait_ge(s_lamr, 1)
            for s in range(SLOTS):
                unit(s, 0, s, first=s == 0)
            with pe.Fori(1, 5) as t:
                for s in range(SLOTS):
                    unit(t * SLOTS + s, t, s)
            unit(NU - 1, 5, 0, ahead=False)

            def head_transposes(g):
                pe.wait_ge(s_hn, 8 * (g // 2) + 8)
                if g >= 2:
                    pe.wait_ge(s_oT2e, g - 1)
                b = g // 2
                transposes(g % 2, [DD[:, (g % 2) * GT + k, b * P:(b + 1) * P] for k in range(GT)], ident[:, :], s_oT2)

            pe.wait_ge(s_exp, 2 + NU * BC)
            head_products(NU - 1)
            head_transposes(0)
            for g in range(NG):
                if g + 1 < NG:
                    head_transposes(g + 1)
                pe.wait_ge(s_oT2e, g + 1)
                for k in range(GT):
                    t = g * GT + k
                    last = pe.matmul(ps[:, 2 + g, k * P:(k + 1) * P], OTT[:, t * P:(t + 1) * P], wT[:, 3, :],
                                     start=True, stop=True)
                last.then_inc(s_wo, 1)

            def ffn_pe(f, before):
                def head_x(g):
                    pe.wait_ge(f["xn"], g + 1)
                    if g:
                        pe.wait_ge(f["xte"], g)
                    transposes(0, [FXN[:, g * GT + k, :] for k in range(GT)], ident[:, :], f["xt"])

                def head_router(g):
                    pe.wait_ge(f["xte"], g + 1)
                    if g:
                        pe.wait_ge(f["sub"], g)
                    for k in range(GT):
                        t = g * GT + k
                        last = pe.matmul(ps[:, 2, k * OHR:(k + 1) * OHR], FXT[:, t * P:(t + 1) * P], rw[:, :],
                                         start=True, stop=True)
                    last.then_inc(f["lg"], 1)

                def head_onehot(g):
                    pe.wait_ge(f["oh"], g + 1)
                    if g:
                        pe.wait_ge(f["ohte"], g)
                    bank = ps[0:OHR, 1, 0:W5 // 2].bitcast(bf16)
                    for k in range(GT):
                        last = pe.transpose(bank[:, k * P:(k + 1) * P],
                                            OH[:, g % 2, k, :, :].rearrange("p a b -> p (a b)"), identb[:, :])
                    last.then_inc(f["oht"], 1)

                def spread(g, e):
                    n = g * NE + e
                    if n >= 2:
                        pe.wait_ge(f["xm"], n - 1)
                    pe.matmul(ps[:, 3 + n % 2, :], sel[:, e, :], OHT[:, g % 2, :], start=True, stop=True
                              ).then_inc(f["g"], 1)

                def expert(g, e):
                    pe.wait_ge(f["xm"], g * NE + e + 1)
                    mm = pe.matmul(ps[:, 5 + g % 2, :], ew[:, e, :], XM[:, e % 4, :], start=False, stop=e == NE - 1)
                    mm.then_inc(f["y"] if e == NE - 1 else f["e"], 1)

                def back(g):
                    pe.wait_ge(f["ye"], g + 1)
                    if g:
                        pe.wait_ge(f["x"], g)
                    transposes(7, [YT[:, g % 2, k * P:(k + 1) * P] for k in range(GT)], ident[:, :], f["yt"])

                head_x(0)
                head_router(0)
                head_onehot(0)
                pe.wait_ge(*before)
                for g in range(NG):
                    pe.wait_ge(f["ohte"], g + 1)
                    if g >= 2:
                        pe.wait_ge(f["ye"], g - 1)
                    pe.matmul(ps[:, 5 + g % 2, :], eb[:, :], OHT[:, g % 2, :], start=True, stop=False)
                    spread(g, 0)
                    spread(g, 1)
                    for e in range(NE):
                        if e == 0 and g + 1 < NG:
                            head_x(g + 1)
                        if e == 1 and g:
                            back(g - 1)
                        if e == 2 and g + 1 < NG:
                            head_router(g + 1)
                        if e == ONEHOT_E and g + 1 < NG:
                            head_onehot(g + 1)
                        expert(g, e)
                        if e + 2 < NE:
                            spread(g, e + 2)
                back(NG - 1)

            pe.wait_ge(s_w2, 16 * 12)
            pe.wait_ge(s_rw, 16)
            pe.wait_ge(s_ebd, 48)
            pe.wait_ge(s_cst, 3)
            ffn_pe(ffn[0], (s_x1, NG))

            pe.wait_ge(ffn[0]["sub"], NG)
            for g in range(NG):
                pe.wait_ge(la["xn"], g + 1)
                if g >= 2:
                    pe.wait_ge(la["xte"], g - 1)
                transposes(g % 2, [BX[:, g * GT + k, :] for k in range(GT)], ident[:, :], la["xt"])
                pe.wait_ge(la["xte"], g + 1)
                for qk in range(2):
                    if g:
                        pe.wait_ge(la["qke"], 2 * (g - 1) + qk + 1)
                    pe.matmul(ps[:, 2 + qk, :], bw[:, qk, :], BXT[:, g * W5:(g + 1) * W5], start=True, stop=True
                              ).then_inc(la["qk"], 1)
                if g:
                    pe.wait_ge(la["ve"], g)
                for k in range(GT):
                    t = g * GT + k
                    last = pe.matmul(ps[:, 4, k * P:(k + 1) * P], BXT[:, t * P:(t + 1) * P], bw[:, 2, :],
                                     start=True, stop=True)
                last.then_inc(la["v"], 1)
            pe.wait_ge(la["qke"], 2 * NG)
            pe.wait_ge(la["ve"], NG)
            for g in range(NG):
                for qk in range(2):
                    n = 2 * g + qk
                    if n >= 2:
                        pe.wait_ge(la["sq"], n - 1)
                    transposes(6 + n % 2, [QKT[:, qk, (g * GT + k) * P:(g * GT + k + 1) * P] for k in range(GT)],
                               ident[:, :], la["nt"])
            pe.wait_ge(s_om, 32)
            for t in range(NT):
                for qk in range(2):
                    n = 2 * t + qk
                    if n >= 6:
                        pe.wait_ge(la["ex"], 2 * (n - 5))
                    pe.matmul(ps[:, n % 6, 0:LH * LM], QKT[:, qk, t * P:(t + 1) * P],
                              om[:, :, :].rearrange("p a b -> p (a b)"), start=True, stop=True).then_inc(la["pr"], 1)
                if t >= 2:
                    feature_transposes(t - 2)
            for t in (NT - 2, NT - 1):
                feature_transposes(t)
            pe.wait_ge(la["ex"], 4 * NT)
            pe.wait_ge(la["fte"], NT)
            pe.wait_ge(la["kp"], NT)

            def at_products(c):
                if c >= 2:
                    pe.wait_ge(la["ate"], c - 1)
                for j in range(LU):
                    t, h = (j // LH) * TB + c, j % LH
                    last = pe.matmul(ps[:, c % 2, j * P:(j + 1) * P], QKPT[:, 1, t, h, :], QKPT[:, 0, t, h, :],
                                     start=True, stop=True)
                last.then_inc(la["at"], 1)

            at_products(0)
            for c in range(TB):
                if c + 1 < TB:
                    at_products(c + 1)
                if c < TB - 1:
                    if c >= 2:
                        pe.wait_ge(la["ste"], c - 1)
                    for j in range(LU):
                        t, h = (j // LH) * TB + c, j % LH
                        last = pe.matmul(ps[:, 2 + c % 2, j * VW:(j + 1) * VW], KP[:, t, h, :], VA[:, t, h, :],
                                         start=True, stop=True)
                    last.then_inc(la["st"], 1)
                pe.wait_ge(la["ate"], c + 1)
                if c:
                    pe.wait_ge(la["ste"], c)
                if c >= 2:
                    pe.wait_ge(la["oe"], c - 1)
                for j in range(LU):
                    t, h = (j // LH) * TB + c, j % LH
                    dst = ps[:, 4 + c % 2, j * VW:(j + 1) * VW]
                    last = pe.matmul(dst, AM[:, c % 2, j, :], VA[:, t, h, :], start=True, stop=c == 0)
                    if c:
                        last = pe.matmul(dst, QKPT[:, 0, t, h, :], ST[:, c - 1, j, :], start=False, stop=True)
                last.then_inc(la["o"], 1)
            pe.wait_ge(la["oe"], TB)
            for g in range(NG):
                if g >= 2:
                    pe.wait_ge(la["ote"], g - 1)
                transposes(g % 2, [AO[:, g * GT + k, :] for k in range(GT)], ident[:, :], la["ot"])
                pe.wait_ge(la["ote"], g + 1)
                for k in range(GT):
                    t = g * GT + k
                    last = pe.matmul(ps[:, 2 + g, k * P:(k + 1) * P], AOT[:, t * P:(t + 1) * P], bw[:, 3, :],
                                     start=True, stop=True)
                last.then_inc(la["wo"], 1)
            pe.wait_ge(la["res"], NG)
            for g in range(NG):
                pe.wait_ge(la["h"], g + 1)
                if g >= 2:
                    pe.wait_ge(la["hte"], g - 1)
                transposes(g % 2, [H2[:, g * GT + k, :] for k in range(GT)], ident[:, :], la["ht"])
                pe.wait_ge(la["hte"], g + 1)
                for f in range(FC):
                    n = g * FC + f
                    if n >= 2:
                        pe.wait_ge(la["ue"], n - 1)
                    pe.matmul(ps[:, 2 + n % 2, :], w1[:, f * P:(f + 1) * P], HT[:, g * W5:(g + 1) * W5],
                              start=True, stop=True).then_inc(la["u"], 1)
                if g >= 2:
                    pe.wait_ge(la["ye"], g - 1)
                for f in range(FC):
                    pe.wait_ge(la["ue"], g * FC + f + 1)
                    last = pe.matmul(ps[:, 4 + g % 2, :], w2[:, f, :], hid(g)[:, f, :], start=f == 0, stop=f == FC - 1)
                last.then_inc(la["y"], 1)
                pe.wait_ge(la["ye"], g + 1)
                if g:
                    pe.wait_ge(la["x"], g)
                transposes(7, [UT[:, g % 2, k * P:(k + 1) * P] for k in range(GT)], ident[:, :], la["yt"])
            ffn_pe(ffn[1], (la["x"], NG))

        @block.vector
        def _(dve):
            chain = [0]

            def fence(ins):
                chain[0] += 1
                ins.then_inc(s_dve, 1)
                dve.wait_ge(s_dve, chain[0])

            def stats(tiles, src, done):
                for t in tiles:
                    last = dve.bn_stats(st[:, t, :], src(t))
                fence(last)
                for t in tiles:
                    last = dve.bn_aggr(mv[:, t, :], st[:, t, :])
                last.then_inc(done, 1)

            def normalise(tiles, dst, src, done):
                for t in tiles:
                    last = dve.tensor_scalar(dst(t), src(t), mv[:, t, 0:1], rstd[:, t:t + 1], ALU.subtract, ALU.mult)
                last.then_inc(done, 1)

            for g in range(NG):
                tiles = range(g * GT, (g + 1) * GT)
                dve.wait_ge(s_x[g], 16)
                stats(tiles, lambda t: X[:, t, :], s_var)
                if g >= 1:
                    before = range((g - 1) * GT, g * GT)
                    dve.wait_ge(s_var, g)
                    dve.wait_ge(s_rstd, g)
                    normalise(before, lambda t: XN[:, t, :], lambda t: X[:, t, :], s_xn)
            dve.wait_ge(s_rstd, NG)
            normalise(tiles, lambda t: XN[:, t, :], lambda t: X[:, t, :], s_xn)
            dve.wait_ge(s_lam, 16)
            for k in range(2):
                last = dve.tensor_tensor(lamw[:, k, :], lamv[:, 2 * k, :], lamv[:, 2 * k + 1, :], ALU.mult)
            fence(last)
            dve.tensor_reduce(lams[:, 0:2], lamw[:, :, :], AX.X, ALU.add).then_inc(s_lsum, 1)

            def cut(b, qk, step):
                QS, part = QSb[b], QPb[b]
                dve.wait_ge(s_cut, 5 * (2 * b + 1 - qk) + step) if step else dve.wait_ge(s_qke, 4 * b + 2 * qk + 2)
                if step == 0:
                    last = dve.tensor_scalar(QS[:, qk, :], QS[:, qk, :], OPERAND_BOUND, -OPERAND_BOUND, ALU.min, ALU.max)
                elif step == 1:
                    last = dve.tensor_copy(part[:, qk, 0, :], QS[:, qk, :])
                elif step == 2:
                    last = dve.tensor_tensor(QR[:, qk, :], QS[:, qk, :], part[:, qk, 0, :], ALU.subtract)
                elif step == 3:
                    last = dve.tensor_copy(part[:, qk, 1, :], QR[:, qk, :])
                else:
                    last = dve.tensor_tensor(part[:, qk, 2, :], QR[:, qk, :], part[:, qk, 1, :], ALU.subtract)
                last.then_inc(s_cut, 1)

            for qk in (1, 0):
                for step in range(5):
                    cut(0, qk, step)
            dve.wait_ge(s_act, 1)
            fence(dve.tensor_tensor(lams[:, 0:1], lams[:, 3:4], lams[:, 2:3], ALU.subtract))
            fence(dve.tensor_scalar(lams[:, 1:2], lams[:, 0:1], 1.0, -LAMBDA_INIT, ALU.mult, ALU.add))
            dve.wait_ge(s_oz, CLEARED)
            dve.tensor_scalar(pick[:, VD + 1:2 * VD + 1], pick[:, VD + 1:2 * VD + 1], lams[:, 1:2], None, ALU.mult
                              ).then_inc(s_lamr, 1)

            def maximum(w, n, slot):
                i, heads = A_GROUPS[n]
                kk = P * (i + 1)
                first = 2 * (n % 2)
                dve.wait_ge(s_a, w * AG + (n + 1))
                out = NM[:, slot, 0 if i >= 4 else 1, heads[0]:heads[-1] + 1, i % 4]
                if len(heads) == 1:
                    src = ps[:, first:first + 2, :].rearrange("p b c -> p (b c)")[:, 0:kk]
                elif kk > 256:
                    src = ps[:, first:first + 2, 0:kk]
                else:
                    src = ps[:, first, 0:2 * kk].rearrange("p (h k) -> p h k", h=2)
                dve.tensor_reduce(out, src, AX.X, ALU.max, negate=True).then_inc(s_max, 1)

            def store_maxima(n, slot, half):
                dve.wait_ge(s_mt, n + 1)
                dve.tensor_copy(MT[:, slot, half, :], ps[0:24, 7, 0:P // 2].bitcast(bf16)).then_inc(s_mte, 1)

            for n in range(AG):
                maximum(0, n, 0)
            store_maxima(0, 0, 0)

            hv = ps[:, 7, HEADS_AT:HEADS_AT + TB * 2 * (VD + 1)].rearrange("p (t h e) -> p t h e", t=TB, h=2)

            def invert_sums(w):
                dve.wait_ge(s_hp, w + 1)
                dve.reciprocal(RL, hv[:, :, :, VD]).then_inc(s_hq, 1)

            def divide(w, first):
                dve.wait_ge(s_hq, w + 1)
                if not first:
                    dve.wait_ge(s_hstep, 4 * w - 3)
                dve.tensor_tensor(TT, hv[:, :, :, 0:VD],
                                  RL.rearrange("p t (h o) -> p t h o", o=1).broadcast_to([P, TB, 2, VD]),
                                  ALU.mult).then_inc(s_ht, 1)

            def sum_squares(w):
                dve.wait_ge(s_hstep, 4 * w + 2)
                dve.tensor_reduce(MS[:, 0, :], SQ, AX.X, ALU.add).then_inc(s_hs, 1)

            def unit(u, s, ahead=True, cuts=(), first=0):
                nxt = (s + 1) % SLOTS
                cuts = list(cuts)
                for n in range(AG):
                    if ahead:
                        maximum(u + 1, n, nxt)
                    if n == INVERT_AT and first != 1:
                        invert_sums(u - 1)
                    if n == INVERT_AT + 1 and first != 1:
                        divide(u - 1, first == 2)
                    if n == INVERT_AT + 3 and first != 1:
                        sum_squares(u - 1)
                    if n % 3 == 1 and cuts:
                        cut(1, *cuts.pop(0))
                    if n == ST1_AT:
                        store_maxima(2 * u + 1, s, 1)
                    if n == ST_AT and ahead:
                        store_maxima(2 * u + 2, nxt, 0)

            steps = [(qk, step) for qk in (1, 0) for step in range(5)]
            for u in range(SLOTS):
                unit(u, u, cuts=steps[4 * u:4 * u + 4], first=u + 1)
            with dve.Fori(1, 5) as t:
                for s in range(SLOTS):
                    unit(t * SLOTS + s, s)
            unit(NU - 1, (NU - 1) % SLOTS, ahead=False)

            invert_sums(NU - 1)
            divide(NU - 1, False)
            sum_squares(NU - 1)
            for g in range(NG):
                dve.wait_ge(s_wo, g + 1)
                xg = X[:, g * GT:(g + 1) * GT, :].rearrange("p a b -> p (a b)")
                dve.tensor_tensor(xg, ps[:, 2 + g, :], xg, ALU.add).then_inc(s_x1, 1)

            def ffn_dve(f, before, after):
                def head_steps(g):
                    tiles = range(g * GT, (g + 1) * GT)

                    def ln():
                        stats(tiles, lambda t: X[:, t, :], f["var"])

                    def b4(a):
                        return a.rearrange("p (t o) -> p t o", o=1).broadcast_to([P, GT, NE])

                    def logits():
                        dve.wait_ge(f["lg"], g + 1)
                        src = ps[:, 2, 0:GT * OHR].rearrange("p (t e) -> p t e", t=GT)[:, :, 0:NE]
                        fence(dve.tensor_tensor(LG[:, g, :, :], src,
                                                rb[:, :].rearrange("p (o e) -> p o e", o=1).broadcast_to([P, GT, NE]),
                                                ALU.add))
                        fence(dve.tensor_reduce(MX[:, 0, g, :], LG[:, g, :, :], AX.X, ALU.max))
                        dve.tensor_tensor(LG[:, g, :, :], LG[:, g, :, :], b4(MX[:, 0, g, :]), ALU.subtract
                                          ).then_inc(f["sub"], 1)

                    def choose():
                        dve.wait_ge(f["exp"], g + 1)
                        dve.tensor_reduce(MX[:, 1, g, :], LE[:, g, :, :], AX.X, ALU.add)
                        fence(dve.tensor_reduce(MX[:, 2, g, :], LE[:, g, :, :], AX.X, ALU.max))
                        dve.reciprocal(MX[:, 3, g, :], MX[:, 1, g, :])
                        fence(dve.tensor_tensor(LG[:, g, :, :], LE[:, g, :, :], b4(MX[:, 2, g, :]), ALU.is_ge))
                        dve.tensor_tensor(MX[:, 3, g, :], MX[:, 3, g, :], MX[:, 2, g, :], ALU.mult)
                        fence(dve.tensor_tensor(LG[:, g, :, :], LG[:, g, :, :],
                                                rev[:, :].rearrange("p (o e) -> p o e", o=1).broadcast_to([P, GT, NE]),
                                                ALU.mult))
                        fence(dve.tensor_reduce(MX[:, 4, g, :], LG[:, g, :, :], AX.X, ALU.max))
                        if g >= 2:
                            dve.wait_ge(f["oht"], g - 1)
                        for k in range(GT):
                            last = dve.tensor_tensor(
                                OH[:, g % 2, k, :, :],
                                LG[:, g, k, :].rearrange("p (o e) -> p o e", o=1).broadcast_to([P, COPIES, NE]),
                                MX[:, 4, g, k:k + 1].rearrange("p (o e) -> p o e", o=1).broadcast_to([P, COPIES, NE]),
                                ALU.is_equal)
                        last.then_inc(f["oh"], 1)

                    return {"ln": ln, LOGITS_E: logits, CHOOSE_E: choose}

                def combine(g):
                    dve.wait_ge(f["yt"], g + 1)
                    for k in range(GT):
                        t = g * GT + k
                        last = dve.scalar_tensor_tensor(out=X[:, t, :], in0=ps[:, 7, k * P:(k + 1) * P],
                                                        scalar=MX[:, 3, g, k:k + 1], in1=X[:, t, :],
                                                        op0=ALU.mult, op1=ALU.add)
                    last.then_inc(f["x"], 1)

                for g in range(NG):
                    dve.wait_ge(before, g + 1)
                    head_steps(g)["ln"]()
                first = head_steps(0)
                first[LOGITS_E]()
                first[CHOOSE_E]()
                for g in range(NG):
                    steps = head_steps(g + 1) if g + 1 < NG else {}
                    for e in range(NE):
                        n = g * NE + e
                        dve.wait_ge(f["g"], n + 1)
                        if n >= 4:
                            back = n - 4
                            if back % NE == NE - 1:
                                dve.wait_ge(f["y"], back // NE + 1)
                            else:
                                dve.wait_ge(f["e"], back - back // NE + 1)
                        dve.tensor_tensor(XM[:, e % 4, :], ps[:, 3 + n % 2, :], FXT[:, g * W5:(g + 1) * W5], ALU.mult
                                          ).then_inc(f["xm"], 1)
                        if e in steps:
                            steps[e]()
                        if e == COMBINE_E and g:
                            combine(g - 1)
                            after(g - 1)
                combine(NG - 1)
                after(NG - 1)

            dve.wait_ge(s_w2, 16 * 12)
            dve.wait_ge(s_cst, 3)
            def stats_la(g):
                dve.wait_ge(ffn[0]["x"], g + 1)
                stats(range(g * GT, (g + 1) * GT), lambda t: X[:, t, :], la["var"])

            ffn_dve(ffn[0], s_x1, stats_la)

            for g in range(NG):
                for qk in range(2):
                    n = 2 * g + qk
                    dve.wait_ge(la["sq"], n + 1)
                    fence(dve.tensor_reduce(NN[:, qk, g * GT:(g + 1) * GT, :],
                                            QKSQ[:, n % 2, :].rearrange("p (t h d) -> p t h d", t=GT, h=LH),
                                            AX.X, ALU.add))
                    nn = NN[:, qk, g * GT:(g + 1) * GT, :].rearrange("p a b -> p (a b)")
                    dve.tensor_scalar(nn, nn, 0.5, None, ALU.mult).then_inc(la["nn"], 1)
            dve.wait_ge(la["nn"], 2 * NG)
            for t in range(NT):
                for qk in range(2):
                    n = 2 * t + qk
                    dve.wait_ge(la["pr"], n + 1)
                    fence(dve.tensor_reduce(RM[:, qk, t, :], ps[:, n % 6, 0:LH * LM].rearrange("p (h m) -> p h m", h=LH),
                                            AX.X, ALU.max))
                    fence(dve.tensor_tensor(RM[:, qk, t, :], RM[:, qk, t, :], NN[:, qk, t, :], ALU.subtract))
                    dve.scalar_tensor_tensor(out=RM[:, qk, t, :], in0=RM[:, qk, t, :], scalar=-1.0,
                                             in1=NN[:, qk, t, :], op0=ALU.mult, op1=ALU.subtract).then_inc(la["rm"], 1)
            mt4 = maskT[:, :].rearrange("p (o q) -> p o q", o=1).broadcast_to([P, LU, P])
            ao = AO[:, :, :].rearrange("p (b t) (h d) -> p b h t d", b=B, h=LH)

            def causal(c):
                dve.wait_ge(la["at"], c + 1)
                if c >= 2:
                    dve.wait_ge(la["o"], c - 1)
                dve.tensor_tensor(AM[:, c % 2, :, :], ps[:, c % 2, :].rearrange("p (j q) -> p j q", j=LU), mt4,
                                  ALU.mult).then_inc(la["ate"], 1)

            causal(0)
            for c in range(TB):
                if c < TB - 1:
                    dve.wait_ge(la["st"], c + 1)
                    src = ps[:, 2 + c % 2, 0:LU * VW].rearrange("p (j v) -> p j v", j=LU)
                    if c == 0:
                        dve.tensor_copy(ST[:, 0, :, :], src).then_inc(la["ste"], 1)
                    else:
                        dve.wait_ge(la["ste"], c)
                        dve.tensor_tensor(ST[:, c, :, :], src, ST[:, c - 1, :, :], ALU.add).then_inc(la["ste"], 1)
                if c + 1 < TB:
                    causal(c + 1)
                dve.wait_ge(la["o"], c + 1)
                res = ps[:, 4 + c % 2, 0:LU * VW].rearrange("p (j v) -> p j v", j=LU)
                fence(dve.tensor_scalar(DN[:, c % 2, :], res[:, :, LD], FEAT_EPS, None, ALU.add))
                fence(dve.reciprocal(DN[:, c % 2, :], DN[:, c % 2, :]))
                for b in range(B):
                    last = dve.tensor_tensor(
                        ao[:, b, :, c, :], res[:, b * LH:(b + 1) * LH, 0:LD],
                        DN[:, c % 2, b * LH:(b + 1) * LH].rearrange("p (j o) -> p j o", o=1).broadcast_to([P, LH, LD]),
                        ALU.mult)
                last.then_inc(la["oe"], 1)
            for g in range(NG):
                dve.wait_ge(la["wo"], g + 1)
                bg = BX[:, g * GT:(g + 1) * GT, :].rearrange("p a b -> p (a b)")
                dve.tensor_tensor(bg, ps[:, 2 + g, :], bg, ALU.add).then_inc(la["res"], 1)
                dve.wait_ge(la["res"], g + 1)
                stats(range(g * GT, (g + 1) * GT), lambda t: BX[:, t, :], la["var2"])
            g4 = gam[:, :].rearrange("p (o d) -> p o d", o=1).broadcast_to([P, GT, D])
            b4 = bet[:, :].rearrange("p (o d) -> p o d", o=1).broadcast_to([P, GT, D])
            for g in range(NG):
                dve.wait_ge(la["var2"], g + 1)
                dve.wait_ge(la["rstd2"], g + 1)
                normalise(range(g * GT, (g + 1) * GT), lambda t: H2[:, t, :], lambda t: BX[:, t, :], la["h1"])
                dve.wait_ge(la["h1"], g + 1)
                hg = H2[:, g * GT:(g + 1) * GT, :]
                fence(dve.tensor_tensor(hg, hg, g4, ALU.mult))
                dve.tensor_tensor(hg, hg, b4, ALU.add).then_inc(la["h"], 1)
            for g in range(NG):
                dve.wait_ge(la["yt"], g + 1)
                xg = X[:, g * GT:(g + 1) * GT, :].rearrange("p a b -> p (a b)")
                dve.tensor_tensor(xg, ps[:, 7, :], xg, ALU.add).then_inc(la["x"], 1)
            ffn_dve(ffn[1], la["x"], lambda g: None)


c_feat = 1.0 / math.sqrt(LM)


def kernel(**inputs):
    import numpy as _np
    import concourse.bacc as _bacc
    from concourse import mybir as _mybir
    from concourse.bass_utils import run_bass_kernel_spmd as _run

    a, b, f = "L0_attn_a_", "L0_attn_b_", "L0_ffn_"
    g = {k: _np.asarray(v) for k, v in inputs.items()}
    arrays = [
        ("x", g[a + "x"].reshape(TOK, D)),
        ("a_wqT", g[a + "Wq"].T), ("a_wkT", g[a + "Wk"].T), ("a_wvT", g[a + "Wv"].T), ("a_woT", g[a + "Wo"].T),
        ("a_lam", _np.stack([g[a + "lq1"], g[a + "lk1"], g[a + "lq2"], g[a + "lk2"]])),
        ("b_wq", g[b + "Wq"]), ("b_wk", g[b + "Wk"]), ("b_wv", g[b + "Wv"]), ("b_wo", g[b + "Wo"]),
        ("b_omegaT", g[b + "omega"].T),
        ("b_w1", g[b + "W1"]), ("b_b1", g[b + "b1"].reshape(FC, P).T), ("b_w2", g[b + "W2"]),
        ("b_b2", g[b + "b2"].reshape(D, 1)), ("b_gamma", g[b + "gamma"].reshape(1, D)),
        ("b_beta", g[b + "beta"].reshape(1, D)),
        ("f_rw", g[f + "router_w"]), ("f_rb", g[f + "router_b"].reshape(1, NE)),
        ("f_ew", g[f + "expert_w"].transpose(1, 0, 2)), ("f_eb", g[f + "expert_b"]),
    ]
    nc = _bacc.Bacc("TRN2", target_bir_lowering=False, num_devices=1)
    feed, args = {}, []
    for name, arr in arrays:
        arr = _np.ascontiguousarray(arr)
        feed[name] = arr
        args.append(nc.dram_tensor(name, arr.shape, _mybir.dt.from_np(arr.dtype), kind="ExternalInput").ap())
    args.append(nc.dram_tensor("out", (TOK, D), _mybir.dt.float32, kind="ExternalOutput").ap())
    hybrid_kernel(nc, *args)
    r = _run(nc, [feed], core_ids=[0])
    return r.results[0]["out"].reshape(B, S, D)
```

```python
import math
from contextlib import ExitStack

import concourse.bass as bass
from concourse import mybir

PACE = 17
MT_AT, ST_AT = 16, 9
MT1_AT, ST1_AT = 6, 4
STO_AT = 17
HEADS_C = (1, 3)
INVERT_AT = 1
LAST = (1, 2, 5, 6, 12, 16)
ONEHOT_E = 6
LOGITS_E = 3
CHOOSE_E = 4
COMBINE_E = 2
CLEARED = 6

P = 128
B, S, D = 2, 1024, 128
TOK = B * S
NT = TOK // P
TB = S // P
GT = 4
NG = NT // GT
W5 = GT * P
HEADS = 8
HD = D // HEADS // 2
VD = 2 * HD
NU = B * HEADS
SLOTS = 3
TERMS = 6
KROWS = TERMS * HD
ZROWS = 96
MROW = 96
PARTS = 3
LAMBDA_INIT = 0.8 - 0.6 * math.exp(-0.3 * 6)
ATT_EPS = 1e-5
HEAD_GAIN = 1.0 - LAMBDA_INIT
HEADS_AT = 64
HEAD_BANKS = (0, 1, 6, 1)
LN_EPS = 1e-5
SCORE_SCALE = HD ** -0.5
OPERAND_BOUND = 4.0e18
MASKED = -3.0e38
AG = 12
BC = 20
NE = 8
COPIES = 12
OHR = COPIES * NE
LH, LD, LM = 2, 64, 128
LU = B * LH
FEAT_EPS = 1e-6
LN2_EPS = 1e6
VW = 96
FF = 512
FC = FF // P

fp32 = mybir.dt.float32
bf16 = mybir.dt.bfloat16
ALU = mybir.AluOpType
ACT = mybir.ActivationFunctionType
AX = mybir.AxisListType

A_GROUPS = [(i, (h,)) for i in (7, 6, 5, 4) for h in (0, 1)] + [(i, (0, 1)) for i in (3, 2, 1, 0)]
B_CHUNKS = []
for half in (0, 1):
    for kt in range(8 if half == 0 else 4):
        width = min(512, 128 * ((8 if half == 0 else 4) - kt))
        for heads in (((0,), (1,)) if width > 256 else ((0, 1),)):
            B_CHUNKS.append((half, kt, heads, width))
assert len(A_GROUPS) == AG and len(B_CHUNKS) == BC
MASKS = [(half, kt) for half in (0, 1) for kt in ((4, 5, 6, 7) if half == 0 else (0, 1, 2, 3))]


def last_chunk(half, kt):
    return max(c for c, (hf, k, _, _) in enumerate(B_CHUNKS) if (hf, k) == (half, kt))


def hybrid_kernel(nc, x_d, wqT_d, wkT_d, wvT_d, woT_d, lam_d, bwq_d, bwk_d, bwv_d, bwo_d, omT_d,
                  w1_d, b1_d, w2_d, b2_d, gam_d, bet_d, rw_d, rb_d, ew_d, eb_d, out_d):
    ctx = ExitStack()
    with ctx:
        def sb(name, shape, dt=fp32):
            return ctx.enter_context(nc.sbuf_tensor(name, shape, dt))

        def sem(name):
            return ctx.enter_context(nc.semaphore(name))

        X = sb("X", [P, NT, D])
        arena = sb("arena", [P, NU * 2 * W5])
        E = sb("E", [P, 12, 2, W5])
        Qop = sb("Qop", [P, SLOTS, 2, S], bf16)
        Kop = sb("Kop", [P, SLOTS, 2, S], bf16)
        Vu = sb("Vu", [P, NU, TB, 32])
        Vs = sb("Vs", [P, SLOTS, TB, 32])
        NM = sb("NM", [P, SLOTS, 2, 2, 4])
        MR = sb("MR", [P, SLOTS, 2, 2, 4])
        M3 = sb("M3", [P, SLOTS, 2, 2, PARTS, 4], bf16)
        MT = sb("MT", [24, SLOTS, 2, P], bf16)
        ident = sb("ident", [P, P])
        identb = sb("identb", [P, P], bf16)
        maskA = sb("maskA", [P, P], bf16)
        maskT = sb("maskT", [P, P])
        half_c = sb("half_c", [P, NT])
        wT = sb("wT", [P, 4, D])
        lamv = sb("lamv", [P, 4, HD])
        lamw = sb("lamw", [P, 2, HD])
        lams = sb("lams", [P, 4])
        warm = sb("warm", [P, 1])
        st = sb("st", [P, NT, 6])
        mv = sb("mv", [P, NT, 2])
        rstd = sb("rstd", [P, NT])
        ve = sb("ve", [P, NT])
        rw = sb("rw", [P, OHR])
        rb = sb("rb", [P, NE])
        ew = sb("ew", [P, NE, D])
        ebf = sb("ebf", [NE, D])
        ebr = sb("ebr", [NE, D])
        ebp = sb("ebp", [NE, PARTS, D], bf16)
        eb = sb("eb", [OHR, D], bf16)
        sel = sb("sel", [OHR, NE, P], bf16)
        rev = sb("rev", [P, NE])
        bw = sb("bw", [P, 4, D])
        om = sb("om", [P, LH, LM])
        w1 = sb("w1", [P, FF])
        b1 = sb("b1", [P, FC])
        w2 = sb("w2", [P, FC, D])
        b2 = sb("b2", [P, 1])
        hsum = sb("hsum", [P, LH])
        pick = sb("pick", [P, 2 * (VD + 1)])
        gam = sb("gam", [P, D])
        bet = sb("bet", [P, D])
        ps = ctx.enter_context(nc.psum_tensor("ps", [P, 8, W5], fp32))

        def view(big, at, shape):
            n = 1
            for k in shape:
                n *= k
            flat = big[:, at:at + n]
            if len(shape) == 1:
                return flat
            names = "abcd"[:len(shape)]
            return flat.rearrange("p (" + " ".join(names) + ") -> p " + " ".join(names),
                                  **{c: k for c, k in zip(names[1:], shape[1:])})

        Ef = E[:, :, :, :].rearrange("p a b c -> p (a b c)")
        XN = view(arena, 0, [NT, D])
        XT = view(arena, 2048, [TOK])
        QSb = [view(arena, 4096, [2, S]), view(arena, 14336, [2, S])]
        QR = view(arena, 6144, [2, S])
        QP = view(arena, 8192, [3072]).bitcast(bf16).rearrange("p (q t s) -> p q t s", q=2, t=3)
        QP2 = view(arena, 11264, [3072]).bitcast(bf16).rearrange("p (q t s) -> p q t s", q=2, t=3)
        QPb = [QP, QP2]
        OT = view(arena, 9216, [2, W5])
        TT = view(arena, 10240, [TB, 2, VD])
        OD = view(arena, 10496, [TB, VD])
        SQ = view(arena, 10624, [TB, VD])
        RL = view(arena, 10752, [TB, 2])
        MS = view(arena, 10768, [2, TB])
        MV = view(arena, 10784, [TB])
        DD = view(arena, 0, [TB, NU * VD])
        OTT = view(arena, 14336, [TOK])
        FXN = view(arena, 2048, [NT, D])
        FXT = view(arena, 4096, [TOK])
        XM = view(arena, 6144, [4, W5])
        YT = view(arena, 8192, [2, W5])
        LG = sb("LG", [P, NG, GT, NE])
        LE = sb("LE", [P, NG, GT, NE])
        MX = sb("MX", [P, 5, NG, GT])
        OH = sb("OH", [P, 2, GT, COPIES, NE], bf16)
        OHT = sb("OHT", [OHR, 2, W5], bf16)
        BX = view(arena, 0, [NT, D])
        BXT = view(arena, 2048, [TOK])
        QKT = view(arena, 4096, [2, TOK])
        EQK = view(arena, 8192, [2, NT, LH, LM])
        KP = view(Ef, 0, [NT, LH, LM])
        QKPT = view(Ef, 4096, [2, NT, LH, P])
        VA = sb("VA", [P, NT, LH, VW])
        Vuf = Vu[:, :, :, :].rearrange("p u a b -> p (u a b)")
        ST = view(Vuf, 0, [TB - 1, LU, VW])
        AM = view(Vuf, 2688, [2, LU, P])
        AO = view(arena, 2048, [NT, D])
        QKSQ = view(Vuf, 0, [2, TOK])
        NN = sb("NN", [P, 2, NT, LH])
        RM = sb("RM", [P, 2, NT, LH])
        DN = sb("DN", [P, 2, LU])
        AOT = view(arena, 8192, [TOK])
        H2 = view(arena, 10240, [NT, D])
        HT = view(arena, 12288, [TOK])
        HID = view(arena, 4096, [FC, W5])
        UT = view(arena, 14336, [2, W5])

        def hid(g):
            return view(arena, 4096 + 2048 * (g % 2), [FC, W5])

        q_scr = nc.dram_tensor("q_scratch", [NU * 2 * KROWS, S], bf16, kind="Internal").ap()
        k_scr = nc.dram_tensor("k_scratch", [NU * 2 * KROWS, S], bf16, kind="Internal").ap()

        s_x = [sem(f"x_loaded_{g}") for g in range(NG)]
        s_w = sem("attention_weights_loaded")
        s_lam = sem("lambda_vectors_loaded")
        s_w2 = sem("other_weights_loaded")
        s_om = sem("omega_loaded")
        s_rw = sem("router_loaded")
        s_ebl = sem("expert_bias_loaded")
        s_ebd = sem("expert_bias_placed")
        s_rwz = sem("router_cleared")
        s_omz = sem("omega_cleared")
        s_cst = sem("constants_ready")
        s_cz = sem("constants_cleared")
        s_oz = sem("operands_cleared")
        s_dve = sem("vector_chain")
        s_pool = sem("pool_chain")
        s_pass = sem("pool_past_a_wait")
        s_act = sem("lambda_exponentials_ready")
        s_lsum = sem("lambda_sums_ready")
        s_var = sem("variances_ready")
        s_rstd = sem("rstd_ready")
        s_xn = sem("normalised")
        s_xt = sem("transposed_in_psum")
        s_xte = sem("transposed_in_sbuf")
        s_qk = sem("qk_projected")
        s_qke = sem("qk_scaled")
        s_qkc = sem("qk_bounded")
        s_vp = sem("v_projected")
        s_ve = sem("v_stored")
        s_cut = sem("steps_of_cutting_k_and_q")
        s_scr = [sem(f"scratch_written_{b}") for b in range(B)]
        s_ld = [sem(f"operands_loaded_{s}") for s in range(SLOTS)]
        s_m = [[sem(f"maxima_placed_{s}_{h}") for h in range(2)] for s in range(SLOTS)]
        s_a = sem("score_group_ready")
        s_max = sem("maximum_taken")
        s_sstep = sem("split_step")
        s_split = sem("maxima_split")
        s_mt = sem("maxima_transposed")
        s_mte = sem("maxima_in_sbuf")
        s_b = sem("score_chunk_ready")
        s_exp = sem("chunk_exponentiated")
        s_mask = sem("diagonal_masked")
        s_pv = sem("outputs_accumulated")
        s_pve = sem("outputs_stored")
        s_vs = sem("values_staged")
        s_lamr = sem("lambda_ready")

        block = ctx.enter_context(nc.Block())


        s_hp = sem("heads_as_tokens")
        s_hq = sem("head_sums_inverted")
        s_ht = sem("heads_divided")
        s_hs = sem("head_squares_summed")
        s_hstep = sem("head_step")
        s_hn = sem("heads_normalised")
        s_oT2 = sem("heads_transposed")
        s_oT2e = sem("heads_transposed_in_sbuf")
        s_wo = sem("attention_projected")
        s_x1 = sem("residual_updated")

        ffn = [dict((n, sem(f"ffn{k}_{n}")) for n in (
            "var", "rstd", "xn", "xt", "xte", "lg", "sub", "exp", "oh", "oht", "ohte",
            "g", "xm", "e", "y", "ye", "yt", "x")) for k in range(2)]
        la = dict((n, sem(f"la_{n}")) for n in (
            "var", "rstd", "xn", "xt", "xte", "qk", "qke", "v", "ve", "vz", "nt", "nn", "pr", "rm",
            "ex", "kp", "ft", "fte", "at", "ate", "st", "ste", "o", "oe", "ot", "ote", "wo", "res",
            "var2", "rstd2", "h1", "h", "ht", "hte", "u", "ue", "y", "ye", "yt", "x"))
        s_out = sem("out_written")

        @block.sync
        def _(sp):
            xv = x_d.rearrange("(t p) d -> p t d", p=P)
            for g in range(NG):
                sp.dma_start(X[:, g * GT:(g + 1) * GT, :], xv[:, g * GT:(g + 1) * GT, :]).then_inc(s_x[g], 16)
                if g == 1:
                    for i, w in enumerate((wqT_d, wkT_d, wvT_d, woT_d)):
                        sp.dma_start(wT[:, i, :], w).then_inc(s_w, 16)
            sp.dma_start(lamv[:, :, :], lam_d.rearrange("(o a) d -> o a d", o=1).broadcast_to([P, 4, HD])).then_inc(s_lam, 16)
            for k, w in enumerate((bwq_d, bwk_d, bwv_d, bwo_d)):
                sp.dma_start(bw[:, k, :], w).then_inc(s_w2, 16)
            sp.dma_start(w1[:, :], w1_d).then_inc(s_w2, 16)
            sp.dma_start(w2[:, :, :], w2_d.rearrange("(c p) d -> p c d", p=P)).then_inc(s_w2, 16)
            sp.dma_start(b1[:, :], b1_d).then_inc(s_w2, 16)
            sp.dma_start(b2[:, :], b2_d).then_inc(s_w2, 16)
            sp.dma_start(gam[:, :], gam_d.broadcast_to([P, D])).then_inc(s_w2, 16)
            sp.dma_start(bet[:, :], bet_d.broadcast_to([P, D])).then_inc(s_w2, 16)
            sp.dma_start(rb[:, :], rb_d.broadcast_to([P, NE])).then_inc(s_w2, 16)
            sp.dma_start(ew[:, :, :], ew_d).then_inc(s_w2, 16)
            sp.dma_start(ebf[:, :], eb_d).then_inc(s_ebl, 16)

            def write_operands(b):
                for scr, qk, terms in ((k_scr, 1, ((0, 1, 2), (3, 4), (5,))), (q_scr, 0, ((0, 3, 5), (1, 4), (2,)))):
                    rows = scr.rearrange("(b r t) s -> b r t s", b=B, t=TERMS)[b]
                    for part in range(PARTS):
                        sp.wait_ge(s_cut, 10 * b + 5 * (1 - qk) + (2, 4, 5)[part])
                        for t in terms[part]:
                            sp.dma_start(rows[:, t, :], QPb[b][:, qk, part, :]).then_inc(s_scr[b], 16)

            def load_operands(w, slot):
                for scr, op in ((q_scr, Qop), (k_scr, Kop)):
                    sp.dma_start(op[0:KROWS, slot, :, :],
                                 scr[bass.ds(w * (2 * KROWS), 2 * KROWS), :].rearrange("(h r) s -> r h s", h=2)
                                 ).then_inc(s_ld[slot], 16)

            def place_maxima(slot, half):
                q0 = (1 - half) * W5
                for h in range(2):
                    sp.dma_start(Qop[MROW:MROW + PARTS, slot, h, q0:q0 + W5].rearrange("r (t q) -> r t q", t=4),
                                 MT[12 * h:12 * h + 12, slot, half, :]).then_inc(s_m[slot][half], 16)

            write_operands(0)
            sp.wait_ge(s_scr[0], 16 * 2 * TERMS)
            sp.wait_ge(s_oz, CLEARED)
            load_operands(0, 0)
            load_operands(1, 1)
            sp.wait_ge(s_mte, 1)
            place_maxima(0, 0)

            def unit(u, s, load=True, ahead=True):
                sp.wait_ge(s_b, u * BC + 1)
                if load:
                    load_operands(u + 2, (s + 2) % SLOTS)
                sp.wait_ge(s_mte, 2 * u + 2)
                place_maxima(s, 1)
                if ahead:
                    sp.wait_ge(s_mte, 2 * u + 3)
                    place_maxima((s + 1) % SLOTS, 0)

            for u in range(SLOTS):
                unit(u, u)
            write_operands(1)
            sp.wait_ge(s_scr[1], 16 * 2 * TERMS)
            with sp.Fori(1, 4) as t:
                for s in range(SLOTS):
                    unit(t * SLOTS + s, s)
            for u in range(12, NU):
                unit(u, u % SLOTS, load=u + 2 < NU, ahead=u + 1 < NU)
            ov = out_d.rearrange("(t p) d -> p t d", p=P)
            for g in range(NG):
                sp.wait_ge(ffn[1]["x"], g + 1)
                sp.dma_start(ov[:, g * GT:(g + 1) * GT, :], X[:, g * GT:(g + 1) * GT, :]).then_inc(s_out, 16)
            sp.wait_ge(s_out, 16 * NG)

        @block.gpsimd
        def _(pool):
            chain = [0]

            def link(ins):
                chain[0] += 1
                ins.then_inc(s_pool, 1)
                pool.wait_ge(s_pool, chain[0])

            pool.memset(ident[:, :], 0.0).then_inc(s_cz, 1)
            pool.wait_ge(s_cz, 1)
            pool.affine_select(out=ident[:, :], in_=ident[:, :], compare_op=ALU.not_equal, fill=1.0, base=0,
                               pattern=[[-1, P]], channel_multiplier=1).then_inc(s_cst, 1)
            pool.memset(half_c[:, :], -0.5).then_inc(s_cst, 1)

            def rsqrt(out, var, tmp, eps, scale, done):
                link(pool.tensor_scalar(tmp, var, scale, eps, ALU.mult, ALU.add))
                pool.tensor_tensor(out, tmp, half_c[:, 0:1].broadcast_to(tmp.shape) if len(tmp.shape) > 1 else tmp,
                                   ALU.pow).then_inc(done, 1)

            pool.wait_ge(s_cst, 2)
            for g in range(NG):
                pool.wait_ge(s_var, g + 1)
                rsqrt(rstd[:, g * GT:(g + 1) * GT], mv[:, g * GT:(g + 1) * GT, 1], ve[:, g * GT:(g + 1) * GT],
                      LN_EPS, 1.0, s_rstd)
                if g == 1:
                    pool.memset(Qop[:, :, :, :].bitcast(fp32), 0.0).then_inc(s_oz, 1)
            link(pool.memset(Kop[:, :, :, :], 1.0))
            pool.memset(Kop[0:ZROWS, :, :, :].bitcast(fp32), 0.0).then_inc(s_oz, 1)
            link(pool.memset(maskT[:, :], 1.0))
            link(pool.affine_select(out=maskT[:, :], in_=maskT[:, :], compare_op=ALU.is_ge, fill=0.0, base=0,
                                    pattern=[[1, P]], channel_multiplier=-1))
            link(pool.memset(maskA[:, :], 0.0))
            pool.affine_select(out=maskA[:, :], in_=maskA[:, :], compare_op=ALU.is_ge, fill=MASKED, base=0,
                               pattern=[[-1, P]], channel_multiplier=1).then_inc(s_oz, 1)
            pool.tensor_copy(identb[:, :], ident[:, :]).then_inc(s_oz, 1)
            pool.memset(E[:, 8 + 1, :, 0:P], 0.0).then_inc(s_pv, 3)
            pool.memset(Vu[:, :, :, VD:32], 0.0).then_inc(s_vs, 1)
            pool.wait_ge(s_vs, 1)
            pool.memset(Vu[:, :, :, VD:VD + 1], 1.0).then_inc(s_oz, 1)
            link(pool.memset(pick[:, :], 0.0))
            for n in range(4):
                cols = pick[:, (n // 2) * (VD + 1):(n // 2 + 1) * (VD + 1)]
                last = pool.affine_select(out=cols, in_=cols, compare_op=ALU.not_equal, fill=1.0, base=-32 * n,
                                          pattern=[[-1, VD + 1]], channel_multiplier=1)
                last.then_inc(s_oz, 1) if n == 3 else link(last)

            def wait(sm, value):
                pool.wait_ge(sm, value)
                pool.sem_inc(s_pass, 1)

            def split(n, slot, half):
                src = NM[:, slot, half, :, :]
                part = [M3[:, slot, half, :, k, :] for k in range(PARTS)]
                rem = MR[:, slot, half, :, :]
                pool.tensor_copy(part[0], src).then_inc(s_sstep, 1)
                wait(s_sstep, n * 3 + 1)
                pool.tensor_tensor(rem, src, part[0], ALU.subtract).then_inc(s_sstep, 1)
                wait(s_sstep, n * 3 + 2)
                pool.tensor_copy(part[1], rem).then_inc(s_sstep, 1)
                wait(s_sstep, n * 3 + 3)
                pool.tensor_tensor(part[2], rem, part[1], ALU.subtract).then_inc(s_split, 1)

            def stage_values(u, slot):
                pool.tensor_copy(Vs[:, slot, :, :].rearrange("p a b -> p (a b)"),
                                 Vu[:, :, :, :].rearrange("p u a b -> p (u a b)")[:, bass.ds(u * (TB * 32), TB * 32)]
                                 ).then_inc(s_vs, 1)

            def mask(u, j):
                half, kt = MASKS[j]
                q0 = P * (kt % 4)
                wait(s_exp, u * BC + (2 + last_chunk(half, kt) + 1))
                diag = E[:, half * 8 + kt, :, q0:q0 + P]
                pool.affine_select(out=diag, in_=diag, compare_op=ALU.is_ge, fill=0.0, base=0,
                                   pattern=[[0, 2], [1, P]], channel_multiplier=-1).then_inc(s_mask, 1)

            def layer_rstd(names, g):
                r = slice(g * GT, (g + 1) * GT)
                pool.wait_ge(names["var"], g + 1)
                rsqrt(rstd[:, r], mv[:, r, 1], ve[:, r], LN_EPS, 1.0, names["rstd"])

            pool.memset(rw[:, :], 0.0).then_inc(s_rwz, 1)
            pool.wait_ge(s_rwz, 1)
            pool.dma_start(rw[:, 0:NE], rw_d).then_inc(s_rw, 16)
            pool.memset(om[:, :, :], 0.0).then_inc(s_omz, 1)
            pool.wait_ge(s_omz, 1)
            for h in range(LH):
                pool.dma_start(om[h * LD:(h + 1) * LD, h, :], omT_d).then_inc(s_om, 16)
            link(pool.memset(eb[:, :], 0.0))
            pool.wait_ge(s_ebl, 16)
            link(pool.tensor_copy(ebp[:, 0, :], ebf[:, :]))
            link(pool.tensor_tensor(ebr[:, :], ebf[:, :], ebp[:, 0, :], ALU.subtract))
            link(pool.tensor_copy(ebp[:, 1, :], ebr[:, :]))
            link(pool.tensor_tensor(ebp[:, 2, :], ebr[:, :], ebp[:, 1, :], ALU.subtract))
            for k in range(PARTS):
                pool.dma_start(eb[k * NE:(k + 1) * NE, :], ebp[:, k, :]).then_inc(s_ebd, 16)
            link(pool.memset(hsum[:, :], 0.0))
            for h in range(LH):
                link(pool.memset(hsum[h * LD:(h + 1) * LD, h:h + 1], 0.5))
            link(pool.memset(sel[:, :, :], 0.0))
            link(pool.affine_select(out=sel[:, :, :], in_=sel[:, :, :], compare_op=ALU.not_equal, fill=1.0, base=0,
                                    pattern=[[-1, NE], [0, P]], channel_multiplier=1))
            for e in range(NE):
                last = pool.memset(rev[:, e:e + 1], float(NE - e))
            last.then_inc(s_cst, 1)
            pool.wait_ge(s_ve, NG)
            pool.wait_ge(s_oz, CLEARED)
            stage_values(0, 0)
            wait(s_max, 8)
            split(0, 0, 0)
            wait(s_max, AG)
            split(1, 0, 1)

            def heads(w):
                wait(s_ht, w + 1)
                pool.tensor_tensor(OD, TT[:, :, 0, :], TT[:, :, 1, :], ALU.add).then_inc(s_hstep, 1)
                wait(s_hstep, 4 * w + 1)
                pool.tensor_tensor(SQ, OD, OD, ALU.mult).then_inc(s_hstep, 1)
                wait(s_hs, w + 1)
                pool.tensor_scalar(MV, MS[:, 0, :], HEAD_GAIN ** -2 / VD, HEAD_GAIN ** -2 * ATT_EPS, ALU.mult, ALU.add
                                   ).then_inc(s_hstep, 1)
                wait(s_hstep, 4 * w + 3)
                pool.tensor_tensor(MS[:, 1, :], MV, half_c[:, 0:TB], ALU.pow).then_inc(s_hstep, 1)
                wait(s_hstep, 4 * w + 4)
                dst = DD[:, :, bass.ds(w * VD, VD)]
                pool.tensor_tensor(dst, OD, MS[:, 1, :].rearrange("p (t o) -> p t o", o=1).broadcast_to([P, TB, VD]),
                                   ALU.mult).then_inc(s_hn, 1)

            def unit(u, s, ahead=True, first=False):
                if ahead:
                    wait(s_pv, 2 * u + 1)
                    stage_values(u + 1, (s + 1) % SLOTS)
                if not first:
                    heads(u - 1)
                mask(u, 0)
                mask(u, 1)
                if ahead:
                    wait(s_max, u * AG + AG + 8)
                    split(2 * u + 2, (s + 1) % SLOTS, 0)
                else:
                    layer_rstd(ffn[0], 0)
                    layer_rstd(ffn[0], 1)
                for j in range(2, 8):
                    mask(u, j)
                if ahead:
                    wait(s_max, u * AG + 2 * AG)
                    split(2 * u + 3, (s + 1) % SLOTS, 1)

            for s in range(SLOTS):
                unit(s, s, first=s == 0)
            with pool.Fori(1, 5) as t:
                for s in range(SLOTS):
                    unit(t * SLOTS + s, s)
            unit(NU - 1, (NU - 1) % SLOTS, ahead=False)
            heads(NU - 1)

            for g in range(2, NG):
                layer_rstd(ffn[0], g)
            link(pool.memset(VA[:, :, :, LD:VW], 0.0))
            pool.memset(VA[:, :, :, LD:LD + 1], 1.0).then_inc(la["vz"], 1)
            for g in range(NG):
                layer_rstd(la, g)
            c = 1.0 / math.sqrt(LM)
            for t in range(NT):
                pool.wait_ge(la["ex"], 8 * (t // 2 + 1))
                pool.tensor_scalar(KP[:, t, :, :].rearrange("p a b -> p (a b)"),
                                   EQK[:, 1, t, :, :].rearrange("p a b -> p (a b)"), c, FEAT_EPS,
                                   ALU.mult, ALU.add).then_inc(la["kp"], 1)
            for g in range(NG):
                r = slice(g * GT, (g + 1) * GT)
                pool.wait_ge(la["var2"], g + 1)
                rsqrt(rstd[:, r], mv[:, r, 1], ve[:, r], LN2_EPS, 1.0, la["rstd2"])
            for g in range(NG):
                layer_rstd(ffn[1], g)

        @block.scalar
        def _(act):
            for g in range(NG):
                act.wait_ge(s_xt, g + 1)
                act.copy(XT[:, g * W5:(g + 1) * W5], ps[:, g % 2, :]).then_inc(s_xte, 1)
                if g % 2 == 0:
                    continue
                b = g // 2
                for qk in (1, 0):
                    for n in range(2):
                        act.wait_ge(s_qk, 4 * b + 2 * (1 - qk) + n + 1)
                        act.activation(QSb[b][:, qk, n * W5:(n + 1) * W5], ps[:, 2 + 2 * qk + n, :], ACT.Copy,
                                       scale=(SCORE_SCALE, 1.0)[qk]).then_inc(s_qke, 1)
                for g2 in (2 * b, 2 * b + 1):
                    act.wait_ge(s_vp, g2 + 1)
                    src = ps[:, 6 + g2 % 2, :].rearrange("p (t h d) -> p h t d", t=GT, h=HEADS)
                    dst = Vu[:, b * HEADS:(b + 1) * HEADS, (g2 % 2) * GT:(g2 % 2 + 1) * GT, 0:VD]
                    for h in range(HEADS):
                        last = act.copy(dst[:, h, :, :], src[:, h, :, :])
                    last.then_inc(s_ve, 1)
            act.wait_ge(s_lsum, 1)
            act.activation(lams[:, 2:4], lams[:, 0:2], ACT.Exp).then_inc(s_act, 1)

            def exp_chunk(u, c):
                half, kt, heads, width = B_CHUNKS[c]
                act.wait_ge(s_b, u * BC + (1 + c + 1))
                if c in (0, 14):
                    act.wait_ge(s_pv, 2 * u + (half + 2))
                bank = 4 + c % 2
                dst = E[:, half * 8 + kt, heads[0]:heads[-1] + 1, W5 - width:W5]
                src = ps[:, bank, 0:len(heads) * width].rearrange("p (h q) -> p h q", h=len(heads))
                act.activation(dst, src, ACT.Exp).then_inc(s_exp, 1)

            def store_outputs(u, half, first):
                act.wait_ge(s_pv, 2 * u + (half + 4))
                if not first:
                    act.wait_ge(s_hp, u)
                act.copy(OT[:, half, :], ps[:, 6, :]).then_inc(s_pve, 1)

            act.wait_ge(s_oz, CLEARED)
            act.activation(warm[:, 0:1], half_c[:, 0:1], ACT.Exp).then_inc(s_exp, 2)

            def unit(u, first=False, after={}):
                for c in range(BC):
                    exp_chunk(u, c)
                    if c in after:
                        after[c]()
                    if c == STO_AT:
                        store_outputs(u, 0, first)
                store_outputs(u, 1, first)

            act.sem_inc(s_pve, 1)
            for s in range(SLOTS):
                unit(s, first=s == 0)
            with act.Fori(1, 5) as t:
                for s in range(SLOTS):
                    unit(t * SLOTS + s)

            def copy_heads(g):
                act.wait_ge(s_oT2, g + 1)
                act.copy(OTT[:, g * W5:(g + 1) * W5], ps[:, HEAD_BANKS[g], :]).then_inc(s_oT2e, 1)

            def ffn_act(f, bank0):
                def copy_x(g):
                    act.wait_ge(f["xt"], g + 1)
                    act.copy(FXT[:, g * W5:(g + 1) * W5], ps[:, 0 if g else bank0, :]).then_inc(f["xte"], 1)

                def gate_exp(g):
                    act.wait_ge(f["sub"], g + 1)
                    act.activation(LE[:, g, :, :], LG[:, g, :, :], ACT.Exp).then_inc(f["exp"], 1)

                def copy_onehot(g):
                    act.wait_ge(f["oht"], g + 1)
                    if g >= 2:
                        act.wait_ge(f["y"], g - 1)
                    act.copy(OHT[:, g % 2, :], ps[0:OHR, 1 if g else bank0, 0:W5 // 2].bitcast(bf16)
                             ).then_inc(f["ohte"], 1)

                def copy_y(g):
                    act.wait_ge(f["y"], g + 1)
                    if g >= 2:
                        act.wait_ge(f["yt"], g - 1)
                    act.copy(YT[:, g % 2, :], ps[:, 5 + g % 2, :]).then_inc(f["ye"], 1)

                def run():
                    for g in range(NG):
                        if g + 1 < NG:
                            copy_x(g + 1)
                        if g:
                            copy_y(g - 1)
                        if g + 1 < NG:
                            gate_exp(g + 1)
                            copy_onehot(g + 1)
                    copy_y(NG - 1)

                return copy_x, gate_exp, copy_onehot, run

            copy_x, gate_exp, copy_onehot, run = ffn_act(ffn[0], 0)
            unit(NU - 1, after={LAST[0] + 2: lambda: copy_heads(0), LAST[1] + 2: lambda: copy_heads(1),
                                LAST[4] + 1: lambda: copy_x(0), 19: lambda: gate_exp(0)})
            copy_heads(2)
            copy_heads(3)
            copy_onehot(0)
            run()
            for g in range(NG):
                act.wait_ge(la["xt"], g + 1)
                act.copy(BXT[:, g * W5:(g + 1) * W5], ps[:, g % 2, :]).then_inc(la["xte"], 1)
                for qk in range(2):
                    act.wait_ge(la["qk"], 2 * g + qk + 1)
                    act.activation(QKT[:, qk, g * W5:(g + 1) * W5], ps[:, 2 + qk, :], ACT.Copy, scale=LD ** -0.25)
                    act.activation(QKSQ[:, qk, g * W5:(g + 1) * W5], ps[:, 2 + qk, :], ACT.Square,
                                   scale=LD ** -0.25).then_inc(la["qke"], 1)
            def store_features(t):
                act.wait_ge(la["ft"], t + 1)
                act.activation(QKPT[:, :, t, :, :], ps[:, 6 + t % 2, :].rearrange("p (q h s) -> p q h s", q=2, h=LH),
                               ACT.Copy, scale=c_feat, bias=FEAT_EPS).then_inc(la["fte"], 1)

            for pair in range(NT // 2):
                for qk in range(2):
                    n = 2 * pair + qk
                    act.wait_ge(la["rm"], n + 1)
                    for k in range(2):
                        t = 2 * pair + k
                        for h in range(LH):
                            at = (k * LH + h) * LM
                            act.activation(EQK[:, qk, t, h, :], ps[:, n % 5, at:at + LM], ACT.Exp,
                                           bias=RM[:, qk, t, h:h + 1]).then_inc(la["ex"], 1)
                if pair >= 2:
                    store_features(2 * pair - 4)
                    store_features(2 * pair - 3)
            for t in range(NT - 4, NT):
                store_features(t)
            for g in range(NG):
                act.wait_ge(la["ot"], g + 1)
                act.copy(AOT[:, g * W5:(g + 1) * W5], ps[:, g % 2 if g else 6, :]).then_inc(la["ote"], 1)
            def copy_h(g):
                act.wait_ge(la["ht"], g + 1)
                act.copy(HT[:, g * W5:(g + 1) * W5], ps[:, g % 2, :]).then_inc(la["hte"], 1)

            copy_x, gate_exp, copy_onehot, run = ffn_act(ffn[1], 6)
            copy_h(0)
            for g in range(NG):
                for f in range(FC):
                    n = g * FC + f
                    act.wait_ge(la["u"], n + 1)
                    if f == 0 and g >= 2:
                        act.wait_ge(la["y"], g - 1)
                    act.activation(hid(g)[:, f, :], ps[:, 2 + n % 2, :], ACT.Relu,
                                   bias=b1[:, f:f + 1]).then_inc(la["ue"], 1)
                if g + 1 < NG:
                    copy_h(g + 1)
                else:
                    gate_exp(0)
                act.wait_ge(la["y"], g + 1)
                if g >= 2:
                    act.wait_ge(la["yt"], g - 1)
                act.activation(UT[:, g % 2, :], ps[:, 4 + g % 2, :], ACT.Identity,
                               bias=b2[:, 0:1]).then_inc(la["ye"], 1)
                if g == 2:
                    copy_x(0)
            copy_onehot(0)
            run()

        @block.tensor
        def _(pe):
            def transposes(bank, srcs, idn, done):
                for k, src in enumerate(srcs):
                    last = pe.transpose(ps[:, bank, k * P:(k + 1) * P], src, idn)
                last.then_inc(done, 1)

            def feature_transposes(t):
                pe.wait_ge(la["ex"], 8 * (t // 2 + 1))
                if t >= 2:
                    pe.wait_ge(la["fte"], t - 1)
                for k in range(4):
                    last = pe.transpose(ps[:, 6 + t % 2, k * P:(k + 1) * P], EQK[:, k // 2, t, k % 2, :], ident[:, :])
                last.then_inc(la["ft"], 1)

            pe.wait_ge(s_cst, 1)
            for g in range(NG):
                pe.wait_ge(s_xn, g + 1)
                if g >= 2:
                    pe.wait_ge(s_xte, g - 1)
                transposes(g % 2, [XN[:, g * GT + k, :] for k in range(GT)], ident[:, :], s_xt)
                if g % 2 == 0:
                    continue
                b = g // 2
                if b == 0:
                    pe.wait_ge(s_w, 64)
                pe.wait_ge(s_xte, g + 1)
                for qk in (1, 0):
                    for n in range(2):
                        if b:
                            pe.wait_ge(s_qke, 2 * (1 - qk) + n + 1)
                        pe.matmul(ps[:, 2 + 2 * qk + n, :], wT[:, qk, :], XT[:, b * S + n * W5:b * S + (n + 1) * W5],
                                  start=True, stop=True).then_inc(s_qk, 1)
                for g2 in (2 * b, 2 * b + 1):
                    if b:
                        pe.wait_ge(s_ve, g2 - 1)
                    for k in range(GT):
                        t = g2 * GT + k
                        last = pe.matmul(ps[:, 6 + g2 % 2, k * P:(k + 1) * P], XT[:, t * P:(t + 1) * P], wT[:, 2, :],
                                         start=True, stop=True)
                    last.then_inc(s_vp, 1)

            def score_group(w, n, slot):
                i, heads = A_GROUPS[n]
                kk = P * (i + 1)
                first = 2 * (n % 2)
                for j, h in enumerate(heads):
                    if len(heads) == 1:
                        pieces = [(first, 0, 0, min(kk, W5))] + ([(first + 1, 0, W5, kk)] if kk > W5 else [])
                    elif kk > 256:
                        pieces = [(first + j, 0, 0, kk)]
                    else:
                        pieces = [(first, j * kk, 0, kk)]
                    for bank, at, k0, k1 in pieces:
                        diag = k1 == kk
                        pe.matmul(ps[:, bank, at:at + k1 - k0], Qop[0:ZROWS, slot, h, i * P:(i + 1) * P],
                                  Kop[0:ZROWS, slot, h, k0:k1], start=True, stop=not diag)
                        if diag:
                            last = pe.matmul(ps[:, bank, at + k1 - k0 - P:at + k1 - k0], identb[:, :], maskA[:, :],
                                             start=False, stop=True)
                last.then_inc(s_a, 1)

            def score_chunk(u, c, slot):
                half, kt, heads, width = B_CHUNKS[c]
                q1 = S if half == 0 else W5
                pe.wait_ge(s_exp, u * BC + (c + 1))
                for j, h in enumerate(heads):
                    last = pe.matmul(ps[:, 4 + c % 2, j * width:(j + 1) * width],
                                     Kop[0:MROW + PARTS, slot, h, kt * P:(kt + 1) * P],
                                     Qop[0:MROW + PARTS, slot, h, q1 - width:q1], start=True, stop=True)
                last.then_inc(s_b, 1)

            def outputs(u, half, kt0, slot):
                last_kt = 7 if half == 0 else 3
                pe.wait_ge(s_exp, u * BC + (2 + last_chunk(half, kt0 + 1) + 1))
                masked = [j for j, (hf, kt) in enumerate(MASKS) if hf == half and kt <= kt0 + 1]
                if masked:
                    pe.wait_ge(s_mask, u * 8 + (max(masked) + 1))
                if kt0 == 0:
                    pe.wait_ge(s_pve, 2 * u + (half + 1))
                    if half == 0:
                        pe.wait_ge(s_vs, u + 2)
                for kt in (kt0, kt0 + 1):
                    q0 = 0 if (half == 0 and kt < 4) or (half == 1 and kt == 1) else P * (kt % 4)
                    for h in (0, 1):
                        col = 32 * (2 * h + kt % 2)
                        last = pe.matmul(ps[col:col + 32, 6, q0:W5], Vs[:, slot, kt, :],
                                         E[:, half * 8 + kt, h, q0:W5], start=kt < 2, stop=kt >= last_kt - 1)
                if kt0 + 1 == last_kt:
                    last.then_inc(s_pv, 1)

            def transpose_maxima(n, slot, half):
                pe.wait_ge(s_split, n + 1)
                pe.wait_ge(s_mte, n)
                pe.transpose(ps[0:24, 7, 0:P // 2].bitcast(bf16),
                             M3[:, slot, half, :, :, :].rearrange("p a b c -> p (a b c)"),
                             identb[:, :]).then_inc(s_mt, 1)

            pe.wait_ge(s_ld[0], 32)
            pe.wait_ge(s_oz, CLEARED)
            pe.wait_ge(s_qke, 4 * B)
            for n in range(AG):
                if n >= 2:
                    pe.wait_ge(s_max, n - 1)
                score_group(0, n, 0)
                if n == AG - 2:
                    transpose_maxima(0, 0, 0)

            def head_products(w, tiles=range(TB), last_unit=False):
                pe.wait_ge(s_pve, 2 * w + 3)
                pe.wait_ge(s_mte, 2 * w + (2 if last_unit else 3))
                for t in tiles:
                    half, q = (1, t) if t < 4 else (0, t - 4)
                    last = pe.matmul(ps[:, 7, HEADS_AT + t * 2 * (VD + 1):HEADS_AT + (t + 1) * 2 * (VD + 1)],
                                     OT[:, half, q * P:(q + 1) * P], pick[:, :], start=True, stop=True)
                if tiles[-1] == TB - 1:
                    last.then_inc(s_hp, 1)

            pe.sem_inc(s_b, 1)

            def unit(u, t, s, ahead=True, first=False, after={}):
                nxt = (s + 1) % SLOTS
                loads = t + 1 if s < 2 else t + 2
                given = 0
                pe.wait_ge(s_m[s][0], 32 * (t + 1))
                for c in range(BC):
                    if c == 14:
                        pe.wait_ge(s_m[s][1], 32 * (t + 1))
                    score_chunk(u, c, s)
                    if c in after:
                        after[c]()
                    if c in HEADS_C and not first:
                        n = TB // len(HEADS_C)
                        k = HEADS_C.index(c)
                        head_products(u - 1, range(k * n, (k + 1) * n))
                    if ahead and given < AG and c * AG >= given * PACE:
                        if given == 0:
                            pe.wait_ge(s_ld[nxt], 32 * loads)
                        pe.wait_ge(s_max, u * AG + (AG + given - 1))
                        score_group(u, given, nxt)
                        given += 1
                    if c == MT1_AT:
                        if not first:
                            pe.wait_ge(s_ht, u)
                        transpose_maxima(2 * u + 1, s, 1)
                    if c == MT_AT and ahead:
                        transpose_maxima(2 * u + 2, nxt, 0)
                    for at, half, kt0 in ((5, 0, 0), (9, 0, 2), (14, 0, 4), (16, 0, 6), (19, 1, 0)):
                        if c == at:
                            outputs(u, half, kt0, s)
                if ahead:
                    while given < AG:
                        pe.wait_ge(s_max, u * AG + (AG + given - 1))
                        score_group(u, given, nxt)
                        given += 1
                outputs(u, 1, 2, s)

            pe.wait_ge(s_lamr, 1)
            for s in range(SLOTS):
                unit(s, 0, s, first=s == 0)
            with pe.Fori(1, 5) as t:
                for s in range(SLOTS):
                    unit(t * SLOTS + s, t, s)

            def head_transposes(g):
                pe.wait_ge(s_hn, 8 * (g // 2) + 8)
                if g >= 2:
                    pe.wait_ge(s_oT2e, g - 1)
                b = g // 2
                transposes(HEAD_BANKS[g], [DD[:, (g % 2) * GT + k, b * P:(b + 1) * P] for k in range(GT)], ident[:, :], s_oT2)


            def project_heads(g):
                pe.wait_ge(s_oT2e, g + 1)
                for k in range(GT):
                    t = g * GT + k
                    last = pe.matmul(ps[:, 2 + g, k * P:(k + 1) * P], OTT[:, t * P:(t + 1) * P], wT[:, 3, :],
                                     start=True, stop=True)
                last.then_inc(s_wo, 1)

            def ffn_pe(f, bank0):
                def head_x(g):
                    pe.wait_ge(f["xn"], g + 1)
                    if g:
                        pe.wait_ge(f["xte"], g)
                    transposes(0 if g else bank0, [FXN[:, g * GT + k, :] for k in range(GT)], ident[:, :], f["xt"])

                def head_router(g):
                    pe.wait_ge(f["xte"], g + 1)
                    if g:
                        pe.wait_ge(f["sub"], g)
                    for k in range(GT):
                        t = g * GT + k
                        last = pe.matmul(ps[:, 2 if g else bank0, k * OHR:(k + 1) * OHR], FXT[:, t * P:(t + 1) * P], rw[:, :],
                                         start=True, stop=True)
                    last.then_inc(f["lg"], 1)

                def head_onehot(g):
                    pe.wait_ge(f["oh"], g + 1)
                    if g:
                        pe.wait_ge(f["ohte"], g)
                    bank = ps[0:OHR, 1 if g else bank0, 0:W5 // 2].bitcast(bf16)
                    for k in range(GT):
                        last = pe.transpose(bank[:, k * P:(k + 1) * P],
                                            OH[:, g % 2, k, :, :].rearrange("p a b -> p (a b)"), identb[:, :])
                    last.then_inc(f["oht"], 1)

                def spread(g, e):
                    n = g * NE + e
                    if n >= 2:
                        pe.wait_ge(f["xm"], n - 1)
                    pe.matmul(ps[:, 3 + n % 2, :], sel[:, e, :], OHT[:, g % 2, :], start=True, stop=True
                              ).then_inc(f["g"], 1)

                def expert(g, e):
                    pe.wait_ge(f["xm"], g * NE + e + 1)
                    mm = pe.matmul(ps[:, 5 + g % 2, :], ew[:, e, :], XM[:, e % 4, :], start=False, stop=e == NE - 1)
                    mm.then_inc(f["y"] if e == NE - 1 else f["e"], 1)

                def back(g):
                    pe.wait_ge(f["ye"], g + 1)
                    if g:
                        pe.wait_ge(f["x"], g)
                    transposes(7, [YT[:, g % 2, k * P:(k + 1) * P] for k in range(GT)], ident[:, :], f["yt"])

                def run():
                    for g in range(NG):
                        pe.wait_ge(f["ohte"], g + 1)
                        if g >= 2:
                            pe.wait_ge(f["ye"], g - 1)
                        pe.matmul(ps[:, 5 + g % 2, :], eb[:, :], OHT[:, g % 2, :], start=True, stop=False)
                        spread(g, 0)
                        spread(g, 1)
                        for e in range(NE):
                            if e == 0 and g + 1 < NG:
                                head_x(g + 1)
                            if e == 1 and g:
                                back(g - 1)
                            if e == 2 and g + 1 < NG:
                                head_router(g + 1)
                            if e == ONEHOT_E and g + 1 < NG:
                                head_onehot(g + 1)
                            expert(g, e)
                            if e + 2 < NE:
                                spread(g, e + 2)
                    back(NG - 1)

                return head_x, head_router, head_onehot, run

            pe.wait_ge(s_w2, 16 * 12)
            pe.wait_ge(s_rw, 16)
            pe.wait_ge(s_ebd, 48)
            pe.wait_ge(s_cst, 3)
            head_x, head_router, head_onehot, run = ffn_pe(ffn[0], 0)
            pe.wait_ge(s_max, NU * AG)
            unit(NU - 1, 5, 0, ahead=False,
                 after={LAST[0]: lambda: head_transposes(0), LAST[1]: lambda: head_transposes(1),
                        LAST[2]: lambda: project_heads(0), LAST[3]: lambda: project_heads(1),
                        LAST[4]: lambda: head_x(0), LAST[5]: lambda: head_router(0)})
            head_products(NU - 1, last_unit=True)
            head_onehot(0)
            head_transposes(2)
            head_transposes(3)
            pe.wait_ge(s_exp, 2 + NU * BC)
            project_heads(2)
            project_heads(3)
            pe.wait_ge(s_x1, NG)
            run()

            pe.wait_ge(ffn[0]["sub"], NG)
            def block_transposes(g):
                pe.wait_ge(la["xn"], g + 1)
                if g >= 2:
                    pe.wait_ge(la["xte"], g - 1)
                transposes(g % 2, [BX[:, g * GT + k, :] for k in range(GT)], ident[:, :], la["xt"])

            def square_sums(g):
                pe.wait_ge(la["qke"], 2 * g + 2)
                if g:
                    pe.wait_ge(la["nn"], g)
                for qk in range(2):
                    for k in range(GT):
                        t, at = g * GT + k, (qk * GT + k) * LH
                        last = pe.matmul(ps[:, 5, at:at + LH], QKSQ[:, qk, t * P:(t + 1) * P], hsum[:, :],
                                         start=True, stop=True)
                last.then_inc(la["nt"], 1)

            block_transposes(0)
            for g in range(NG):
                if g + 1 < NG:
                    block_transposes(g + 1)
                pe.wait_ge(la["xte"], g + 1)
                for qk in range(2):
                    if g:
                        pe.wait_ge(la["qke"], 2 * (g - 1) + qk + 1)
                    pe.matmul(ps[:, 2 + qk, :], bw[:, qk, :], BXT[:, g * W5:(g + 1) * W5], start=True, stop=True
                              ).then_inc(la["qk"], 1)
                if g:
                    pe.wait_ge(la["ve"], g)
                for k in range(GT):
                    t = g * GT + k
                    last = pe.matmul(ps[:, 4, k * P:(k + 1) * P], BXT[:, t * P:(t + 1) * P], bw[:, 2, :],
                                     start=True, stop=True)
                last.then_inc(la["v"], 1)
                if g:
                    square_sums(g - 1)
            square_sums(NG - 1)
            pe.wait_ge(la["ve"], NG)
            pe.wait_ge(s_om, 32)
            for pair in range(NT // 2):
                for qk in range(2):
                    n = 2 * pair + qk
                    if n >= 5:
                        pe.wait_ge(la["ex"], 4 * (n - 4))
                    for k in range(2):
                        t = 2 * pair + k
                        last = pe.matmul(ps[:, n % 5, k * LH * LM:(k + 1) * LH * LM], QKT[:, qk, t * P:(t + 1) * P],
                                         om[:, :, :].rearrange("p a b -> p (a b)"), start=True, stop=True)
                    last.then_inc(la["pr"], 1)
                if pair >= 2:
                    feature_transposes(2 * pair - 4)
                    feature_transposes(2 * pair - 3)
            for t in range(NT - 4, NT):
                feature_transposes(t)
            pe.wait_ge(la["ex"], 4 * NT)
            pe.wait_ge(la["fte"], NT)
            pe.wait_ge(la["kp"], NT)

            def at_products(c):
                if c >= 2:
                    pe.wait_ge(la["ate"], c - 1)
                for j in range(LU):
                    t, h = (j // LH) * TB + c, j % LH
                    last = pe.matmul(ps[:, c % 2, j * P:(j + 1) * P], QKPT[:, 1, t, h, :], QKPT[:, 0, t, h, :],
                                     start=True, stop=True)
                last.then_inc(la["at"], 1)

            def attention_transposes(g):
                if g >= 2:
                    pe.wait_ge(la["ote"], g - 1)
                transposes(g % 2 if g else 6, [AO[:, g * GT + k, :] for k in range(GT)], ident[:, :], la["ot"])

            def project_attention(g):
                pe.wait_ge(la["ote"], g + 1)
                for k in range(GT):
                    t = g * GT + k
                    last = pe.matmul(ps[:, 2 + g if g else 7, k * P:(k + 1) * P], AOT[:, t * P:(t + 1) * P],
                                     bw[:, 3, :], start=True, stop=True)
                last.then_inc(la["wo"], 1)

            at_products(0)
            for c in range(TB):
                if c + 1 < TB:
                    at_products(c + 1)
                if c < TB - 1:
                    if c >= 2:
                        pe.wait_ge(la["ste"], c - 1)
                    for j in range(LU):
                        t, h = (j // LH) * TB + c, j % LH
                        last = pe.matmul(ps[:, 2 + c % 2, j * VW:(j + 1) * VW], KP[:, t, h, :], VA[:, t, h, :],
                                         start=True, stop=True)
                    last.then_inc(la["st"], 1)
                pe.wait_ge(la["ate"], c + 1)
                if c:
                    pe.wait_ge(la["ste"], c)
                if c >= 2:
                    pe.wait_ge(la["oe"], c - 1)
                for j in range(LU):
                    t, h = (j // LH) * TB + c, j % LH
                    dst = ps[:, 4 + c % 2, j * VW:(j + 1) * VW]
                    last = pe.matmul(dst, AM[:, c % 2, j, :], VA[:, t, h, :], start=True, stop=c == 0)
                    if c:
                        last = pe.matmul(dst, QKPT[:, 0, t, h, :], ST[:, c - 1, j, :], start=False, stop=True)
                last.then_inc(la["o"], 1)
                if c == GT:
                    pe.wait_ge(la["oe"], GT)
                    attention_transposes(0)
                if c == GT + 1:
                    project_attention(0)
            pe.wait_ge(la["oe"], TB)
            attention_transposes(1)
            for g in range(1, NG):
                if g + 1 < NG:
                    attention_transposes(g + 1)
                project_attention(g)

            def h_transposes(g):
                pe.wait_ge(la["h"], g + 1)
                if g >= 2:
                    pe.wait_ge(la["hte"], g - 1)
                transposes(g % 2, [H2[:, g * GT + k, :] for k in range(GT)], ident[:, :], la["ht"])

            def back(g):
                pe.wait_ge(la["ye"], g + 1)
                if g:
                    pe.wait_ge(la["x"], g)
                transposes(7, [UT[:, g % 2, k * P:(k + 1) * P] for k in range(GT)], ident[:, :], la["yt"])

            head_x, head_router, head_onehot, run = ffn_pe(ffn[1], 6)
            h_transposes(0)
            pe.wait_ge(la["res"], 2)
            for g in range(NG):
                pe.wait_ge(la["hte"], g + 1)
                for f in range(FC):
                    n = g * FC + f
                    if n >= 2:
                        pe.wait_ge(la["ue"], n - 1)
                    pe.matmul(ps[:, 2 + n % 2, :], w1[:, f * P:(f + 1) * P], HT[:, g * W5:(g + 1) * W5],
                              start=True, stop=True).then_inc(la["u"], 1)
                if g:
                    back(g - 1)
                if g + 1 < NG:
                    h_transposes(g + 1)
                else:
                    head_router(0)
                if g == 0:
                    pe.wait_ge(la["res"], NG)
                if g >= 2:
                    pe.wait_ge(la["ye"], g - 1)
                for f in range(FC):
                    pe.wait_ge(la["ue"], g * FC + f + 1)
                    last = pe.matmul(ps[:, 4 + g % 2, :], w2[:, f, :], hid(g)[:, f, :], start=f == 0, stop=f == FC - 1)
                last.then_inc(la["y"], 1)
                if g == 2:
                    head_x(0)
            head_onehot(0)
            back(NG - 1)
            run()

        @block.vector
        def _(dve):
            chain = [0]

            def fence(ins, wait=True):
                chain[0] += 1
                ins.then_inc(s_dve, 1)
                if wait:
                    dve.wait_ge(s_dve, chain[0])
                return chain[0]

            def partial_stats(tiles, src):
                for t in tiles:
                    last = dve.bn_stats(st[:, t, :], src(t))
                return fence(last, wait=False)

            def aggregate(tiles, done):
                for t in tiles:
                    last = dve.bn_aggr(mv[:, t, :], st[:, t, :])
                last.then_inc(done, 1)

            def stats(tiles, src, done):
                dve.wait_ge(s_dve, partial_stats(tiles, src))
                aggregate(tiles, done)

            def normalise(tiles, dst, src, done):
                for t in tiles:
                    last = dve.tensor_scalar(dst(t), src(t), mv[:, t, 0:1], rstd[:, t:t + 1], ALU.subtract, ALU.mult)
                last.then_inc(done, 1)

            for g in range(NG):
                tiles = range(g * GT, (g + 1) * GT)
                dve.wait_ge(s_x[g], 16)
                stats(tiles, lambda t: X[:, t, :], s_var)
                if g >= 1:
                    before = range((g - 1) * GT, g * GT)
                    dve.wait_ge(s_var, g)
                    dve.wait_ge(s_rstd, g)
                    normalise(before, lambda t: XN[:, t, :], lambda t: X[:, t, :], s_xn)
            dve.wait_ge(s_rstd, NG)
            normalise(tiles, lambda t: XN[:, t, :], lambda t: X[:, t, :], s_xn)
            dve.wait_ge(s_lam, 16)
            for k in range(2):
                last = dve.tensor_tensor(lamw[:, k, :], lamv[:, 2 * k, :], lamv[:, 2 * k + 1, :], ALU.mult)
            fence(last)
            dve.tensor_reduce(lams[:, 0:2], lamw[:, :, :], AX.X, ALU.add).then_inc(s_lsum, 1)

            def cut(b, qk, step):
                QS, part = QSb[b], QPb[b]
                dve.wait_ge(s_cut, 5 * (2 * b + 1 - qk) + step) if step else dve.wait_ge(s_qke, 4 * b + 2 * (1 - qk) + 2)
                if step == 0:
                    last = dve.tensor_scalar(QS[:, qk, :], QS[:, qk, :], OPERAND_BOUND, -OPERAND_BOUND, ALU.min, ALU.max)
                elif step == 1:
                    last = dve.tensor_copy(part[:, qk, 0, :], QS[:, qk, :])
                elif step == 2:
                    last = dve.tensor_tensor(QR[:, qk, :], QS[:, qk, :], part[:, qk, 0, :], ALU.subtract)
                elif step == 3:
                    last = dve.tensor_copy(part[:, qk, 1, :], QR[:, qk, :])
                else:
                    last = dve.tensor_tensor(part[:, qk, 2, :], QR[:, qk, :], part[:, qk, 1, :], ALU.subtract)
                last.then_inc(s_cut, 1)

            for qk in (1, 0):
                for step in range(5):
                    cut(0, qk, step)
            dve.wait_ge(s_act, 1)
            fence(dve.tensor_tensor(lams[:, 0:1], lams[:, 3:4], lams[:, 2:3], ALU.subtract))
            fence(dve.tensor_scalar(lams[:, 1:2], lams[:, 0:1], 1.0, -LAMBDA_INIT, ALU.mult, ALU.add))
            dve.wait_ge(s_oz, CLEARED)
            dve.tensor_scalar(pick[:, VD + 1:2 * VD + 1], pick[:, VD + 1:2 * VD + 1], lams[:, 1:2], None, ALU.mult
                              ).then_inc(s_lamr, 1)

            def maximum(w, n, slot):
                i, heads = A_GROUPS[n]
                kk = P * (i + 1)
                first = 2 * (n % 2)
                dve.wait_ge(s_a, w * AG + (n + 1))
                out = NM[:, slot, 0 if i >= 4 else 1, heads[0]:heads[-1] + 1, i % 4]
                if len(heads) == 1:
                    src = ps[:, first:first + 2, :].rearrange("p b c -> p (b c)")[:, 0:kk]
                elif kk > 256:
                    src = ps[:, first:first + 2, 0:kk]
                else:
                    src = ps[:, first, 0:2 * kk].rearrange("p (h k) -> p h k", h=2)
                dve.tensor_reduce(out, src, AX.X, ALU.max, negate=True).then_inc(s_max, 1)

            def store_maxima(n, slot, half):
                dve.wait_ge(s_mt, n + 1)
                dve.tensor_copy(MT[:, slot, half, :], ps[0:24, 7, 0:P // 2].bitcast(bf16)).then_inc(s_mte, 1)

            for n in range(AG):
                maximum(0, n, 0)
                if n == AG - 2:
                    store_maxima(0, 0, 0)

            hv = ps[:, 7, HEADS_AT:HEADS_AT + TB * 2 * (VD + 1)].rearrange("p (t h e) -> p t h e", t=TB, h=2)

            def invert_sums(w):
                dve.wait_ge(s_hp, w + 1)
                dve.reciprocal(RL, hv[:, :, :, VD]).then_inc(s_hq, 1)

            def divide(w, first):
                dve.wait_ge(s_hq, w + 1)
                if not first:
                    dve.wait_ge(s_hstep, 4 * w - 3)
                dve.tensor_tensor(TT, hv[:, :, :, 0:VD],
                                  RL.rearrange("p t (h o) -> p t h o", o=1).broadcast_to([P, TB, 2, VD]),
                                  ALU.mult).then_inc(s_ht, 1)

            def sum_squares(w):
                dve.wait_ge(s_hstep, 4 * w + 2)
                dve.tensor_reduce(MS[:, 0, :], SQ, AX.X, ALU.add).then_inc(s_hs, 1)

            def unit(u, s, ahead=True, cuts=(), first=0):
                nxt = (s + 1) % SLOTS
                cuts = list(cuts)
                for n in range(AG):
                    if ahead:
                        maximum(u + 1, n, nxt)
                    if n == INVERT_AT and first != 1:
                        invert_sums(u - 1)
                    if n == INVERT_AT + 1 and first != 1:
                        divide(u - 1, first == 2)
                    if n == INVERT_AT + 3 and first != 1:
                        sum_squares(u - 1)
                    if n % 3 == 1 and cuts:
                        cut(1, *cuts.pop(0))
                    if n == ST1_AT:
                        store_maxima(2 * u + 1, s, 1)
                    if n == ST_AT and ahead:
                        store_maxima(2 * u + 2, nxt, 0)

            steps = [(qk, step) for qk in (1, 0) for step in range(5)]
            for u in range(SLOTS):
                unit(u, u, cuts=steps[4 * u:4 * u + 4], first=u + 1)
            with dve.Fori(1, 5) as t:
                for s in range(SLOTS):
                    unit(t * SLOTS + s, s)
            unit(NU - 1, (NU - 1) % SLOTS, ahead=False)

            def residual(g):
                dve.wait_ge(s_wo, g + 1)
                xg = X[:, g * GT:(g + 1) * GT, :].rearrange("p a b -> p (a b)")
                dve.tensor_tensor(xg, ps[:, 2 + g, :], xg, ALU.add).then_inc(s_x1, 1)

            def ffn_dve(f, before, bank0, between, early={}):
                chosen = {}

                def head_steps(g):
                    tiles = range(g * GT, (g + 1) * GT)

                    def ln():
                        dve.wait_ge(before, g + 1)
                        stats(tiles, lambda t: X[:, t, :], f["var"])

                    def norm():
                        dve.wait_ge(f["var"], g + 1)
                        dve.wait_ge(f["rstd"], g + 1)
                        normalise(tiles, lambda t: FXN[:, t, :], lambda t: X[:, t, :], f["xn"])

                    def b4(a):
                        return a.rearrange("p (t o) -> p t o", o=1).broadcast_to([P, GT, NE])

                    def logits():
                        dve.wait_ge(f["lg"], g + 1)
                        src = ps[:, 2 if g else bank0, 0:GT * OHR].rearrange("p (t e) -> p t e", t=GT)[:, :, 0:NE]
                        fence(dve.tensor_tensor(LG[:, g, :, :], src,
                                                rb[:, :].rearrange("p (o e) -> p o e", o=1).broadcast_to([P, GT, NE]),
                                                ALU.add))
                        fence(dve.tensor_reduce(MX[:, 0, g, :], LG[:, g, :, :], AX.X, ALU.max))
                        dve.tensor_tensor(LG[:, g, :, :], LG[:, g, :, :], b4(MX[:, 0, g, :]), ALU.subtract
                                          ).then_inc(f["sub"], 1)

                    def choose():
                        dve.wait_ge(f["exp"], g + 1)
                        dve.tensor_reduce(MX[:, 1, g, :], LE[:, g, :, :], AX.X, ALU.add)
                        fence(dve.tensor_reduce(MX[:, 2, g, :], LE[:, g, :, :], AX.X, ALU.max))
                        dve.reciprocal(MX[:, 3, g, :], MX[:, 1, g, :])
                        fence(dve.tensor_tensor(LG[:, g, :, :], LE[:, g, :, :], b4(MX[:, 2, g, :]), ALU.is_ge))
                        dve.tensor_tensor(MX[:, 3, g, :], MX[:, 3, g, :], MX[:, 2, g, :], ALU.mult)
                        chosen[g] = fence(dve.tensor_tensor(
                            LG[:, g, :, :], LG[:, g, :, :],
                            rev[:, :].rearrange("p (o e) -> p o e", o=1).broadcast_to([P, GT, NE]), ALU.mult), wait=False)

                    def mark():
                        dve.wait_ge(s_dve, chosen[g])
                        fence(dve.tensor_reduce(MX[:, 4, g, :], LG[:, g, :, :], AX.X, ALU.max))
                        if g >= 2:
                            dve.wait_ge(f["oht"], g - 1)
                        dve.tensor_tensor(
                            OH[:, g % 2, :, :, :],
                            LG[:, g, :, :].rearrange("p t (o e) -> p t o e", o=1).broadcast_to([P, GT, COPIES, NE]),
                            MX[:, 4, g, :].rearrange("p (t o e) -> p t o e", o=1, e=1).broadcast_to([P, GT, COPIES, NE]),
                            ALU.is_equal).then_inc(f["oh"], 1)

                    return {"ln": ln, "norm": norm, LOGITS_E: logits, CHOOSE_E: choose, CHOOSE_E + 1: mark}

                def combine(g):
                    dve.wait_ge(f["yt"], g + 1)
                    for k in range(GT):
                        t = g * GT + k
                        last = dve.scalar_tensor_tensor(out=X[:, t, :], in0=ps[:, 7, k * P:(k + 1) * P],
                                                        scalar=MX[:, 3, g, k:k + 1], in1=X[:, t, :],
                                                        op0=ALU.mult, op1=ALU.add)
                    last.then_inc(f["x"], 1)

                def step(name, g):
                    if name == "choose":
                        head_steps(g)[CHOOSE_E]()
                        head_steps(g)[CHOOSE_E + 1]()
                    else:
                        head_steps(g)[LOGITS_E if name == "logits" else name]()

                def run():
                    for g in range(NG):
                        steps = head_steps(g + 1) if g + 1 < NG else {}
                        for e in range(NE):
                            n = g * NE + e
                            dve.wait_ge(f["g"], n + 1)
                            if n >= 4:
                                back = n - 4
                                if back % NE == NE - 1:
                                    dve.wait_ge(f["y"], back // NE + 1)
                                else:
                                    dve.wait_ge(f["e"], back - back // NE + 1)
                            dve.tensor_tensor(XM[:, e % 4, :], ps[:, 3 + n % 2, :], FXT[:, g * W5:(g + 1) * W5], ALU.mult
                                              ).then_inc(f["xm"], 1)
                            if e in steps:
                                steps[e]()
                            if e == COMBINE_E and g:
                                combine(g - 1)
                            if e in early and g == 0:
                                step(*early[e])
                            if e in between and g:
                                between[e](g - 1)
                    combine(NG - 1)

                return step, run

            dve.wait_ge(s_w2, 16 * 12)
            dve.wait_ge(s_cst, 3)
            count = {}

            def norm_la(g):
                dve.wait_ge(la["var"], g + 1)
                dve.wait_ge(la["rstd"], g + 1)
                normalise(range(g * GT, (g + 1) * GT), lambda t: BX[:, t, :], lambda t: X[:, t, :], la["xn"])

            def stats_la(g):
                dve.wait_ge(ffn[0]["x"], g + 1)
                count[g] = partial_stats(range(g * GT, (g + 1) * GT), lambda t: X[:, t, :])

            def spread_la(g):
                dve.wait_ge(s_dve, count[g])
                aggregate(range(g * GT, (g + 1) * GT), la["var"])
                if g:
                    norm_la(g - 1)

            step, run = ffn_dve(ffn[0], s_x1, 0, {6: stats_la, 7: spread_la},
                                 {1: ("ln", 2), 2: ("ln", 3), 6: ("norm", 2), 7: ("norm", 3)})
            residual(0)
            step("ln", 0)
            residual(1)
            step("ln", 1)
            step("norm", 0)
            step("norm", 1)
            step("logits", 0)
            step("choose", 0)
            invert_sums(NU - 1)
            divide(NU - 1, False)
            sum_squares(NU - 1)
            residual(2)
            residual(3)
            run()
            stats_la(NG - 1)
            spread_la(NG - 1)
            norm_la(NG - 1)

            def store_v(g):
                dve.wait_ge(la["v"], g + 1)
                dve.tensor_copy(VA[:, g * GT:(g + 1) * GT, :, 0:LD],
                                ps[:, 4, :].rearrange("p (t h d) -> p t h d", t=GT, h=LH)).then_inc(la["ve"], 1)

            dve.wait_ge(la["vz"], 1)
            store_v(0)
            for g in range(NG):
                if g + 1 < NG:
                    store_v(g + 1)
                dve.wait_ge(la["nt"], g + 1)
                dve.tensor_copy(NN[:, :, g * GT:(g + 1) * GT, :],
                                ps[:, 5, 0:2 * GT * LH].rearrange("p (q t h) -> p q t h", q=2, t=GT)
                                ).then_inc(la["nn"], 1)
            dve.wait_ge(la["nn"], NG)
            for n in range(NT):
                dve.wait_ge(la["pr"], n + 1)
                rm = RM[:, n % 2, n // 2 * 2:n // 2 * 2 + 2, :].rearrange("p t h -> p (t h)")
                nn = NN[:, n % 2, n // 2 * 2:n // 2 * 2 + 2, :].rearrange("p t h -> p (t h)")
                fence(dve.tensor_reduce(rm, ps[:, n % 5, :].rearrange("p (h m) -> p h m", m=LM), AX.X, ALU.max))
                fence(dve.tensor_tensor(rm, rm, nn, ALU.subtract))
                dve.scalar_tensor_tensor(out=rm, in0=rm, scalar=-1.0, in1=nn, op0=ALU.mult, op1=ALU.subtract
                                         ).then_inc(la["rm"], 1)
            mt4 = maskT[:, :].rearrange("p (o q) -> p o q", o=1).broadcast_to([P, LU, P])
            ao = AO[:, :, :].rearrange("p (b t) (h d) -> p b h t d", b=B, h=LH)

            def causal(c):
                dve.wait_ge(la["at"], c + 1)
                if c >= 2:
                    dve.wait_ge(la["o"], c - 1)
                dve.tensor_tensor(AM[:, c % 2, :, :], ps[:, c % 2, :].rearrange("p (j q) -> p j q", j=LU), mt4,
                                  ALU.mult).then_inc(la["ate"], 1)

            g4 = gam[:, :].rearrange("p (o d) -> p o d", o=1).broadcast_to([P, GT, D])
            b4 = bet[:, :].rearrange("p (o d) -> p o d", o=1).broadcast_to([P, GT, D])

            def add_attention(g):
                dve.wait_ge(la["wo"], g + 1)
                bg = BX[:, g * GT:(g + 1) * GT, :].rearrange("p a b -> p (a b)")
                dve.tensor_tensor(bg, ps[:, 2 + g if g else 7, :], bg, ALU.add).then_inc(la["res"], 1)
                dve.wait_ge(la["res"], g + 1)
                stats(range(g * GT, (g + 1) * GT), lambda t: BX[:, t, :], la["var2"])

            def normalise_h(g):
                dve.wait_ge(la["var2"], g + 1)
                dve.wait_ge(la["rstd2"], g + 1)
                normalise(range(g * GT, (g + 1) * GT), lambda t: H2[:, t, :], lambda t: BX[:, t, :], la["h1"])
                dve.wait_ge(la["h1"], g + 1)
                hg = H2[:, g * GT:(g + 1) * GT, :]
                fence(dve.tensor_tensor(hg, hg, g4, ALU.mult))
                dve.tensor_tensor(hg, hg, b4, ALU.add).then_inc(la["h"], 1)

            causal(0)
            for c in range(TB):
                if c < TB - 1:
                    dve.wait_ge(la["st"], c + 1)
                    src = ps[:, 2 + c % 2, 0:LU * VW].rearrange("p (j v) -> p j v", j=LU)
                    if c == 0:
                        dve.tensor_copy(ST[:, 0, :, :], src).then_inc(la["ste"], 1)
                    else:
                        dve.wait_ge(la["ste"], c)
                        dve.tensor_tensor(ST[:, c, :, :], src, ST[:, c - 1, :, :], ALU.add).then_inc(la["ste"], 1)
                if c + 1 < TB:
                    causal(c + 1)
                dve.wait_ge(la["o"], c + 1)
                res = ps[:, 4 + c % 2, 0:LU * VW].rearrange("p (j v) -> p j v", j=LU)
                fence(dve.tensor_scalar(DN[:, c % 2, :], res[:, :, LD], FEAT_EPS, None, ALU.add))
                fence(dve.reciprocal(DN[:, c % 2, :], DN[:, c % 2, :]))
                for b in range(B):
                    last = dve.tensor_tensor(
                        ao[:, b, :, c, :], res[:, b * LH:(b + 1) * LH, 0:LD],
                        DN[:, c % 2, b * LH:(b + 1) * LH].rearrange("p (j o) -> p j o", o=1).broadcast_to([P, LH, LD]),
                        ALU.mult)
                last.then_inc(la["oe"], 1)
                if c == GT + 2:
                    add_attention(0)
            normalise_h(0)
            for g in range(1, NG):
                add_attention(g)
                if g > 1:
                    normalise_h(g - 1)
            normalise_h(NG - 1)
            step, run = ffn_dve(ffn[1], la["x"], 6, {})
            for g in range(NG):
                dve.wait_ge(la["yt"], g + 1)
                xg = X[:, g * GT:(g + 1) * GT, :].rearrange("p a b -> p (a b)")
                dve.tensor_tensor(xg, ps[:, 7, :], xg, ALU.add).then_inc(la["x"], 1)
                step("ln", g)
                step("norm", g)
                if g == 2:
                    step("logits", 0)
                    step("choose", 0)
            run()


c_feat = 1.0 / math.sqrt(LM)


def kernel(**inputs):
    import numpy as _np
    import concourse.bacc as _bacc
    from concourse import mybir as _mybir
    from concourse.bass_utils import run_bass_kernel_spmd as _run

    a, b, f = "L0_attn_a_", "L0_attn_b_", "L0_ffn_"
    g = {k: _np.asarray(v) for k, v in inputs.items()}
    arrays = [
        ("x", g[a + "x"].reshape(TOK, D)),
        ("a_wqT", g[a + "Wq"].T), ("a_wkT", g[a + "Wk"].T), ("a_wvT", g[a + "Wv"].T), ("a_woT", g[a + "Wo"].T),
        ("a_lam", _np.stack([g[a + "lq1"], g[a + "lk1"], g[a + "lq2"], g[a + "lk2"]])),
        ("b_wq", g[b + "Wq"]), ("b_wk", g[b + "Wk"]), ("b_wv", g[b + "Wv"]), ("b_wo", g[b + "Wo"]),
        ("b_omegaT", g[b + "omega"].T),
        ("b_w1", g[b + "W1"]), ("b_b1", g[b + "b1"].reshape(FC, P).T), ("b_w2", g[b + "W2"]),
        ("b_b2", g[b + "b2"].reshape(D, 1)), ("b_gamma", g[b + "gamma"].reshape(1, D)),
        ("b_beta", g[b + "beta"].reshape(1, D)),
        ("f_rw", g[f + "router_w"]), ("f_rb", g[f + "router_b"].reshape(1, NE)),
        ("f_ew", g[f + "expert_w"].transpose(1, 0, 2)), ("f_eb", g[f + "expert_b"]),
    ]
    nc = _bacc.Bacc("TRN2", target_bir_lowering=False, num_devices=1)
    feed, args = {}, []
    for name, arr in arrays:
        arr = _np.ascontiguousarray(arr)
        feed[name] = arr
        args.append(nc.dram_tensor(name, arr.shape, _mybir.dt.from_np(arr.dtype), kind="ExternalInput").ap())
    args.append(nc.dram_tensor("out", (TOK, D), _mybir.dt.float32, kind="ExternalOutput").ap())
    hybrid_kernel(nc, *args)
    r = _run(nc, [feed], core_ids=[0])
    return r.results[0]["out"].reshape(B, S, D)
```
